# Optimizing a Trainium2 kernel written in Bass

```python
import numpy as np
import jax
import jax.numpy as jnp

def _softmax(x, axis=-1):
    return jax.nn.softmax(x, axis=axis)

def _gelu(x):
    return jax.nn.gelu(x, approximate=True)

def _silu(x):
    return jax.nn.silu(x)

def _sigmoid(x):
    return jax.nn.sigmoid(x)

def _layernorm(x, axis=-1, eps=1e-05):
    m = jnp.mean(x, axis=axis, keepdims=True)
    v = jnp.var(x, axis=axis, keepdims=True)
    return (x - m) / jnp.sqrt(v + eps)

def _scatter_add(tgt, idx, src, axis=0):
    return tgt.at[idx].add(src)

def _segment_sum(src, seg, n):
    return jax.ops.segment_sum(src, seg, n)
kernel_name = 'mk_flamingo_gated_d1_seqx_r8_3c6505'

def setup_inputs(seed: int=0):
    np.random.seed(seed)
    _w = jnp.asarray

    def _rec_inputs():
        import jax
        import jax.numpy as jnp
        _rk = jax.random.key(seed)
        x = -0.0002928 + 1 * jax.random.normal(jax.random.fold_in(_rk, 1), (64, 64, 128), jnp.float32)
        _lenS = 64 - jax.random.randint(jax.random.fold_in(_rk, 7), (64,), 0, max(1, 64 // 4) + 1, jnp.int32)
        _lenS2 = 64 - jax.random.randint(jax.random.fold_in(_rk, 8), (64,), 0, max(1, 64 // 4) + 1, jnp.int32)
        _ctx_1024P = jax.random.normal(jax.random.fold_in(_rk, 11), (64, 16, 128), jnp.float32)
        _ctx_1024c = jax.random.dirichlet(jax.random.fold_in(_rk, 511), 0.3 * jnp.ones((16,), jnp.float32), (64, 64))
        _ctx_1024t = jnp.einsum('bsk,bkd->bsd', _ctx_1024c, _ctx_1024P)
        _ctx_1024t = _ctx_1024t * jax.lax.rsqrt(jnp.mean(jnp.square(_ctx_1024t)) + 1e-12) * 0.953939
        ctx_1024 = -1.39393e-06 + 0.999914 * (_ctx_1024t + 0.3 * jax.random.normal(jax.random.fold_in(_rk, 611), (64, 64, 128), jnp.float32))
        _validS = jnp.arange(64)[None, :] < _lenS[:, None]
        _validS2 = jnp.arange(64)[None, :] < _lenS2[:, None]
        _causal = jnp.tril(jnp.ones((64, 64), dtype=bool))
        mask_BxS2_bk0 = jnp.logical_not(jnp.broadcast_to(_validS2[:, :], (64, 64)))
        _g = jax.random.normal(jax.random.fold_in(_rk, 9001), (2, 1), jnp.float32)
        _g = jnp.sign(_g) * jnp.maximum(jnp.abs(_g), 1.0) + (_g == 0) * 1.0
        g_xattn = _g[0]
        g_ffn = _g[1]
        return (x, ctx_1024, mask_BxS2_bk0, g_xattn, g_ffn)
    x, ctx_1024, mask_BxS2_bk0, g_xattn, g_ffn = _rec_inputs()

    def _L0_xattn_setup():
        import jax, jax.numpy as jnp
        import numpy as np
        B, S, D = (2, 256, 128)
        H, DH = (16, 64)
        INNER = H * DH
        FF = 512
        SCALE = DH ** (-0.5)
        EPS = 1e-05

        def layernorm(x, g, b):
            m = jnp.mean(x, axis=-1, keepdims=True)
            v = jnp.var(x, axis=-1, keepdims=True)
            return (x - m) * jax.lax.rsqrt(v + EPS) * g + b

        def attention(x, ctx, mask, wq, wk, wv, wo, bo):
            b, n, _ = x.shape
            j = ctx.shape[1]
            q = (x @ wq).reshape(b, n, H, DH).transpose(0, 2, 1, 3)
            k = (ctx @ wk).reshape(b, j, H, DH).transpose(0, 2, 1, 3)
            v = (ctx @ wv).reshape(b, j, H, DH).transpose(0, 2, 1, 3)
            sim = jnp.einsum('bhid,bhjd->bhij', q, k) * SCALE
            if mask is not None:
                neg = -jnp.finfo(sim.dtype).max
                sim = jnp.where(mask[:, None, None, :], neg, sim)
            attn = jax.nn.softmax(sim, axis=-1)
            out = jnp.einsum('bhij,bhjd->bhid', attn, v)
            out = out.transpose(0, 2, 1, 3).reshape(b, n, INNER)
            return out @ wo + bo
        key = jax.random.key(seed)
        ks = jax.random.split(key, 26)
        w = lambda k, shp, fan: (jax.random.normal(k, shp, jnp.float32) / np.sqrt(fan)).astype(jnp.float32)
        return {'x': jax.random.normal(ks[0], (B, S, D), jnp.float32), 'enc_output': jax.random.normal(ks[1], (B, S, D), jnp.float32), 'sa_wq': w(ks[2], (D, INNER), D), 'sa_wk': w(ks[3], (D, INNER), D), 'sa_wv': w(ks[4], (D, INNER), D), 'sa_wo': w(ks[5], (INNER, D), INNER), 'sa_bo': jnp.zeros((D,), jnp.float32), 'ca_wq': w(ks[6], (D, INNER), D), 'ca_wk': w(ks[7], (D, INNER), D), 'ca_wv': w(ks[8], (D, INNER), D), 'ca_wo': w(ks[9], (INNER, D), INNER), 'ca_bo': jnp.zeros((D,), jnp.float32), 'ln1_g': jnp.ones((D,), jnp.float32), 'ln1_b': jnp.zeros((D,), jnp.float32), 'ln2_g': jnp.ones((D,), jnp.float32), 'ln2_b': jnp.zeros((D,), jnp.float32), 'ln3_g': jnp.ones((D,), jnp.float32), 'ln3_b': jnp.zeros((D,), jnp.float32), 'fc1_w': w(ks[10], (D, FF), D), 'fc1_b': jnp.zeros((FF,), jnp.float32), 'fc2_w': w(ks[11], (FF, D), FF), 'fc2_b': jnp.zeros((D,), jnp.float32), 'tgt_mask': jax.random.bernoulli(ks[12], 0.1, (B, S)), 'src_mask': jax.random.bernoulli(ks[13], 0.1, (B, S))}
    _L0_xattn_all = _L0_xattn_setup()
    _L0_xattn_in = {k: v for k, v in _L0_xattn_all.items() if k in ('sa_wq', 'sa_wk', 'sa_wv', 'sa_wo', 'sa_bo', 'ca_wq', 'ca_wk', 'ca_wv', 'ca_wo', 'ca_bo', 'ln1_g', 'ln1_b', 'ln2_g', 'ln2_b', 'ln3_g', 'ln3_b', 'fc1_w', 'fc1_b', 'fc2_w', 'fc2_b')}
    del _L0_xattn_all

    def _L0_ffn_setup():
        import jax, jax.numpy as jnp
        import numpy as np
        B, S, H, I, E_ROUTED, TOP_K = (8, 256, 128, 256, 8, 2)

        def _expert(x, Wg, Wu, Wd):
            return jax.nn.silu(x @ Wg.T) * (x @ Wu.T) @ Wd.T
        key = jax.random.key(seed)
        ks = jax.random.split(key, 9)
        s = 0.02
        return {'x': jax.random.normal(ks[0], (B, S, H), dtype=jnp.float32), 'Wg_s': jax.random.normal(ks[1], (I, H), dtype=jnp.float32) * s, 'Wu_s': jax.random.normal(ks[2], (I, H), dtype=jnp.float32) * s, 'Wd_s': jax.random.normal(ks[3], (H, I), dtype=jnp.float32) * s, 'Wg': jax.random.normal(ks[4], (E_ROUTED, I, H), dtype=jnp.float32) * s, 'Wu': jax.random.normal(ks[5], (E_ROUTED, I, H), dtype=jnp.float32) * s, 'Wd': jax.random.normal(ks[6], (E_ROUTED, H, I), dtype=jnp.float32) * s, 'Wr': jax.random.normal(ks[7], (E_ROUTED, H), dtype=jnp.float32) * s, 'rb': jnp.zeros((E_ROUTED,), dtype=jnp.float32)}
    _L0_ffn_all = _L0_ffn_setup()
    _L0_ffn_in = {k: v for k, v in _L0_ffn_all.items() if k in ('Wg_s', 'Wu_s', 'Wd_s', 'Wg', 'Wu', 'Wd', 'Wr', 'rb')}
    del _L0_ffn_all
    return {'x': x, 'ctx_1024': ctx_1024, 'mask_BxS2_bk0': mask_BxS2_bk0, 'g_xattn': g_xattn, 'g_ffn': g_ffn, 'L0_xattn_sa_wq': _L0_xattn_in['sa_wq'], 'L0_xattn_sa_wk': _L0_xattn_in['sa_wk'], 'L0_xattn_sa_wv': _L0_xattn_in['sa_wv'], 'L0_xattn_sa_wo': _L0_xattn_in['sa_wo'], 'L0_xattn_sa_bo': _L0_xattn_in['sa_bo'], 'L0_xattn_ca_wq': _L0_xattn_in['ca_wq'], 'L0_xattn_ca_wk': _L0_xattn_in['ca_wk'], 'L0_xattn_ca_wv': _L0_xattn_in['ca_wv'], 'L0_xattn_ca_wo': _L0_xattn_in['ca_wo'], 'L0_xattn_ca_bo': _L0_xattn_in['ca_bo'], 'L0_xattn_ln1_g': _L0_xattn_in['ln1_g'], 'L0_xattn_ln1_b': _L0_xattn_in['ln1_b'], 'L0_xattn_ln2_g': _L0_xattn_in['ln2_g'], 'L0_xattn_ln2_b': _L0_xattn_in['ln2_b'], 'L0_xattn_ln3_g': _L0_xattn_in['ln3_g'], 'L0_xattn_ln3_b': _L0_xattn_in['ln3_b'], 'L0_xattn_fc1_w': _L0_xattn_in['fc1_w'], 'L0_xattn_fc1_b': _L0_xattn_in['fc1_b'], 'L0_xattn_fc2_w': _L0_xattn_in['fc2_w'], 'L0_xattn_fc2_b': _L0_xattn_in['fc2_b'], 'L0_ffn_Wg_s': _L0_ffn_in['Wg_s'], 'L0_ffn_Wu_s': _L0_ffn_in['Wu_s'], 'L0_ffn_Wd_s': _L0_ffn_in['Wd_s'], 'L0_ffn_Wg': _L0_ffn_in['Wg'], 'L0_ffn_Wu': _L0_ffn_in['Wu'], 'L0_ffn_Wd': _L0_ffn_in['Wd'], 'L0_ffn_Wr': _L0_ffn_in['Wr'], 'L0_ffn_rb': _L0_ffn_in['rb']}

def reference(x, ctx_1024, mask_BxS2_bk0, g_xattn, g_ffn, L0_xattn_sa_wq, L0_xattn_sa_wk, L0_xattn_sa_wv, L0_xattn_sa_wo, L0_xattn_sa_bo, L0_xattn_ca_wq, L0_xattn_ca_wk, L0_xattn_ca_wv, L0_xattn_ca_wo, L0_xattn_ca_bo, L0_xattn_ln1_g, L0_xattn_ln1_b, L0_xattn_ln2_g, L0_xattn_ln2_b, L0_xattn_ln3_g, L0_xattn_ln3_b, L0_xattn_fc1_w, L0_xattn_fc1_b, L0_xattn_fc2_w, L0_xattn_fc2_b, L0_ffn_Wg_s, L0_ffn_Wu_s, L0_ffn_Wd_s, L0_ffn_Wg, L0_ffn_Wu, L0_ffn_Wd, L0_ffn_Wr, L0_ffn_rb):
    import jax
    import jax.numpy as jnp

    def _L0_xattn_ref(x, enc_output, sa_wq, sa_wk, sa_wv, sa_wo, sa_bo, ca_wq, ca_wk, ca_wv, ca_wo, ca_bo, ln1_g, ln1_b, ln2_g, ln2_b, ln3_g, ln3_b, fc1_w, fc1_b, fc2_w, fc2_b, tgt_mask, src_mask):
        import jax, jax.numpy as jnp
        import numpy as np
        B, S, D = (2, 256, 128)
        H, DH = (16, 64)
        INNER = H * DH
        FF = 512
        SCALE = DH ** (-0.5)
        EPS = 1e-05

        def layernorm(x, g, b):
            m = jnp.mean(x, axis=-1, keepdims=True)
            v = jnp.var(x, axis=-1, keepdims=True)
            return (x - m) * jax.lax.rsqrt(v + EPS) * g + b

        def attention(x, ctx, mask, wq, wk, wv, wo, bo):
            b, n, _ = x.shape
            j = ctx.shape[1]
            q = (x @ wq).reshape(b, n, H, DH).transpose(0, 2, 1, 3)
            k = (ctx @ wk).reshape(b, j, H, DH).transpose(0, 2, 1, 3)
            v = (ctx @ wv).reshape(b, j, H, DH).transpose(0, 2, 1, 3)
            sim = jnp.einsum('bhid,bhjd->bhij', q, k) * SCALE
            if mask is not None:
                neg = -jnp.finfo(sim.dtype).max
                sim = jnp.where(mask[:, None, None, :], neg, sim)
            attn = jax.nn.softmax(sim, axis=-1)
            out = jnp.einsum('bhij,bhjd->bhid', attn, v)
            out = out.transpose(0, 2, 1, 3).reshape(b, n, INNER)
            return out @ wo + bo
        a = attention(x, x, tgt_mask, sa_wq, sa_wk, sa_wv, sa_wo, sa_bo)
        x = layernorm(x + a, ln1_g, ln1_b)
        a = attention(x, enc_output, src_mask, ca_wq, ca_wk, ca_wv, ca_wo, ca_bo)
        x = layernorm(x + a, ln2_g, ln2_b)
        h = jax.nn.gelu(x @ fc1_w + fc1_b, approximate=False)
        ff = h @ fc2_w + fc2_b
        x = layernorm(x + ff, ln3_g, ln3_b)
        return x

    def _L0_ffn_ref(x, Wg_s, Wu_s, Wd_s, Wg, Wu, Wd, Wr, rb):
        import jax, jax.numpy as jnp
        import numpy as np
        B, S, H, I, E_ROUTED, TOP_K = (8, 256, 128, 256, 8, 2)

        def _expert(x, Wg, Wu, Wd):
            return jax.nn.silu(x @ Wg.T) * (x @ Wu.T) @ Wd.T
        shared = _expert(x, Wg_s, Wu_s, Wd_s)
        logits = jnp.einsum('bsh,eh->bse', x, Wr) + rb
        probs = jax.nn.sigmoid(logits)
        scores, idx = jax.lax.top_k(probs, TOP_K)
        cw = (jax.nn.one_hot(idx, E_ROUTED, dtype=x.dtype) * scores[..., None]).sum(-2)
        out = shared
        for e in range(E_ROUTED):
            out = out + cw[..., e:e + 1] * _expert(x, Wg[e], Wu[e], Wd[e])
        return out
    x = x + jnp.tanh(g_xattn[0]) * _L0_xattn_ref(_layernorm(x, axis=-1), ctx_1024, L0_xattn_sa_wq, L0_xattn_sa_wk, L0_xattn_sa_wv, L0_xattn_sa_wo, L0_xattn_sa_bo, L0_xattn_ca_wq, L0_xattn_ca_wk, L0_xattn_ca_wv, L0_xattn_ca_wo, L0_xattn_ca_bo, L0_xattn_ln1_g, L0_xattn_ln1_b, L0_xattn_ln2_g, L0_xattn_ln2_b, L0_xattn_ln3_g, L0_xattn_ln3_b, L0_xattn_fc1_w, L0_xattn_fc1_b, L0_xattn_fc2_w, L0_xattn_fc2_b, mask_BxS2_bk0, mask_BxS2_bk0)
    x = x + jnp.tanh(g_ffn[0]) * _L0_ffn_ref(_layernorm(x, axis=-1), L0_ffn_Wg_s, L0_ffn_Wu_s, L0_ffn_Wd_s, L0_ffn_Wg, L0_ffn_Wu, L0_ffn_Wd, L0_ffn_Wr, L0_ffn_rb)
    return x

_drawn_inputs = setup_inputs


def setup_inputs(seed=0):
    import zlib

    import numpy as np

    out = dict(_drawn_inputs(seed))
    spreads = {'L0_xattn_sa_bo': (0.0, 0.1),
     'L0_xattn_ca_bo': (0.0, 0.1),
     'L0_xattn_ln1_g': (1.0, 0.2),
     'L0_xattn_ln1_b': (0.0, 0.1),
     'L0_xattn_ln2_g': (1.0, 0.2),
     'L0_xattn_ln2_b': (0.0, 0.1),
     'L0_xattn_ln3_g': (1.0, 0.2),
     'L0_xattn_ln3_b': (0.0, 0.1),
     'L0_xattn_fc1_b': (0.0, 0.301),
     'L0_xattn_fc2_b': (0.0, 0.1),
     'L0_ffn_rb': (0.0, 0.8)}
    factors = {'L0_ffn_Wg_s': 8.0,
     'L0_ffn_Wu_s': 8.0,
     'L0_ffn_Wd_s': 8.0,
     'L0_ffn_Wg': 8.0,
     'L0_ffn_Wu': 8.0,
     'L0_ffn_Wd': 8.0,
     'L0_ffn_Wr': 8.0}
    for name, (base, spread) in spreads.items():
        noise = np.random.default_rng([zlib.crc32(name.encode()), seed]).standard_normal(out[name].shape)
        drawn = base * np.exp(spread * noise) if base else spread * noise
        out[name] = jnp.asarray(drawn.astype(out[name].dtype))
    for name, factor in factors.items():
        out[name] = (out[name] * factor).astype(out[name].dtype)
    return out
```

```python
from contextlib import ExitStack

import concourse.bass as bass
from concourse import mybir

ALU = mybir.AluOpType
ACT = mybir.ActivationFunctionType
AX = mybir.AxisListType
F32, F32R, F16, BF16, U8 = (mybir.dt.float32, mybir.dt.float32r, mybir.dt.float16, mybir.dt.bfloat16,
                            mybir.dt.uint8)

P = 128
B, S, D = 64, 64, 128
H, DH = 16, 64
HP = H // 2
TOK = B * S
GT = 512
NG = TOK // GT
TG = GT // P
FF, EXP, I = 512, 8, 256
EW = 3 * 2 * (EXP + 1)
EPS = 1e-5
SCALE = DH ** -0.5
MASKED = -float(2 ** 100)


class Loop:

    def __init__(self, reg, first, step, n):
        self.reg, self.first, self.step, self.n = reg, first, step, n

    def __add__(self, k):
        return Loop(self.reg, self.first + k, self.step, self.n)

    def __sub__(self, k):
        return self + (-k)


def sample(G):
    return G if isinstance(G, int) else G.first


class Count:

    def __init__(self, groups, order, each=1):
        self.n, total = {}, 0
        for g in groups:
            for ev in order(g):
                total += each
                self.n[(ev, g)] = total
        self.total = total

    def after(self, ev, G):
        if isinstance(G, int):
            return self.n[(ev, G)]
        v = [self.n[(ev, G.first + G.step * i)] for i in range(G.n)]
        d = v[1] - v[0]
        assert all(v[i + 1] - v[i] == d for i in range(G.n - 1))
        return G.reg * d + v[0]


class Net:
    pass


def mm3(nc, out, w_hi, w_lo, x_hi, x_lo, start=True, stop=True):
    nc.tensor.matmul(out, w_hi, x_hi, start=start, stop=False, skip_group_check=True)
    nc.tensor.matmul(out, w_hi, x_lo, start=False, stop=False, skip_group_check=True)
    return nc.tensor.matmul(out, w_lo, x_hi, start=False, stop=stop, skip_group_check=True)


def f32(ap):
    return ap.bitcast(F32)


def row_moments(nc, dve, rows, stats, parts, mean, var, step_done, at):
    d, total, squares = parts[:, 0], parts[:, 1], parts[:, 2]
    for t in range(TG):
        ins = nc.vector.bn_stats(stats[:, t, :], rows(t))
    ins.then_inc(step_done, 1)
    dve.wait_ge(step_done, at(1))
    nc.vector.tensor_tensor(d, stats[:, :, 1], stats[:, :, 4], ALU.subtract)
    nc.vector.tensor_tensor(total, stats[:, :, 1], stats[:, :, 4], ALU.add)
    nc.vector.tensor_tensor(squares, stats[:, :, 2], stats[:, :, 5], ALU.add).then_inc(step_done, 1)
    dve.wait_ge(step_done, at(2))
    nc.vector.scalar_tensor_tensor(out=parts[:, 3], in0=d, scalar=0.25, in1=d, op0=ALU.mult, op1=ALU.mult)
    nc.vector.tensor_scalar(mean, total, 0.5, None, ALU.mult)
    nc.vector.tensor_scalar(parts[:, 4], squares, 1.0 / D, EPS, ALU.mult, ALU.add).then_inc(step_done, 1)
    dve.wait_ge(step_done, at(3))
    return nc.vector.tensor_tensor(var, parts[:, 3], parts[:, 4], ALU.add)


def prepare(nc, net, a):
    with ExitStack() as ctx:
        sb = lambda name, shape, dt=F32: ctx.enter_context(nc.sbuf_tensor(name, shape, dt))
        sem = lambda name: ctx.enter_context(nc.semaphore(name))
        raw = {(p, w): sb(f"raw_{p}_{w}", [P, 8, P]) for p in ("sa", "ca") for w in ("wq", "wk", "wv", "wo")}
        turned = {(p, w): sb(f"turned_{p}_{w}", [P, 8, P]) for p in ("sa", "ca") for w in ("wq", "wk", "wv")}
        mask_u8 = sb("mask_u8", [1, TOK], U8)
        x_in = sb("x_in", [P, NG, TG, P])
        stats = sb("p_stats", [P, TG, 6])
        parts, mean = sb("p_parts", [P, 5, TG]), sb("p_mean", [P, TG])
        var = sb("p_var", [P, TG])
        rstd = sb("p_rstd", [P, TG])
        ps = ctx.enter_context(nc.psum_tensor("p_ps", [P, 8, 512], F32))
        const_in, x_loaded, xn_stored = sem("const_in"), sem("x_loaded"), sem("xn_stored")
        w_in = {p: sem(f"w_in_{p}") for p in ("sa", "ca")}
        zeroed, ready, mask_ready, tanh_done = sem("zeroed"), sem("ready"), sem("mask_ready"), sem("tanh_done")
        pe_done, act_done, dve_done = sem("p_pe_done"), sem("p_act_done"), sem("p_dve_done")
        step_done, var_done, rstd_done, norm_done = sem("step_done"), sem("var_done"), sem("rstd_done"), sem("norm_done")

        jobs = []
        for p in ("sa", "ca"):
            jobs += [("turn", p, w, half) for w in ("wq", "wk", "wv") for half in range(2)]
            jobs += [(what, p, half, par) for what in "MN" for half in range(2) for par in range(2)]
        lo_after = {}
        for j, job in enumerate(jobs):
            if job[0] != "turn":
                lo_after[j] = len(lo_after) + 1
        x_view = a["x"].rearrange("(g t p) d -> p g t d", p=P, t=TG)
        xn_view = net.xn.rearrange("(g t p) d -> g p t d", p=P, t=TG)

        block = ctx.enter_context(nc.Block())

        @block.sync
        def _(sp):
            for p in ("sa", "ca"):
                for w in ("wq", "wk", "wv"):
                    sp.dma_start(raw[p, w][:], a[f"{p}_{w}"].rearrange("d (c n) -> d c n", n=P)).then_inc(w_in[p], 16)
                sp.dma_start(raw[p, "wo"][:], a[f"{p}_wo"].rearrange("(c p) n -> p c n", p=P)).then_inc(w_in[p], 16)
            sp.wait_ge(xn_stored, 16 * NG)

        @block.tensor
        def _(pe):
            pe.wait_ge(ready, 2)
            for j, (what, p, x, y) in enumerate(jobs):
                if j % (len(jobs) // 2) == 0:
                    pe.wait_ge(w_in[p], 16 * 4)
                if j >= 8:
                    pe.wait_ge(act_done, j - 7)
                    if j - 8 in lo_after:
                        pe.wait_ge(dve_done, lo_after[j - 8])
                if what != "turn" and x == 0 and y == 0:
                    base = 0 if p == "sa" else len(jobs) // 2
                    pe.wait_ge(act_done, base + (4 if what == "M" else 6))
                for c in range(4):
                    out = ps[:, j % 8, c * P:(c + 1) * P]
                    if what == "turn":
                        ins = nc.tensor.transpose(out, raw[p, x][:, 4 * y + c, :], net.ident[:])
                    else:
                        rows = slice(64 * y, 64 * y + 64)
                        left, right = ("wq", turned[p, "wk"]) if what == "M" else ("wv", raw[p, "wo"])
                        ins = nc.tensor.matmul(out, turned[p, left][rows, 4 * x + c, :],
                                               right[rows, 4 * x + c, :], start=True, stop=True)
                ins.then_inc(pe_done, 1)

        def composed(what, p, x, y):
            hi, lo = net.M[p] if what == "M" else net.N[p]
            heads = slice(8 * x + y, 8 * x + y + 7, 2)
            return hi[:, heads, :], lo[:, heads, :], SCALE if what == "M" else 1.0

        @block.scalar
        def _(act):
            act.dma_start(x_in[:], x_view).then_inc(x_loaded, 16)
            for j, (what, p, x, y) in enumerate(jobs):
                act.wait_ge(pe_done, j + 1)
                src = ps[:, j % 8, :].rearrange("p (c n) -> p c n", c=4)
                if what == "turn":
                    nc.scalar.activation(turned[p, x][:, 4 * y:4 * y + 4, :], src, ACT.Copy).then_inc(act_done, 1)
                else:
                    hi, lo, scale = composed(what, p, x, y)
                    nc.scalar.activation(hi, src, ACT.Copy, scale=scale).then_inc(act_done, 1)
            act.wait_ge(const_in, 16 * net.n_const)
            nc.scalar.activation(net.gates[:], net.gates_raw[:], ACT.Tanh).then_inc(tanh_done, 1)

        @block.vector
        def _(dve):
            dve.wait_ge(const_in, 16 * net.n_const)
            nc.vector.tensor_scalar(net.mask_row[:], mask_u8[:], MASKED, None, ALU.mult).then_inc(mask_ready, 1)
            for j, (what, p, x, y) in enumerate(jobs):
                if what != "turn":
                    dve.wait_ge(act_done, j + 1)
                    hi, lo, scale = composed(what, p, x, y)
                    src = ps[:, j % 8, :].rearrange("p (c n) -> p c n", c=4)
                    nc.vector.scalar_tensor_tensor(out=lo, in0=src, scalar=scale, in1=f32(hi), op0=ALU.mult,
                                                   op1=ALU.subtract).then_inc(dve_done, 1)
            nc.vector.memset(net.half_neg[:], -0.5)
            dve.wait_ge(x_loaded, 16)
            with dve.Fori(0, NG) as g:
                row_moments(nc, dve, lambda t: x_in[:, g, t, :], stats, parts, mean[:], var[:], step_done,
                            lambda n: g * 3 + n).then_inc(var_done, 1)
                dve.wait_ge(rstd_done, g + 1)
                for t in range(TG):
                    ins = nc.vector.tensor_scalar(x_in[:, g, t, :], x_in[:, g, t, :], mean[:, t:t + 1],
                                                  rstd[:, t:t + 1], ALU.subtract, ALU.mult)
                ins.then_inc(norm_done, 1)

        @block.gpsimd
        def _(pool):
            for dst, src in net.const_loads(mask_u8):
                pool.dma_start(dst, src).then_inc(const_in, 16)
            for n, ident in enumerate((net.ident, net.ident16)):
                nc.gpsimd.memset(ident[:], 0.0).then_inc(zeroed, 1)
                pool.wait_ge(zeroed, n + 1)
                nc.gpsimd.affine_select(out=ident[:], in_=ident[:], compare_op=ALU.not_equal, fill=1.0, base=0,
                                        pattern=[[-1, P]], channel_multiplier=1).then_inc(ready, 1)
            nc.gpsimd.memset(net.ones_row[:], 1.0).then_inc(zeroed, 1)
            with pool.Fori(0, NG) as g:
                pool.wait_ge(var_done, g + 1)
                nc.gpsimd.tensor_tensor(rstd[:], var[:], net.half_neg[:], ALU.pow).then_inc(rstd_done, 1)
                pool.wait_ge(norm_done, g + 1)
                pool.dma_start(xn_view[g], x_in[:, g]).then_inc(xn_stored, 16)


def attention(nc, net, p, x, ctx_dram, gain, bias, out):
    K = TG
    with ExitStack() as ctx:
        sb = lambda name, shape, dt=F32: ctx.enter_context(nc.sbuf_tensor(f"{p}_{name}", shape, dt))
        sem = lambda name: ctx.enter_context(nc.semaphore(f"{p}_{name}"))
        x_nat, c_nat, res = sb("x_nat", [P, TG, P]), sb("c_nat", [P, TG, P]), sb("res", [P, TG, P])
        xT_hi, xT_lo = sb("xT_hi", [P, GT], F32R), sb("xT_lo", [P, GT], F32R)
        cT_hi, cT_lo = sb("cT_hi", [P, GT], F32R), sb("cT_lo", [P, GT], F32R)
        c16_hi, c16_lo = sb("c16_hi", [P, GT], F16), sb("c16_lo", [P, GT], F16)
        q_hi, q_lo = sb("q_hi", [P, 2, 8, H, S], F16), sb("q_lo", [P, 2, 8, H, S], F16)
        v_hi, v_lo = sb("v_hi", [P, 2, H, P], F16), sb("v_lo", [P, 2, H, P], F16)
        prob = sb("prob", [P, 2, HP, S])
        p_hi, p_lo = sb("p_hi", [P, 2, HP, 2, S], F16), sb("p_lo", [P, 2, HP, 2, S], F16)
        pT_hi, pT_lo = sb("pT_hi", [P, HP, P], F16), sb("pT_lo", [P, HP, P], F16)
        yT = sb("yT", [P, GT])
        z = sb("z", [P, TG, P])
        top, total, rtotal = sb("top", [P, 2, HP]), sb("total", [P, 2, HP]), sb("rtotal", [P, 2, HP])
        stats, parts = sb("stats", [P, TG, 6]), sb("parts", [P, 5, TG])
        mean, var, rstd = sb("mean", [P, TG]), sb("var", [P, TG]), sb("rstd", [P, TG])

        score_ps = ctx.enter_context(nc.psum_tensor(f"{p}_score_ps", [P, 2, HP, S], F32))
        turn_ps = ctx.enter_context(nc.psum_tensor(f"{p}_turn_ps", [P, HP, P], F16))
        y_ps = ctx.enter_context(nc.psum_tensor(f"{p}_y_ps", [P, 2, 512], F32))
        long_ps = ctx.enter_context(nc.psum_tensor(f"{p}_long_ps", [P, 3, 512], F32))

        def long_products(G):
            if G == -1:
                return [("x",), ("c",)] + [("q", k, j) for k in range(K) for j in range(4)]
            if G == NG:
                return [("tail",)]
            ev = []
            for k in range(K):
                ev += [("v", k, j) for j in range(4)]
                ev += [("tail",) if G > 0 else None] * (k == 1)
                if G < NG - 1:
                    ev += [("x",)] * (k == 0) + [("q", k, 0), ("q", k, 1)] + [("c",)] * (k == 3)
                    ev += [("q", k, 2), ("q", k, 3)]
            return ev

        ALL = range(-1, NG + 1)
        bank_of = {(ev, g): i % 3 for g in ALL for i, ev in enumerate(long_products(g)) if ev}

        def bank(ev, G):
            return bank_of[(ev, sample(G))]

        long_use = [Count(ALL, lambda g, b=b: [ev for ev in long_products(g) if ev and bank_of[(ev, g)] == b])
                    for b in range(3)]
        split = Count(ALL, lambda g: [ev for ev in long_products(g) if ev and ev != ("tail",)])
        slots = lambda g: range(K) if 0 <= g < NG else ()
        batch = Count(ALL, lambda g: [(k, b) for k in slots(g) for b in range(2)])
        behind = lambda g: [k for k in range(K) if 0 < K * g + k <= K * NG]
        turn = Count(ALL, lambda g: [(k, h) for k in behind(g) for h in range(2)])
        pv = Count(ALL, behind)
        tails = Count(ALL, lambda g: [()] * (g > 0))
        norm_steps = Count(ALL, lambda g: ["stats", "sums", "parts", "var", "norm"] * (g > 0))
        loads = Count(ALL, lambda g: [()] * (g < NG - 1), each=16)
        res_loads = Count(ALL, lambda g: [()] * (g > 0), each=16)
        stores = Count(list(ALL) + [NG + 1], lambda g: [()] * (g > 1), each=16)

        x_loaded, c_loaded, res_loaded, stored = sem("x_loaded"), sem("c_loaded"), sem("res_loaded"), sem("stored")
        long_full = [sem(f"long_full{b}") for b in range(3)]
        long_free = [sem(f"long_free{b}") for b in range(3)]
        hi_done = sem("hi_done")
        score_ready, shifted, exp_done = sem("score_ready"), sem("shifted"), sem("exp_done")
        top_done, sum_done, recip_done = sem("top_done"), sem("sum_done"), sem("recip_done")
        prob_done, phi_done, plo_done = sem("prob_done"), sem("phi_done"), sem("plo_done")
        turned, turn_copied = sem("turned"), sem("turn_copied")
        pv_done, y_copied = sem("pv_done"), sem("y_copied")
        step_done, rstd_done, scaled, gained = sem("step_done"), sem("rstd_done"), sem("scaled"), sem("gained")

        def long_done(eng, ev, G):
            eng.wait_ge(long_full[bank(ev, G)], long_use[bank(ev, G)].after(ev, G))

        def long_read(eng, ev, G):
            eng.wait_ge(long_free[bank(ev, G)], long_use[bank(ev, G)].after(ev, G))

        before = lambda k, G: (k - 1, G) if k else (K - 1, G - 1)
        number = lambda k, G: K * sample(G) + k
        x_view, c_view, out_view = (t.rearrange("(g t p) d -> g p t d", p=P, t=TG) for t in (x, ctx_dram, out))
        M_hi, M_lo = net.M[p]
        N_hi, N_lo = net.N[p]
        index = lambda G: G if isinstance(G, int) else G.reg * G.step + G.first

        def over_groups(eng, body, first=1, last=NG - 2):
            body(-1)
            body(0)
            with eng.Fori(0, (last - first + 1) // 2) as i:
                for par in range(2):
                    body(Loop(i, first + par, 2, (last - first + 1) // 2))
            body(NG - 1)
            body(NG)

        block = ctx.enter_context(nc.Block())

        @block.sync
        def _(sp):
            def group(G):
                g = sample(G)
                if g > 1:
                    sp.wait_ge(gained, tails.after((), G - 1))
                    sp.dma_start(out_view[index(G - 2)], z[:]).then_inc(stored, 16)
                if g < NG - 1:
                    if g >= 0:
                        long_done(sp, ("x",), G - 1)
                    sp.dma_start(x_nat[:], x_view[index(G + 1)]).then_inc(x_loaded, 16)
                    if g >= 0:
                        long_done(sp, ("c",), G - 1)
                    sp.dma_start(c_nat[:], c_view[index(G + 1)]).then_inc(c_loaded, 16)
                if g > 0:
                    if g > 1:
                        long_read(sp, ("tail",), G - 1)
                    sp.dma_start(res[:], x_view[index(G - 1)]).then_inc(res_loaded, 16)

            for g in (-1, 0, 1):
                group(g)
            with sp.Fori(0, NG - 3) as i:
                group(Loop(i, 2, 1, NG - 3))
            group(NG - 1)
            group(NG)
            sp.wait_ge(gained, tails.after((), NG))
            sp.dma_start(out_view[NG - 1], z[:]).then_inc(stored, 16)
            sp.wait_ge(stored, 16 * NG)

        @block.tensor
        def _(pe):
            def take(ev, G):
                b = bank(ev, G)
                n = long_use[b].after(ev, G)
                if sample(G) > -1 or n > 1:
                    pe.wait_ge(long_free[b], n - 1)
                return long_ps[:, b, :]

            def turn_tiles(ev, G, src):
                pe.wait_ge(x_loaded if ev == ("x",) else c_loaded, loads.after((), G))
                out = take(ev, G)
                for t in range(TG):
                    ins = nc.tensor.transpose(out[:, t * P:(t + 1) * P], src[:, t, :], net.ident[:])
                ins.then_inc(long_full[bank(ev, G)], 1)
                return ins

            def x_product(k, j, G):
                ev, h = ("q", k, j), 4 * k + j
                out = take(ev, G)
                if (k, j) == (0, 0):
                    long_read(pe, ("x",), G)
                mm3(nc, out, M_hi[:, h, :], M_lo[:, h, :], xT_hi[:], xT_lo[:]).then_inc(long_full[bank(ev, G)], 1)

            def ctx_product(k, j, G):
                ev, hs, toks = ("v", k, j), slice(4 * j, 4 * j + 4), slice(k * P, (k + 1) * P)
                out = take(ev, G)
                if (k, j) == (0, 0):
                    long_read(pe, ("c",), G - 1)
                mm3(nc, out, cT_hi[:, toks], cT_lo[:, toks], N_hi[:, hs, :], N_lo[:, hs, :])\
                    .then_inc(long_full[bank(ev, G)], 1)

            def scores(k, b, G, par):
                if (k, b) == (0, 0):
                    long_read(pe, ("q", K - 1, 3), G - 1)
                if number(k, G) > 0:
                    pe.wait_ge(shifted, batch.after((k, b), G) - 2)
                n = 2 * k + b
                keys = slice(n * S, (n + 1) * S)
                for c in range(HP):
                    mm3(nc, score_ps[:, b, c, :], q_hi[:, par, n, 2 * c:2 * c + 2, :], q_lo[:, par, n, 2 * c:2 * c + 2, :],
                        c16_hi[:, keys], c16_lo[:, keys], start=(c == 0), stop=False)
                at = index(G) * GT + n * S
                row = net.mask_row[0:1, bass.ds(at, S)].unsqueeze(1).to_broadcast([1, HP, S])
                nc.tensor.matmul(score_ps[:, b, :, :], net.ones_row[:], row, start=False, stop=True,
                                 skip_group_check=True).then_inc(score_ready, 1)

            def turn_probs(k, half, G, par):
                kb, Gb = before(k, G)
                pe.wait_ge(plo_done if half else phi_done, batch.after((kb, 1), Gb))
                if number(k, G) > 1 or half:
                    pe.wait_ge(turn_copied, turn.after((k, half), G) - 1)
                src = (p_lo if half else p_hi)[:, kb % 2]
                for c in range(HP):
                    ins = nc.tensor.transpose(turn_ps[:, c, :], src[:, c, :, :], net.ident16[:])
                ins.then_inc(turned, 1)

            def prob_product(k, G):
                kb, Gb = before(k, G)
                pe.wait_ge(turn_copied, turn.after((k, 1), G))
                if number(k, G) > 1:
                    pe.wait_ge(y_copied, pv.after(k, G) - 1)
                for h in range(H):
                    for x_hi, w_hi, b in ((1, 1, 0), (1, 1, 1), (0, 1, 0), (0, 1, 1), (1, 0, 0), (1, 0, 1)):
                        rows = slice(64 * b, 64 * b + 64)
                        w = (v_hi if w_hi else v_lo)[rows, kb % 2, h, :]
                        x = (pT_hi if x_hi else pT_lo)[rows, h // 2, 64 * (h % 2):64 * (h % 2) + 64]
                        ins = nc.tensor.matmul(y_ps[:, b, 0:S], w, x, start=bool(h == 0 and x_hi and w_hi),
                                               stop=bool(h == H - 1 and not w_hi))
                ins.then_inc(pv_done, 1)

            def turn_y(G):
                out = take(("tail",), G)
                pe.wait_ge(y_copied, pv.after(0, G))
                for t in range(TG):
                    ins = nc.tensor.transpose(out[:, t * P:(t + 1) * P], yT[:, t * P:(t + 1) * P], net.ident[:])
                ins.then_inc(long_full[bank(("tail",), G)], 1)

            def group(G):
                g = sample(G)
                par = g % 2
                if g == -1:
                    turn_tiles(("x",), G, x_nat)
                    turn_tiles(("c",), G, c_nat)
                    for k in range(K):
                        for j in range(4):
                            x_product(k, j, G)
                    return
                if g == NG:
                    turn_probs(0, 0, G, 0)
                    turn_probs(0, 1, G, 0)
                    prob_product(0, G)
                    turn_y(G)
                    return
                for k in range(K):
                    scores(k, 0, G, par)
                    ctx_product(k, 0, G)
                    ctx_product(k, 1, G)
                    scores(k, 1, G, par)
                    ctx_product(k, 2, G)
                    ctx_product(k, 3, G)
                    if k == 1 and g > 0:
                        turn_y(G)
                    if k == 0 and g < NG - 1:
                        turn_tiles(("x",), G, x_nat)
                    if number(k, G) > 0:
                        turn_probs(k, 0, G, 0)
                    if g < NG - 1:
                        x_product(k, 0, G)
                        x_product(k, 1, G)
                        if k == 3:
                            turn_tiles(("c",), G, c_nat)
                    if number(k, G) > 0:
                        turn_probs(k, 1, G, 0)
                    if g < NG - 1:
                        x_product(k, 2, G)
                        x_product(k, 3, G)
                    if number(k, G) > 0:
                        prob_product(k, G)

            over_groups(pe, group)

        def split_parts(ev, G):
            b, g = bank(ev, G), sample(G)
            src = long_ps[:, b, :]
            if ev[0] == "x":
                return src, [(xT_hi[:], xT_lo[:])]
            if ev[0] == "c":
                return src, [(cT_hi[:], cT_lo[:]), (c16_hi[:], c16_lo[:])]
            if ev[0] == "q":
                par, h = (g + 1) % 2, 4 * ev[1] + ev[2]
                return src.rearrange("p (n s) -> p n s", n=8), [(q_hi[:, par, :, h, :], q_lo[:, par, :, h, :])]
            hs = slice(4 * ev[2], 4 * ev[2] + 4)
            return (src.rearrange("p (h n) -> p h n", h=4),
                    [(v_hi[:, ev[1] % 2, hs, :], v_lo[:, ev[1] % 2, hs, :])])

        @block.scalar
        def _(act):
            def high(ev, G):
                long_done(act, ev, G)
                if ev[0] == "v" and ev[2] == 0 and number(ev[1], G) > 1:
                    act.wait_ge(pv_done, pv.after(*before(ev[1], G)))
                src, parts = split_parts(ev, G)
                for hi, _lo in parts:
                    ins = nc.scalar.activation(hi, src, ACT.Copy)
                ins.then_inc(hi_done, 1)

            def exponential(k, b, G):
                act.wait_ge(shifted, batch.after((k, b), G))
                nc.scalar.activation(prob[:, b], prob[:, b], ACT.Exp).then_inc(exp_done, 1)

            def prob_high(k, b, G):
                act.wait_ge(prob_done, batch.after((k, b), G))
                if number(k, G) > 1 and b == 0:
                    act.wait_ge(turned, turn.after((before(k, G)[0], 1), before(k, G)[1]))
                nc.scalar.activation(p_hi[:, k % 2, :, b, :], prob[:, b], ACT.Copy).then_inc(phi_done, 1)

            def copy_turned(k, half, G):
                act.wait_ge(turned, turn.after((k, half), G))
                if number(k, G) > 1:
                    act.wait_ge(pv_done, pv.after(k, G) - 1)
                nc.scalar.activation((pT_lo if half else pT_hi)[:], turn_ps[:], ACT.Copy).then_inc(turn_copied, 1)

            def copy_y(k, G):
                act.wait_ge(pv_done, pv.after(k, G))
                col = ((k - 1) % K) * P
                if k == 1 and sample(G) > 0:
                    long_done(act, ("tail",), G)
                nc.scalar.activation(yT[:, col:col + P].rearrange("p (b s) -> p b s", b=2), y_ps[:, :, 0:S],
                                     ACT.Identity, bias=net.out_bias[p][:, 0:1]).then_inc(y_copied, 1)

            def group(G):
                g = sample(G)
                if g == -1:
                    for ev in long_products(g):
                        high(ev, G)
                    return
                for k in range(K if g < NG else 1):
                    if g < NG:
                        high(("v", k, 0), G)
                        high(("v", k, 1), G)
                    if number(k, G) > 1:
                        copy_y(*before(k, G))
                    if g < NG:
                        exponential(k, 0, G)
                        high(("v", k, 2), G)
                        high(("v", k, 3), G)
                        if k == 0 and g < NG - 1:
                            high(("x",), G)
                        prob_high(k, 0, G)
                        exponential(k, 1, G)
                    if number(k, G) > 0:
                        copy_turned(k, 0, G)
                    if g < NG - 1:
                        high(("q", k, 0), G)
                        high(("q", k, 1), G)
                        if k == 3:
                            high(("c",), G)
                    if number(k, G) > 0:
                        copy_turned(k, 1, G)
                    if g < NG - 1:
                        high(("q", k, 2), G)
                        high(("q", k, 3), G)
                    if g < NG:
                        prob_high(k, 1, G)
                if g == NG:
                    copy_y(0, G)

            over_groups(act, group)

        @block.vector
        def _(dve):
            def low(ev, G):
                b = bank(ev, G)
                dve.wait_ge(hi_done, split.after(ev, G))
                src, parts = split_parts(ev, G)
                for hi, lo in parts:
                    hi = f32(hi) if ev[0] in "xc" and hi is parts[0][0] else hi
                    ins = nc.vector.tensor_tensor(lo, src, hi, ALU.subtract)
                ins.then_inc(long_free[b], 1)

            def shift(k, b, G):
                n = batch.after((k, b), G)
                dve.wait_ge(score_ready, n)
                nc.vector.tensor_reduce(top[:, b, :], score_ps[:, b], AX.X, ALU.max).then_inc(top_done, 1)
                if number(k, G) > 0:
                    dve.wait_ge(plo_done, n - 2)
                dve.wait_ge(top_done, n)
                nc.vector.tensor_tensor(prob[:, b], score_ps[:, b], top[:, b, :].unsqueeze(2).to_broadcast([P, HP, S]),
                                        ALU.subtract).then_inc(shifted, 1)

            def totals(k, b, G):
                n = batch.after((k, b), G)
                dve.wait_ge(exp_done, n)
                nc.vector.tensor_reduce(total[:, b, :], prob[:, b], AX.X, ALU.add).then_inc(sum_done, 1)
                dve.wait_ge(sum_done, n)
                nc.vector.reciprocal(rtotal[:, b, :], total[:, b, :]).then_inc(recip_done, 1)

            def residual(G):
                b = bank(("tail",), G)
                dve.wait_ge(res_loaded, res_loads.after((), G))
                if sample(G) > 1:
                    dve.wait_ge(stored, stores.after((), G))
                long_done(dve, ("tail",), G)
                nc.vector.tensor_tensor(z[:], long_ps[:, b, :].rearrange("p (t n) -> p t n", t=TG), res[:],
                                        ALU.add).then_inc(long_free[b], 1)

            def moments(G):
                long_read(dve, ("tail",), G)
                row_moments(nc, dve, lambda t: z[:, t, :], stats, parts, mean[:], var[:], step_done,
                            lambda n: norm_steps.after(("stats", "sums", "parts")[n - 1], G)).then_inc(step_done, 1)

            def normed(G):
                dve.wait_ge(rstd_done, tails.after((), G))
                for t in range(TG):
                    ins = nc.vector.tensor_scalar(z[:, t, :], z[:, t, :], mean[:, t:t + 1], rstd[:, t:t + 1],
                                                  ALU.subtract, ALU.mult)
                ins.then_inc(step_done, 1)

            def group(G):
                g = sample(G)
                if g == -1:
                    for ev in long_products(g):
                        low(ev, G)
                    return
                if g == NG:
                    residual(G)
                    moments(G)
                    normed(G)
                    return
                for k in range(K):
                    shift(k, 0, G)
                    low(("v", k, 0), G)
                    low(("v", k, 1), G)
                    totals(k, 0, G)
                    shift(k, 1, G)
                    low(("v", k, 2), G)
                    low(("v", k, 3), G)
                    if k == 0 and g < NG - 1:
                        low(("x",), G)
                    if k == 1 and g > 0:
                        residual(G)
                    totals(k, 1, G)
                    if g < NG - 1:
                        low(("q", k, 0), G)
                        low(("q", k, 1), G)
                        if k == 3:
                            low(("c",), G)
                        low(("q", k, 2), G)
                        low(("q", k, 3), G)
                    if k == 2 and g > 0:
                        moments(G)
                    if k == 3 and g > 0:
                        normed(G)

            over_groups(dve, group)

        @block.gpsimd
        def _(pool):
            def probabilities(k, b, G):
                n = batch.after((k, b), G)
                pool.wait_ge(recip_done, n)
                nc.gpsimd.tensor_tensor(prob[:, b], prob[:, b], rtotal[:, b, :].unsqueeze(2).to_broadcast([P, HP, S]),
                                        ALU.mult).then_inc(prob_done, 1)

            def prob_low(k, b, G):
                pool.wait_ge(phi_done, batch.after((k, b), G))
                nc.gpsimd.tensor_tensor(p_lo[:, k % 2, :, b, :], prob[:, b], p_hi[:, k % 2, :, b, :],
                                        ALU.subtract).then_inc(plo_done, 1)

            def root(G):
                pool.wait_ge(step_done, norm_steps.after("var", G))
                nc.gpsimd.tensor_tensor(rstd[:], var[:], net.half_neg[:], ALU.pow).then_inc(rstd_done, 1)

            def gain_and_bias(G):
                pool.wait_ge(step_done, norm_steps.after("norm", G))
                wide = lambda t: t[:].unsqueeze(1).to_broadcast([P, TG, P])
                nc.gpsimd.tensor_tensor(z[:], z[:], wide(gain), ALU.mult).then_inc(scaled, 1)
                pool.wait_ge(scaled, tails.after((), G))
                nc.gpsimd.tensor_tensor(z[:], z[:], wide(bias), ALU.add).then_inc(gained, 1)

            def group(G):
                g = sample(G)
                if g == NG:
                    root(G)
                    gain_and_bias(G)
                if not 0 <= g < NG:
                    return
                for k in range(K):
                    probabilities(k, 0, G)
                    prob_low(k, 0, G)
                    probabilities(k, 1, G)
                    prob_low(k, 1, G)
                    if k == 2 and g > 0:
                        root(G)
                    if k == 3 and g > 0:
                        gain_and_bias(G)

            over_groups(pool, group)


def feed(nc, net, a, x, out):
    NC = FF // P
    with ExitStack() as ctx:
        sb = lambda name, shape, dt=F32: ctx.enter_context(nc.sbuf_tensor(f"f_{name}", shape, dt))
        sem = lambda name: ctx.enter_context(nc.semaphore(f"f_{name}"))
        raw = sb("raw", [P, EW, P])
        raw_router = sb("raw_router", [EXP, P])
        raw_fc = sb("raw_fc", [P, 2, NC, P])
        fc_hi, fc_lo = sb("fc_hi", [P, 2, NC, P], F32R), sb("fc_lo", [P, 2, NC, P], F32R)
        x_nat, res = sb("x_nat", [P, TG, P]), sb("res", [P, TG, P])
        xT_hi, xT_lo = sb("xT_hi", [P, GT], F32R), sb("xT_lo", [P, GT], F32R)
        h = sb("h", [P, NC, GT])
        h_hi, h_lo = sb("h_hi", [P, NC, GT], F32R), sb("h_lo", [P, NC, GT], F32R)
        yT, z = sb("yT", [P, GT]), sb("z", [P, TG, P])
        ps = ctx.enter_context(nc.psum_tensor("f_ps", [P, 8, 512], F32))
        h_ps, xT_ps, y_ps, yt_ps = ps[:, 0:4], ps[:, 4], ps[:, 5], ps[:, 6]

        raw_in, router_in, fc_in = sem("raw_in"), sem("router_in"), sem("fc_in")
        w_turned, w_hi, w_lo = sem("w_turned"), sem("w_hi"), sem("w_lo")
        x_loaded, res_loaded, stored = sem("x_loaded"), sem("res_loaded"), sem("stored")
        x_turned, x_hi, x_lo = sem("x_turned"), sem("x_hi"), sem("x_lo")
        h_ready, h_act, hi_done, lo_done = sem("h_ready"), sem("h_act"), sem("hi_done"), sem("lo_done")
        y_ready, y_copied, y_turned, added = sem("y_ready"), sem("y_copied"), sem("y_turned"), sem("added")

        SLOTS = range(-1, NG + 1)
        once = lambda first, last: Count(SLOTS, lambda g: [()] * (first <= g <= last))
        turns, firsts_n, backs = once(-1, NG - 2), once(0, NG - 1), once(1, NG)
        seconds = once(1, NG)
        chunks = Count(SLOTS, lambda g: list(range(NC)) if 0 <= g < NG else [])
        jobs = [list(range(j, min(j + 4, EW))) for j in range(0, EW, 4)]
        n_jobs = len(jobs) + 1
        index = lambda G: G if isinstance(G, int) else G.reg * G.step + G.first
        x_view, out_view = (t.rearrange("(g t p) d -> g p t d", p=P, t=TG) for t in (x, out))

        def over_slots(eng, body):
            for g in (-1, 0, 1):
                body(g)
            with eng.Fori(0, NG - 3) as i:
                body(Loop(i, 2, 1, NG - 3))
            for g in (NG - 1, NG):
                body(g)

        block = ctx.enter_context(nc.Block())

        @block.sync
        def _(sp):
            sp.dma_start(x_nat[:], x_view[0]).then_inc(x_loaded, 16)
            sp.dma_start(raw_fc[:, 0], a["fc1_w"].rearrange("d (c n) -> d c n", n=P)).then_inc(fc_in, 16)
            sp.dma_start(raw_fc[:, 1], a["fc2_w"].rearrange("(c p) n -> p c n", p=P)).then_inc(fc_in, 16)
            halves = lambda t: t.rearrange("(h p) d -> p h d", p=P)
            experts_of = lambda t: t.rearrange("e (h p) d -> p (e h) d", p=P)
            for m, (shared, routed) in enumerate((("Wg_s", "Wg"), ("Wu_s", "Wu"))):
                sp.dma_start(raw[:, 18 * m:18 * m + 2], halves(a[shared])).then_inc(raw_in, 16)
                sp.dma_start(raw[:, 18 * m + 2:18 * m + 18], experts_of(a[routed])).then_inc(raw_in, 16)
            sp.dma_start(raw[:, 36:38], a["Wd_s"].rearrange("d (h i) -> d h i", i=P)).then_inc(raw_in, 16)
            for e in range(EXP):
                sp.dma_start(raw[:, 38 + 2 * e:40 + 2 * e], a["Wd"][e].rearrange("d (h i) -> d h i", i=P)).then_inc(raw_in, 16)
            sp.dma_start(raw_router[:], a["Wr"]).then_inc(router_in, 16)

            def slot(G):
                g = sample(G)
                if 0 <= g < NG - 1:
                    sp.wait_ge(x_turned, turns.after((), G - 1))
                    sp.dma_start(x_nat[:], x_view[index(G + 1)]).then_inc(x_loaded, 16)
                if g >= 1:
                    if g > 1:
                        sp.wait_ge(added, backs.after((), G - 1))
                        sp.dma_start(out_view[index(G - 2)], z[:]).then_inc(stored, 16)
                    sp.dma_start(res[:], x_view[index(G - 1)]).then_inc(res_loaded, 16)

            for g in (0, 1):
                slot(g)
            with sp.Fori(0, NG - 3) as i:
                slot(Loop(i, 2, 1, NG - 3))
            for g in (NG - 1, NG):
                slot(g)
            sp.wait_ge(added, backs.after((), NG))
            sp.dma_start(out_view[NG - 1], z[:]).then_inc(stored, 16)
            sp.wait_ge(stored, 16 * NG)

        @block.tensor
        def _(pe):
            pe.wait_ge(router_in, 16)
            nc.tensor.transpose(ps[:, 7, 0:EXP], raw_router[:], net.ident[0:EXP, 0:EXP]).then_inc(w_turned, 1)
            pe.wait_ge(raw_in, 16 * (5 + EXP))
            for j, tiles in enumerate(jobs):
                if j >= 8:
                    pe.wait_ge(w_lo, j - 6)
                if j == 7:
                    pe.wait_ge(w_lo, 1)
                for c, t in enumerate(tiles):
                    ins = nc.tensor.transpose(ps[:, j % 8, c * P:(c + 1) * P], raw[:, t, :], net.ident[:])
                ins.then_inc(w_turned, 1)
            pe.wait_ge(w_lo, n_jobs + 2)

            def slot(G):
                g = sample(G)
                if 1 <= g <= NG:
                    if g > 1:
                        pe.wait_ge(y_copied, seconds.after((), G) - 1)
                    for c in range(NC):
                        pe.wait_ge(lo_done, chunks.after(c, G - 1))
                        ins = mm3(nc, y_ps, fc_hi[:, 1, c, :], fc_lo[:, 1, c, :], h_hi[:, c, :], h_lo[:, c, :],
                                  start=(c == 0), stop=(c == NC - 1))
                    ins.then_inc(y_ready, 1)
                if 0 <= g < NG:
                    pe.wait_ge(x_lo, turns.after((), G - 1))
                    for c in range(NC):
                        if g > 0:
                            pe.wait_ge(h_act, chunks.after(c, G - 1))
                        mm3(nc, h_ps[:, c], fc_hi[:, 0, c, :], fc_lo[:, 0, c, :], xT_hi[:], xT_lo[:])\
                            .then_inc(h_ready, 1)
                if g < NG - 1:
                    pe.wait_ge(x_loaded, index(G) * 16 + 32)
                    for t in range(TG):
                        ins = nc.tensor.transpose(xT_ps[:, t * P:(t + 1) * P], x_nat[:, t, :], net.ident[:])
                    ins.then_inc(x_turned, 1)
                if g >= 1:
                    pe.wait_ge(y_copied, seconds.after((), G))
                    if g > 1:
                        pe.wait_ge(added, backs.after((), G) - 1)
                    for t in range(TG):
                        ins = nc.tensor.transpose(yt_ps[:, t * P:(t + 1) * P], yT[:, t * P:(t + 1) * P], net.ident[:])
                    ins.then_inc(y_turned, 1)

            over_slots(pe, slot)

        @block.scalar
        def _(act):
            act.wait_ge(w_turned, 1)
            nc.scalar.activation(net.router_hi[:], ps[:, 7, 0:EXP], ACT.Copy).then_inc(w_hi, 1)
            for j, tiles in enumerate(jobs):
                act.wait_ge(w_turned, j + 2)
                n = len(tiles)
                nc.scalar.activation(net.experts_hi[:, tiles[0]:tiles[0] + n, :],
                                     ps[:, j % 8, 0:n * P].rearrange("p (t n) -> p t n", n=P), ACT.Copy).then_inc(w_hi, 1)
            act.wait_ge(fc_in, 32)
            for m in range(2):
                nc.scalar.activation(fc_hi[:, m], raw_fc[:, m], ACT.Copy).then_inc(w_hi, 1)

            def slot(G):
                g = sample(G)
                if 1 <= g <= NG:
                    act.wait_ge(y_ready, seconds.after((), G))
                    if g > 1:
                        act.wait_ge(y_turned, backs.after((), G - 1))
                    nc.scalar.activation(yT[:], y_ps, ACT.Identity, bias=net.out_bias["fc2"][:, 0:1])\
                        .then_inc(y_copied, 1)
                if 0 <= g < NG:
                    for c in range(NC):
                        act.wait_ge(h_ready, chunks.after(c, G))
                        if g > 0:
                            act.wait_ge(lo_done, chunks.after(c, G - 1))
                        nc.scalar.activation(h[:, c, :], h_ps[:, c], ACT.Gelu, bias=net.fc1_bias[:, c:c + 1])\
                            .then_inc(h_act, 1)
                        if c > 0:
                            high(c - 1, G)
                    high(NC - 1, G)
                if g < NG - 1:
                    act.wait_ge(x_turned, turns.after((), G))
                    nc.scalar.activation(xT_hi[:], xT_ps, ACT.Copy).then_inc(x_hi, 1)

            def high(c, G):
                act.wait_ge(h_act, chunks.after(c, G))
                nc.scalar.activation(h_hi[:, c, :], h[:, c, :], ACT.Copy).then_inc(hi_done, 1)

            over_slots(act, slot)

        @block.vector
        def _(dve):
            dve.wait_ge(w_hi, 1)
            nc.vector.tensor_tensor(net.router_lo[:], ps[:, 7, 0:EXP], f32(net.router_hi[:]), ALU.subtract).then_inc(w_lo, 1)
            for j, tiles in enumerate(jobs):
                dve.wait_ge(w_hi, j + 2)
                n = len(tiles)
                part = slice(tiles[0], tiles[0] + n)
                nc.vector.tensor_tensor(net.experts_lo[:, part, :], ps[:, j % 8, 0:n * P].rearrange("p (t n) -> p t n", n=P),
                                        f32(net.experts_hi[:, part, :]), ALU.subtract).then_inc(w_lo, 1)
            dve.wait_ge(fc_in, 32)
            for m in range(2):
                dve.wait_ge(w_hi, n_jobs + 1 + m)
                nc.vector.tensor_tensor(fc_lo[:, m], raw_fc[:, m], f32(fc_hi[:, m]), ALU.subtract).then_inc(w_lo, 1)

            def slot(G):
                g = sample(G)
                if 0 <= g < NG:
                    for c in range(NC):
                        dve.wait_ge(hi_done, chunks.after(c, G))
                        nc.vector.tensor_tensor(h_lo[:, c, :], h[:, c, :], f32(h_hi[:, c, :]), ALU.subtract)\
                            .then_inc(lo_done, 1)
                if g < NG - 1:
                    dve.wait_ge(x_hi, turns.after((), G))
                    nc.vector.tensor_tensor(xT_lo[:], xT_ps, f32(xT_hi[:]), ALU.subtract).then_inc(x_lo, 1)
                if g >= 1:
                    dve.wait_ge(y_turned, backs.after((), G))
                    dve.wait_ge(res_loaded, index(G) * 16)
                    if g > 1:
                        dve.wait_ge(stored, index(G) * 16 - 16)
                    nc.vector.tensor_tensor(z[:], yt_ps.rearrange("p (t n) -> p t n", t=TG), res[:], ALU.add)\
                        .then_inc(added, 1)

            over_slots(dve, slot)


def experts(nc, net, a, x3, out):
    NE = EXP + 1
    with ExitStack() as ctx:
        sb = lambda name, shape, dt=F32: ctx.enter_context(nc.sbuf_tensor(f"m_{name}", shape, dt))
        sem = lambda name: ctx.enter_context(nc.semaphore(f"m_{name}"))
        x_in, z, r, m = sb("x_in", [P, TG, P]), sb("z", [P, TG, P]), sb("r", [P, 2, TG, P]), sb("m", [P, TG, P])
        xT_hi, xT_lo = sb("xT_hi", [P, 2, GT], F32R), sb("xT_lo", [P, 2, GT], F32R)
        cw_wide = sb("cw_wide", [P, 2, EXP, GT])
        act_g, h = sb("act_g", [P, 3, 2, GT]), sb("h", [P, 3, 2, GT])
        h_hi, h_lo = sb("h_hi", [P, 3, 2, GT], F32R), sb("h_lo", [P, 3, 2, GT], F32R)
        yT, o = sb("yT", [P, GT]), sb("o", [P, TG, P])
        stats, parts = sb("stats", [P, TG, 6]), sb("parts", [P, 5, TG])
        mean, var, rstd = sb("mean", [P, TG]), sb("var", [P, TG]), sb("rstd", [P, TG])
        logit, e_neg, prob = sb("logit", [P, TG, EXP]), sb("e_neg", [P, TG, EXP]), sb("prob", [P, TG, EXP])
        e_base = sb("e_base", [P, TG, EXP])
        above, equal = sb("above", [P, TG, EXP, EXP]), sb("equal", [P, TG, EXP, EXP])
        earlier, later = sb("earlier", [P, EXP, EXP]), sb("later", [P, EXP, EXP])
        rank, cw, cwT = sb("rank", [P, TG, EXP]), sb("cw", [P, TG, EXP]), sb("cwT", [EXP, GT])
        cw_dram = nc.dram_tensor("cw_dram", (NG, EXP, GT), F32, kind="Internal").ap()
        psum = lambda name, n: ctx.enter_context(nc.psum_tensor(f"m_{name}_ps", [P, n, 512], F32))
        gate_ps, up_ps, y_ps, turn_ps, logit_ps = psum("gate", 2), psum("up", 2), psum("y", 2), psum("turn", 1), psum("logit", 1)

        SLOTS = range(-1, NG + 1)
        expert = Count(SLOTS, lambda g: list(range(NE)) if 0 <= g < NG else [])
        half = Count(SLOTS, lambda g: [(j, n) for j in range(NE) for n in range(2)] if 0 <= g < NG else [])
        routed = Count(SLOTS, lambda g: [(j, n) for j in range(1, NE) for n in range(2)] if 0 <= g < NG else [])
        pre = Count(SLOTS, lambda g: [()] * (g < NG - 1))
        post = Count(SLOTS, lambda g: [()] * (g > 0))
        turns = Count(SLOTS, lambda g: ["y"] * (g > 0) + ["x", "cw"] * (g < NG - 1))
        NORM3 = ["3 stats", "3 sums", "3 parts", "3 var", "3 norm"]
        NORM_M = ["r", "m stats", "m sums", "m parts", "m var", "m norm"]
        ROUTE = ["logit", "one more", "prob", "compare", "masked", "sum", "rank", "cw"]
        steps = Count(SLOTS, lambda g: (NORM3 + NORM_M + ROUTE) * (g < NG - 1))
        roots = Count(SLOTS, lambda g: ["3", "m"] * (g < NG - 1))

        x3_loaded, x_loaded, cw_saved, stored = sem("x3_loaded"), sem("x_loaded"), sem("cw_saved"), sem("stored")
        cw_loaded = [sem(f"cw_loaded{n}") for n in range(2)]
        gate_ready, up_ready, y_ready = sem("gate_ready"), sem("up_ready"), sem("down_done")
        silu_done, weighted, h_done, hi_done, lo_done = sem("silu_done"), sem("weighted"), sem("h_done"), sem("hi_done"), sem("lo_done")
        step, root_done, scaled, gained = sem("step"), sem("root_done"), sem("scaled"), sem("gained")
        turned, x_hi, x_lo, cw_copied = sem("turned"), sem("x_hi"), sem("x_lo"), sem("cw_copied")
        logits_ready, e_done, y_copied, o_done = sem("logits_ready"), sem("e_done"), sem("y_copied"), sem("o_done")
        consts = sem("consts")

        index = lambda G: G if isinstance(G, int) else G.reg * G.step + G.first
        x_view, x3_view, out_view = (t.rearrange("(g t p) d -> g p t d", p=P, t=TG) for t in (a["x"], x3, out))
        weights = lambda matrix, j, n: (net.experts_hi[:, 18 * matrix + 2 * j + n, :], net.experts_lo[:, 18 * matrix + 2 * j + n, :])

        def lag(j, G, n):
            return (j - n, G) if j >= n else (j - n + NE, G - 1)

        def over_slots(eng, body):
            body(-1)
            body(0)
            with eng.Fori(0, NG // 2 - 1) as i:
                for par in range(2):
                    body(Loop(i, 1 + par, 2, NG // 2 - 1))
            body(NG - 1)
            body(NG)

        block = ctx.enter_context(nc.Block())

        @block.sync
        def _(sp):
            def slot(G):
                g = sample(G)
                if g < NG - 1:
                    if g >= 0:
                        sp.wait_ge(step, steps.after("r", G - 1))
                    sp.dma_start(z[:], x3_view[index(G + 1)]).then_inc(x3_loaded, 16)
                    sp.dma_start(x_in[:], x_view[index(G + 1)]).then_inc(x_loaded, 16)
                if g > 0:
                    sp.wait_ge(o_done, post.after((), G))
                    sp.dma_start(out_view[index(G - 1)], o[:]).then_inc(stored, 16)
                if g < NG - 1:
                    sp.wait_ge(cw_copied, pre.after((), G))
                    sp.dma_start(cw_dram[index(G + 1)], cwT[:]).then_inc(cw_saved, 16)
                    if g > 0:
                        sp.wait_ge(weighted, routed.after((NE - 1, 1), G - 1))
                    sp.wait_ge(cw_saved, index(G) * 16 + 32)
                    for n in range(2):
                        src = cw_dram[index(G + 1), 4 * n:4 * n + 4, :].rearrange("(o e) t -> o e t", o=1)
                        sp.dma_start(cw_wide[:, (g + 1) % 2, 4 * n:4 * n + 4, :], src.to_broadcast([P, 4, GT]))\
                            .then_inc(cw_loaded[n], 16)

            over_slots(sp, slot)
            sp.wait_ge(stored, 16 * NG)

        @block.tensor
        def _(pe):
            def gates_and_ups(j, G):
                par = sample(G) % 2
                if j == 0:
                    pe.wait_ge(x_lo, pre.after((), G - 1))
                for matrix, ps, ready, free in ((0, gate_ps, gate_ready, silu_done), (1, up_ps, up_ready, h_done)):
                    for n in range(2):
                        if j or sample(G):
                            jb, Gb = lag(j, G, 1)
                            pe.wait_ge(free, half.after((jb, n), Gb))
                        mm3(nc, ps[:, n, :], *weights(matrix, j, n), xT_hi[:, par, :], xT_lo[:, par, :]).then_inc(ready, 1)

            def down(j, G):
                if j == 0 and sample(G) > 1:
                    pe.wait_ge(y_copied, post.after((), G - 1))
                for n in range(2):
                    pe.wait_ge(lo_done, half.after((j, n), G))
                    ins = mm3(nc, y_ps[:, sample(G) % 2, :], *weights(2, j, n), h_hi[:, j % 3, n, :], h_lo[:, j % 3, n, :],
                              start=(j == 0 and n == 0), stop=(j == NE - 1 and n == 1))
                ins.then_inc(y_ready, 1)

            def turn_y(G):
                pe.wait_ge(y_copied, post.after((), G))
                if sample(G) < NG:
                    pe.wait_ge(cw_copied, pre.after((), G - 1))
                else:
                    pe.wait_ge(o_done, post.after((), G - 1))
                for t in range(TG):
                    ins = nc.tensor.transpose(turn_ps[:, 0, t * P:(t + 1) * P], yT[:, t * P:(t + 1) * P], net.ident[:])
                ins.then_inc(turned, 1)

            def turn_x(G):
                pe.wait_ge(step, steps.after("m norm", G))
                if sample(G) > 0:
                    pe.wait_ge(o_done, post.after((), G))
                elif sample(G) == 0:
                    pe.wait_ge(cw_copied, pre.after((), G - 1))
                for t in range(TG):
                    ins = nc.tensor.transpose(turn_ps[:, 0, t * P:(t + 1) * P], m[:, t, :], net.ident[:])
                ins.then_inc(turned, 1)

            def logits(G):
                par = (sample(G) + 1) % 2
                pe.wait_ge(x_lo, pre.after((), G))
                if sample(G) >= 0:
                    pe.wait_ge(step, steps.after("logit", G - 1))
                for t in range(TG):
                    toks = slice(t * P, (t + 1) * P)
                    ins = mm3(nc, logit_ps[:, 0, t * EXP:(t + 1) * EXP], xT_hi[:, par, toks], xT_lo[:, par, toks],
                              net.router_hi[:], net.router_lo[:])
                ins.then_inc(logits_ready, 1)

            def turn_cw(G):
                pe.wait_ge(step, steps.after("cw", G))
                for t in range(TG):
                    ins = nc.tensor.transpose(turn_ps[0:EXP, 0, t * P:(t + 1) * P], cw[:, t, :], net.ident[:])
                ins.then_inc(turned, 1)

            def slot(G):
                g = sample(G)
                for j in range(NE):
                    if 0 <= g < NG:
                        gates_and_ups(j, G)
                    if (0 <= g < NG and (g > 0 or j >= 2)) or (g == NG and j < 2):
                        down(*lag(j, G, 2))
                    if j == 2 and g > 0:
                        turn_y(G)
                    if g < NG - 1:
                        if j == 4:
                            turn_x(G)
                        if j == 5:
                            logits(G)
                        if j == 7:
                            turn_cw(G)

            over_slots(pe, slot)

        @block.scalar
        def _(act):
            def silu(j, n, G):
                act.wait_ge(gate_ready, half.after((j, n), G))
                if j >= 3 or sample(G) > 0:
                    jb, Gb = lag(j, G, 3)
                    act.wait_ge(h_done, half.after((jb, n), Gb))
                nc.scalar.activation(act_g[:, j % 3, n, :], gate_ps[:, n, :], ACT.Silu).then_inc(silu_done, 1)

            def high(j, n, G):
                act.wait_ge(h_done, half.after((j, n), G))
                if j >= 3 or sample(G) > 0:
                    jb, Gb = lag(j, G, 3)
                    act.wait_ge(y_ready, expert.after(jb, Gb))
                nc.scalar.activation(h_hi[:, j % 3, n, :], h[:, j % 3, n, :], ACT.Copy).then_inc(hi_done, 1)

            def copy_y(G):
                act.wait_ge(y_ready, expert.after(NE - 1, G - 1))
                if sample(G) > 1:
                    act.wait_ge(turned, turns.after("y", G - 1))
                nc.scalar.activation(yT[:], y_ps[:, (sample(G) - 1) % 2, :], ACT.Copy).then_inc(y_copied, 1)

            def x_high(G):
                act.wait_ge(turned, turns.after("x", G))
                nc.scalar.activation(xT_hi[:, (sample(G) + 1) % 2, :], turn_ps[:, 0, :], ACT.Copy).then_inc(x_hi, 1)

            def copy_cw(G):
                act.wait_ge(turned, turns.after("cw", G))
                if sample(G) >= 0:
                    act.wait_ge(cw_saved, index(G) * 16 + 16)
                nc.scalar.activation(cwT[:], turn_ps[0:EXP, 0, :], ACT.Copy).then_inc(cw_copied, 1)

            def slot(G):
                g = sample(G)
                for j in range(NE):
                    if 0 <= g < NG:
                        silu(j, 0, G)
                        silu(j, 1, G)
                        high(j, 0, G)
                        high(j, 1, G)
                    if j == 1 and g > 0:
                        copy_y(G)
                    if g < NG - 1:
                        if j == 4:
                            x_high(G)
                        if j == 7:
                            copy_cw(G)

            over_slots(act, slot)

        @block.vector
        def _(dve):
            nc.vector.memset(e_base[:], 1 / 2.718281828459045)
            dve.wait_ge(consts, 4)

            def product(j, n, G):
                dve.wait_ge(up_ready, half.after((j, n), G))
                if j == 0:
                    dve.wait_ge(silu_done, half.after((j, n), G))
                else:
                    dve.wait_ge(weighted, routed.after((j, n), G))
                nc.vector.tensor_tensor(h[:, j % 3, n, :], up_ps[:, n, :], act_g[:, j % 3, n, :], ALU.mult).then_inc(h_done, 1)

            def low(j, n, G):
                dve.wait_ge(hi_done, half.after((j, n), G))
                nc.vector.tensor_tensor(h_lo[:, j % 3, n, :], h[:, j % 3, n, :], f32(h_hi[:, j % 3, n, :]),
                                        ALU.subtract).then_inc(lo_done, 1)

            def output(G):
                dve.wait_ge(turned, turns.after("y", G))
                if sample(G) > 1:
                    dve.wait_ge(stored, index(G) * 16 - 16)
                nc.vector.scalar_tensor_tensor(out=o[:], in0=turn_ps[:, 0, :].rearrange("p (t n) -> p t n", t=TG),
                                               scalar=net.gates[:, 1:2], in1=r[:, (sample(G) - 1) % 2], op0=ALU.mult,
                                               op1=ALU.add).then_inc(o_done, 1)

            def moments(G, rows, names):
                row_moments(nc, dve, rows, stats, parts, mean[:], var[:], step,
                            lambda n: steps.after(names[n - 1], G)).then_inc(step, 1)

            def normed(G, src, dst, root):
                dve.wait_ge(root_done, roots.after(root, G))
                for t in range(TG):
                    ins = nc.vector.tensor_scalar(dst(t), src(t), mean[:, t:t + 1], rstd[:, t:t + 1], ALU.subtract, ALU.mult)
                ins.then_inc(step, 1)

            def gated(G):
                dve.wait_ge(gained, pre.after((), G))
                dve.wait_ge(x_loaded, index(G) * 16 + 32)
                nc.vector.scalar_tensor_tensor(out=r[:, (sample(G) + 1) % 2], in0=z[:], scalar=net.gates[:, 0:1], in1=x_in[:],
                                               op0=ALU.mult, op1=ALU.add).then_inc(step, 1)
                dve.wait_ge(step, steps.after("r", G))

            def x_low(G):
                par = (sample(G) + 1) % 2
                dve.wait_ge(x_hi, pre.after((), G))
                nc.vector.tensor_tensor(xT_lo[:, par, :], turn_ps[:, 0, :], f32(xT_hi[:, par, :]), ALU.subtract).then_inc(x_lo, 1)

            def add_bias(G):
                dve.wait_ge(logits_ready, pre.after((), G))
                nc.vector.tensor_tensor(logit[:], logit_ps[:, 0, 0:TG * EXP].rearrange("p (t e) -> p t e", t=TG),
                                        net.router_bias[:].unsqueeze(1).to_broadcast([P, TG, EXP]), ALU.add).then_inc(step, 1)

            def route(G):
                def then(ins, name):
                    ins.then_inc(step, 1)
                    dve.wait_ge(step, steps.after(name, G))
                dve.wait_ge(e_done, pre.after((), G))
                then(nc.vector.tensor_scalar(logit[:], e_neg[:], 1.0, None, ALU.add), "one more")
                then(nc.vector.reciprocal(prob[:], logit[:]), "prob")
                other, own = prob[:].unsqueeze(2).to_broadcast([P, TG, EXP, EXP]), prob[:].unsqueeze(3).to_broadcast([P, TG, EXP, EXP])
                wide = lambda t: t[:].unsqueeze(1).to_broadcast([P, TG, EXP, EXP])
                nc.vector.tensor_tensor(equal[:], other, own, ALU.is_ge)
                then(nc.vector.tensor_tensor(above[:], other, own, ALU.is_gt), "compare")
                nc.vector.tensor_tensor(equal[:], equal[:], wide(earlier), ALU.mult)
                then(nc.vector.tensor_tensor(above[:], above[:], wide(later), ALU.mult), "masked")
                then(nc.vector.tensor_tensor(above[:], above[:], equal[:], ALU.add), "sum")
                then(nc.vector.tensor_reduce(rank[:], above[:], AX.X, ALU.add), "rank")
                nc.vector.scalar_tensor_tensor(out=cw[:], in0=rank[:], scalar=1.5, in1=prob[:], op0=ALU.is_lt,
                                               op1=ALU.mult).then_inc(step, 1)

            def slot(G):
                g = sample(G)
                for j in range(NE):
                    if 0 <= g < NG:
                        product(j, 0, G)
                        product(j, 1, G)
                        low(j, 0, G)
                        low(j, 1, G)
                    if j == 2 and g > 0:
                        output(G)
                    if g >= NG - 1:
                        continue
                    if j == 0:
                        dve.wait_ge(x3_loaded, index(G) * 16 + 32)
                        moments(G, lambda t: z[:, t, :], NORM3)
                    if j == 1:
                        normed(G, lambda t: z[:, t, :], lambda t: z[:, t, :], "3")
                    if j == 3:
                        gated(G)
                        moments(G, lambda t: r[:, (sample(G) + 1) % 2, t, :], NORM_M[1:])
                    if j == 4:
                        normed(G, lambda t: r[:, (sample(G) + 1) % 2, t, :], lambda t: m[:, t, :], "m")
                        x_low(G)
                    if j == 5:
                        add_bias(G)
                    if j == 6:
                        route(G)

            over_slots(dve, slot)

        @block.gpsimd
        def _(pool):
            for n, (t, sign, keep) in enumerate(((earlier, 1, ALU.is_gt), (later, -1, ALU.is_ge))):
                nc.gpsimd.memset(t[:], 1.0).then_inc(consts, 1)
                pool.wait_ge(consts, 2 * n + 1)
                nc.gpsimd.affine_select(out=t[:], in_=t[:], compare_op=keep, fill=0.0, base=0,
                                        pattern=[[sign, EXP], [-sign, EXP]], channel_multiplier=0).then_inc(consts, 1)

            def weight(j, n, G):
                pool.wait_ge(silu_done, half.after((j, n), G))
                if n == 0 and j in (1, 5):
                    pool.wait_ge(cw_loaded[j // 5], index(G) * 16 + 16)
                nc.gpsimd.tensor_tensor(act_g[:, j % 3, n, :], act_g[:, j % 3, n, :], cw_wide[:, sample(G) % 2, j - 1, :],
                                        ALU.mult).then_inc(weighted, 1)

            def root(G, name, which):
                pool.wait_ge(step, steps.after(name, G))
                nc.gpsimd.tensor_tensor(rstd[:], var[:], net.half_neg[:], ALU.pow).then_inc(root_done, 1)

            def gain_and_bias(G):
                wide = lambda t: t[:].unsqueeze(1).to_broadcast([P, TG, P])
                pool.wait_ge(step, steps.after("3 norm", G))
                nc.gpsimd.tensor_tensor(z[:], z[:], wide(net.wide["ln3_g"]), ALU.mult).then_inc(scaled, 1)
                pool.wait_ge(scaled, pre.after((), G))
                nc.gpsimd.tensor_tensor(z[:], z[:], wide(net.wide["ln3_b"]), ALU.add).then_inc(gained, 1)

            def exponential(G):
                pool.wait_ge(step, steps.after("logit", G))
                nc.gpsimd.tensor_tensor(e_neg[:], e_base[:], logit[:], ALU.pow).then_inc(e_done, 1)

            def slot(G):
                g = sample(G)
                for j in range(NE):
                    if 0 <= g < NG and j > 0:
                        weight(j, 0, G)
                        weight(j, 1, G)
                    if g >= NG - 1:
                        continue
                    if j == 0:
                        root(G, "3 var", "3")
                    if j == 1:
                        gain_and_bias(G)
                    if j == 3:
                        root(G, "m var", "m")
                    if j == 5:
                        exponential(G)

            over_slots(pool, slot)


def program(nc, a, out, stages=4):
    with ExitStack() as ctx:
        net = Net()
        dram = lambda name, shape: nc.dram_tensor(name, shape, F32, kind="Internal").ap()
        sb = lambda name, shape, dt=F32: ctx.enter_context(nc.sbuf_tensor(name, shape, dt))
        net.xn, net.x1, net.x2, net.x3 = (dram(n, (TOK, D)) for n in ("xn", "x1", "x2", "x3"))
        net.ident, net.ident16 = sb("ident", [P, P]), sb("ident16", [P, P], F16)
        net.ones_row, net.mask_row = sb("ones_row", [1, P], BF16), sb("mask_row", [1, TOK], BF16)
        net.half_neg = sb("half_neg", [P, TG])
        net.gates_raw, net.gates = sb("gates_raw", [P, 2]), sb("gates", [P, 2])
        net.wide = {n: sb(f"wide_{n}", [P, D]) for n in ("ln1_g", "ln1_b", "ln2_g", "ln2_b", "ln3_g", "ln3_b")}
        net.router_bias = sb("router_bias", [P, EXP])
        net.out_bias = {n: sb(f"bias_{n}", [P, 1]) for n in ("sa", "ca", "fc2")}
        net.fc1_bias = sb("fc1_bias", [P, FF // P])

        def const_loads(mask_u8):
            loads = [(mask_u8[:], a["mask"].rearrange("(o b) s -> o (b s)", o=1))]
            loads += [(t[:], a[n].rearrange("(o d) -> o d", o=1).to_broadcast([P, D])) for n, t in net.wide.items()]
            loads += [(net.router_bias[:], a["rb"].rearrange("(o d) -> o d", o=1).to_broadcast([P, EXP]))]
            loads += [(net.gates_raw[:, i:i + 1], a[n].rearrange("(o d) -> o d", o=1).to_broadcast([P, 1]))
                      for i, n in enumerate(("g_xattn", "g_ffn"))]
            loads += [(t[:], a[{"sa": "sa_bo", "ca": "ca_bo", "fc2": "fc2_b"}[n]].rearrange("(d o) -> d o", o=1))
                      for n, t in net.out_bias.items()]
            fc1_b = a["fc1_b"].rearrange("(c p o) -> c p o", p=P, o=1)
            loads += [(net.fc1_bias[:, c:c + 1], fc1_b[c]) for c in range(FF // P)]
            return loads

        net.const_loads = const_loads
        net.n_const = 13 + FF // P
        with ExitStack() as ctx_a:
            sba = lambda name: ctx_a.enter_context(nc.sbuf_tensor(name, [P, H, P], F32R))
            net.M = {p: (sba(f"M_hi_{p}"), sba(f"M_lo_{p}")) for p in ("sa", "ca")}
            net.N = {p: (sba(f"N_hi_{p}"), sba(f"N_lo_{p}")) for p in ("sa", "ca")}
            prepare(nc, net, a)
            if stages >= 1:
                attention(nc, net, "sa", net.xn, net.xn, net.wide["ln1_g"], net.wide["ln1_b"], net.x1 if stages > 1 else out)
            if stages >= 2:
                attention(nc, net, "ca", net.x1, a["ctx"], net.wide["ln2_g"], net.wide["ln2_b"], net.x2 if stages > 2 else out)
        net.experts_hi, net.experts_lo = sb("experts_hi", [P, EW, P], F32R), sb("experts_lo", [P, EW, P], F32R)
        net.router_hi, net.router_lo = sb("router_hi", [P, EXP], F32R), sb("router_lo", [P, EXP], F32R)
        if stages >= 3:
            feed(nc, net, a, net.x2, net.x3 if stages > 3 else out)
        if stages >= 4:
            experts(nc, net, a, net.x3, out)


_NAMES = {"x": "x", "ctx": "ctx_1024", "mask": "mask_BxS2_bk0", "g_xattn": "g_xattn", "g_ffn": "g_ffn"}
_NAMES |= {n: f"L0_xattn_{n}" for n in (
    "sa_wq", "sa_wk", "sa_wv", "sa_wo", "sa_bo", "ca_wq", "ca_wk", "ca_wv", "ca_wo", "ca_bo", "ln1_g", "ln1_b",
    "ln2_g", "ln2_b", "ln3_g", "ln3_b", "fc1_w", "fc1_b", "fc2_w", "fc2_b")}
_NAMES |= {n: f"L0_ffn_{n}" for n in ("Wg_s", "Wu_s", "Wd_s", "Wg", "Wu", "Wd", "Wr", "rb")}


def kernel(**inputs):
    import numpy as np
    import concourse.bacc as bacc
    from concourse.bass_utils import run_bass_kernel_spmd

    nc = bacc.Bacc("TRN2", target_bir_lowering=False, num_devices=1)
    arrays, a = {}, {}
    for short, name in _NAMES.items():
        v = np.ascontiguousarray(inputs[name])
        if short in ("x", "ctx"):
            v = v.reshape(TOK, D)
        arrays[f"in_{short}"] = v
        dt = U8 if v.dtype == np.bool_ else mybir.dt.from_np(v.dtype)
        a[short] = nc.dram_tensor(f"in_{short}", v.shape, dt, kind="ExternalInput").ap()
    out = nc.dram_tensor("out", (TOK, D), F32, kind="ExternalOutput").ap()
    program(nc, a, out)
    r = run_bass_kernel_spmd(nc, [arrays], core_ids=[0])
    return r.results[0]["out"].reshape(B, S, D)
```

```python
from contextlib import ExitStack

import concourse.bass as bass
from concourse import mybir

ALU = mybir.AluOpType
ACT = mybir.ActivationFunctionType
AX = mybir.AxisListType
F32, F32R, F16, BF16, U8 = (mybir.dt.float32, mybir.dt.float32r, mybir.dt.float16, mybir.dt.bfloat16,
                            mybir.dt.uint8)

P = 128
B, S, D = 64, 64, 128
H, DH = 16, 64
HP = H // 2
TOK = B * S
GT = 512
NG = TOK // GT
TG = GT // P
FF, EXP, I = 512, 8, 256
EW = 3 * 2 * (EXP + 1)
AT_TURN_Y, AT_TURN_X, AT_TURN_CW = 2, 3, 7
EPS = 1e-5
SCALE = DH ** -0.5
MASKED = -float(2 ** 100)


class Loop:

    def __init__(self, reg, first, step, n):
        self.reg, self.first, self.step, self.n = reg, first, step, n

    def __add__(self, k):
        return Loop(self.reg, self.first + k, self.step, self.n)

    def __sub__(self, k):
        return self + (-k)


def sample(G):
    return G if isinstance(G, int) else G.first


class Count:

    def __init__(self, groups, order, each=1):
        self.n, total = {}, 0
        for g in groups:
            for ev in order(g):
                total += each
                self.n[(ev, g)] = total
        self.total = total

    def after(self, ev, G):
        if isinstance(G, int):
            return self.n[(ev, G)]
        v = [self.n[(ev, G.first + G.step * i)] for i in range(G.n)]
        d = v[1] - v[0]
        assert all(v[i + 1] - v[i] == d for i in range(G.n - 1))
        return G.reg * d + v[0]


class Net:
    pass


def mm3(nc, out, w_hi, w_lo, x_hi, x_lo, start=True, stop=True):
    nc.tensor.matmul(out, w_hi, x_hi, start=start, stop=False, skip_group_check=True)
    nc.tensor.matmul(out, w_hi, x_lo, start=False, stop=False, skip_group_check=True)
    return nc.tensor.matmul(out, w_lo, x_hi, start=False, stop=stop, skip_group_check=True)


def f32(ap):
    return ap.bitcast(F32)


def row_moments(nc, dve, rows, stats, parts, mean, var, step_done, at):
    d, total, squares = parts[:, 0], parts[:, 1], parts[:, 2]
    for t in range(TG):
        ins = nc.vector.bn_stats(stats[:, t, :], rows(t))
    ins.then_inc(step_done, 1)
    dve.wait_ge(step_done, at(1))
    nc.vector.tensor_tensor(d, stats[:, :, 1], stats[:, :, 4], ALU.subtract)
    nc.vector.tensor_tensor(total, stats[:, :, 1], stats[:, :, 4], ALU.add)
    nc.vector.tensor_tensor(squares, stats[:, :, 2], stats[:, :, 5], ALU.add).then_inc(step_done, 1)
    dve.wait_ge(step_done, at(2))
    nc.vector.scalar_tensor_tensor(out=parts[:, 3], in0=d, scalar=0.25, in1=d, op0=ALU.mult, op1=ALU.mult)
    nc.vector.tensor_scalar(mean, total, 0.5, None, ALU.mult)
    nc.vector.tensor_scalar(parts[:, 4], squares, 1.0 / D, EPS, ALU.mult, ALU.add).then_inc(step_done, 1)
    dve.wait_ge(step_done, at(3))
    return nc.vector.tensor_tensor(var, parts[:, 3], parts[:, 4], ALU.add)


def prepare(nc, net, a):
    with ExitStack() as ctx:
        sb = lambda name, shape, dt=F32: ctx.enter_context(nc.sbuf_tensor(name, shape, dt))
        sem = lambda name: ctx.enter_context(nc.semaphore(name))
        raw = {(p, w): sb(f"raw_{p}_{w}", [P, 8, P]) for p in ("sa", "ca") for w in ("wq", "wk", "wv", "wo")}
        turned = {(p, w): sb(f"turned_{p}_{w}", [P, 8, P]) for p in ("sa", "ca") for w in ("wq", "wk", "wv")}
        mask_u8 = sb("mask_u8", [1, TOK], U8)
        x_in = sb("x_in", [P, NG, TG, P])
        stats = sb("p_stats", [P, TG, 6])
        parts, mean = sb("p_parts", [P, 5, TG]), sb("p_mean", [P, TG])
        var = sb("p_var", [P, TG])
        rstd = sb("p_rstd", [P, TG])
        ps = ctx.enter_context(nc.psum_tensor("p_ps", [P, 8, 512], F32))
        const_in, x_loaded, xn_stored = sem("const_in"), sem("x_loaded"), sem("xn_stored")
        w_in = {p: sem(f"w_in_{p}") for p in ("sa", "ca")}
        zeroed, ready, mask_ready, tanh_done = sem("zeroed"), sem("ready"), sem("mask_ready"), sem("tanh_done")
        pe_done, act_done, dve_done = sem("p_pe_done"), sem("p_act_done"), sem("p_dve_done")
        step_done, var_done, rstd_done, norm_done = sem("step_done"), sem("var_done"), sem("rstd_done"), sem("norm_done")

        jobs = []
        for p in ("sa", "ca"):
            jobs += [("turn", p, w, half) for w in ("wq", "wk", "wv") for half in range(2)]
            jobs += [(what, p, half, par) for what in "MN" for half in range(2) for par in range(2)]
        lo_after = {}
        for j, job in enumerate(jobs):
            if job[0] != "turn":
                lo_after[j] = len(lo_after) + 1
        x_view = a["x"].rearrange("(g t p) d -> p g t d", p=P, t=TG)
        xn_view = net.xn.rearrange("(g t p) d -> g p t d", p=P, t=TG)

        block = ctx.enter_context(nc.Block())

        @block.sync
        def _(sp):
            for p in ("sa", "ca"):
                for w in ("wq", "wk", "wv"):
                    sp.dma_start(raw[p, w][:], a[f"{p}_{w}"].rearrange("d (c n) -> d c n", n=P)).then_inc(w_in[p], 16)
                sp.dma_start(raw[p, "wo"][:], a[f"{p}_wo"].rearrange("(c p) n -> p c n", p=P)).then_inc(w_in[p], 16)
            sp.wait_ge(xn_stored, 16 * NG)

        @block.tensor
        def _(pe):
            pe.wait_ge(ready, 2)
            for j, (what, p, x, y) in enumerate(jobs):
                if j % (len(jobs) // 2) == 0:
                    pe.wait_ge(w_in[p], 16 * 4)
                if j >= 8:
                    pe.wait_ge(act_done, j - 7)
                    if j - 8 in lo_after:
                        pe.wait_ge(dve_done, lo_after[j - 8])
                if what != "turn" and x == 0 and y == 0:
                    base = 0 if p == "sa" else len(jobs) // 2
                    pe.wait_ge(act_done, base + (4 if what == "M" else 6))
                for c in range(4):
                    out = ps[:, j % 8, c * P:(c + 1) * P]
                    if what == "turn":
                        ins = nc.tensor.transpose(out, raw[p, x][:, 4 * y + c, :], net.ident[:])
                    else:
                        rows = slice(64 * y, 64 * y + 64)
                        left, right = ("wq", turned[p, "wk"]) if what == "M" else ("wv", raw[p, "wo"])
                        ins = nc.tensor.matmul(out, turned[p, left][rows, 4 * x + c, :],
                                               right[rows, 4 * x + c, :], start=True, stop=True)
                ins.then_inc(pe_done, 1)

        def composed(what, p, x, y):
            hi, lo = net.M[p] if what == "M" else net.N[p]
            heads = slice(8 * x + y, 8 * x + y + 7, 2)
            return hi[:, heads, :], lo[:, heads, :], SCALE if what == "M" else 1.0

        @block.scalar
        def _(act):
            act.dma_start(x_in[:], x_view).then_inc(x_loaded, 16)
            for j, (what, p, x, y) in enumerate(jobs):
                act.wait_ge(pe_done, j + 1)
                src = ps[:, j % 8, :].rearrange("p (c n) -> p c n", c=4)
                if what == "turn":
                    nc.scalar.activation(turned[p, x][:, 4 * y:4 * y + 4, :], src, ACT.Copy).then_inc(act_done, 1)
                else:
                    hi, lo, scale = composed(what, p, x, y)
                    nc.scalar.activation(hi, src, ACT.Copy, scale=scale).then_inc(act_done, 1)
            act.wait_ge(const_in, 16 * net.n_const)
            nc.scalar.activation(net.gates[:], net.gates_raw[:], ACT.Tanh).then_inc(tanh_done, 1)

        @block.vector
        def _(dve):
            dve.wait_ge(const_in, 16 * net.n_const)
            nc.vector.tensor_scalar(net.mask_row[:], mask_u8[:], MASKED, None, ALU.mult).then_inc(mask_ready, 1)
            for j, (what, p, x, y) in enumerate(jobs):
                if what != "turn":
                    dve.wait_ge(act_done, j + 1)
                    hi, lo, scale = composed(what, p, x, y)
                    src = ps[:, j % 8, :].rearrange("p (c n) -> p c n", c=4)
                    nc.vector.scalar_tensor_tensor(out=lo, in0=src, scalar=scale, in1=f32(hi), op0=ALU.mult,
                                                   op1=ALU.subtract).then_inc(dve_done, 1)
            nc.vector.memset(net.half_neg[:], -0.5)
            dve.wait_ge(x_loaded, 16)
            with dve.Fori(0, NG) as g:
                row_moments(nc, dve, lambda t: x_in[:, g, t, :], stats, parts, mean[:], var[:], step_done,
                            lambda n: g * 3 + n).then_inc(var_done, 1)
                dve.wait_ge(rstd_done, g + 1)
                for t in range(TG):
                    ins = nc.vector.tensor_scalar(x_in[:, g, t, :], x_in[:, g, t, :], mean[:, t:t + 1],
                                                  rstd[:, t:t + 1], ALU.subtract, ALU.mult)
                ins.then_inc(norm_done, 1)

        @block.gpsimd
        def _(pool):
            for dst, src in net.const_loads(mask_u8):
                pool.dma_start(dst, src).then_inc(const_in, 16)
            for n, ident in enumerate((net.ident, net.ident16)):
                nc.gpsimd.memset(ident[:], 0.0).then_inc(zeroed, 1)
                pool.wait_ge(zeroed, n + 1)
                nc.gpsimd.affine_select(out=ident[:], in_=ident[:], compare_op=ALU.not_equal, fill=1.0, base=0,
                                        pattern=[[-1, P]], channel_multiplier=1).then_inc(ready, 1)
            nc.gpsimd.memset(net.ones_row[:], 1.0).then_inc(zeroed, 1)
            with pool.Fori(0, NG) as g:
                pool.wait_ge(var_done, g + 1)
                nc.gpsimd.tensor_tensor(rstd[:], var[:], net.half_neg[:], ALU.pow).then_inc(rstd_done, 1)
                pool.wait_ge(norm_done, g + 1)
                pool.dma_start(xn_view[g], x_in[:, g]).then_inc(xn_stored, 16)


def attention(nc, net, p, x, ctx_dram, gain, bias, out):
    K = TG
    with ExitStack() as ctx:
        sb = lambda name, shape, dt=F32: ctx.enter_context(nc.sbuf_tensor(f"{p}_{name}", shape, dt))
        sem = lambda name: ctx.enter_context(nc.semaphore(f"{p}_{name}"))
        x_nat, c_nat, res = sb("x_nat", [P, TG, P]), sb("c_nat", [P, TG, P]), sb("res", [P, TG, P])
        xT_hi, xT_lo = sb("xT_hi", [P, GT], F32R), sb("xT_lo", [P, GT], F32R)
        cT_hi, cT_lo = sb("cT_hi", [P, GT], F32R), sb("cT_lo", [P, GT], F32R)
        c16_hi, c16_lo = sb("c16_hi", [P, GT], F16), sb("c16_lo", [P, GT], F16)
        q_hi, q_lo = sb("q_hi", [P, 2, 8, H, S], F16), sb("q_lo", [P, 2, 8, H, S], F16)
        v_hi, v_lo = sb("v_hi", [P, 2, H, P], F16), sb("v_lo", [P, 2, H, P], F16)
        prob = sb("prob", [P, 2, HP, S])
        p_hi, p_lo = sb("p_hi", [P, 2, HP, 2, S], F16), sb("p_lo", [P, 2, HP, 2, S], F16)
        pT_hi, pT_lo = sb("pT_hi", [P, HP, P], F16), sb("pT_lo", [P, HP, P], F16)
        yT = sb("yT", [P, GT])
        z = sb("z", [P, TG, P])
        top, total, rtotal = sb("top", [P, 2, HP]), sb("total", [P, 2, HP]), sb("rtotal", [P, 2, HP])
        stats, parts = sb("stats", [P, TG, 6]), sb("parts", [P, 5, TG])
        mean, var, rstd = sb("mean", [P, TG]), sb("var", [P, TG]), sb("rstd", [P, TG])

        score_ps = ctx.enter_context(nc.psum_tensor(f"{p}_score_ps", [P, 2, HP, S], F32))
        turn_ps = ctx.enter_context(nc.psum_tensor(f"{p}_turn_ps", [P, HP, P], F16))
        y_ps = ctx.enter_context(nc.psum_tensor(f"{p}_y_ps", [P, 2, 512], F32))
        long_ps = ctx.enter_context(nc.psum_tensor(f"{p}_long_ps", [P, 3, 512], F32))

        def long_products(G):
            if G == -1:
                return [("x",), ("c",)] + [("q", k, j) for k in range(K) for j in range(4)]
            if G == NG:
                return [("tail",)]
            ev = []
            more = G < NG - 1
            for k in range(K):
                q, v = [("q", k, 0)] * more, [("v", k, 0)]
                ev += [("x",)] * (k == 0 and more) + (v + q if k == 0 else q + v) + [("v", k, 1)]
                ev += [("q", k, 1)] * more + [None] * (k == 2 and more)
                ev += [("v", k, 2), ("v", k, 3)]
                ev += [("tail",) if G > 0 else None] * (k == 1) + [("c",)] * (k == 3 and more)
                ev += [("q", k, 2), ("q", k, 3)] * more
            return ev

        ALL = range(-1, NG + 1)
        bank_of = {(ev, g): i % 3 for g in ALL for i, ev in enumerate(long_products(g)) if ev}

        def bank(ev, G):
            return bank_of[(ev, sample(G))]

        long_use = [Count(ALL, lambda g, b=b: [ev for ev in long_products(g) if ev and bank_of[(ev, g)] == b])
                    for b in range(3)]
        split = Count(ALL, lambda g: [ev for ev in long_products(g) if ev and ev != ("tail",)])
        slots = lambda g: range(K) if 0 <= g < NG else ()
        batch = Count(ALL, lambda g: [(k, b) for k in slots(g) for b in range(2)])
        behind = lambda g: [k for k in range(K) if 0 < K * g + k <= K * NG]
        turn = Count(ALL, lambda g: [(k, h) for k in behind(g) for h in range(2)])
        behind2 = lambda g: [k for k in range(K) if 1 < K * g + k <= K * NG + 1]
        pv = Count(ALL, lambda g: [(k, quarter) for k in behind2(g) for quarter in range(4)])
        copies = Count(ALL, behind2)
        tails = Count(ALL, lambda g: [()] * (g > 0))
        norm_steps = Count(ALL, lambda g: ["stats", "sums", "parts", "var", "norm"] * (g > 0))
        loads = Count(ALL, lambda g: [()] * (g < NG - 1), each=16)
        res_loads = Count(ALL, lambda g: [()] * (g > 0), each=16)
        stores = Count(list(ALL) + [NG + 1], lambda g: [()] * (g > 1), each=16)

        x_loaded, c_loaded, res_loaded, stored = sem("x_loaded"), sem("c_loaded"), sem("res_loaded"), sem("stored")
        long_full = [sem(f"long_full{b}") for b in range(3)]
        long_free = [sem(f"long_free{b}") for b in range(3)]
        hi_done = sem("hi_done")
        score_ready, shifted, exp_done = sem("score_ready"), sem("shifted"), sem("exp_done")
        top_done, sum_done, recip_done = sem("top_done"), sem("sum_done"), sem("recip_done")
        prob_done, phi_done, plo_done = sem("prob_done"), sem("phi_done"), sem("plo_done")
        turned, turn_copied = sem("turned"), sem("turn_copied")
        pv_done, y_copied = sem("pv_done"), sem("y_copied")
        step_done, rstd_done, scaled, gained = sem("step_done"), sem("rstd_done"), sem("scaled"), sem("gained")

        def long_done(eng, ev, G):
            eng.wait_ge(long_full[bank(ev, G)], long_use[bank(ev, G)].after(ev, G))

        def long_read(eng, ev, G):
            eng.wait_ge(long_free[bank(ev, G)], long_use[bank(ev, G)].after(ev, G))

        before = lambda k, G: (k - 1, G) if k else (K - 1, G - 1)
        number = lambda k, G: K * sample(G) + k
        x_view, c_view, out_view = (t.rearrange("(g t p) d -> g p t d", p=P, t=TG) for t in (x, ctx_dram, out))
        M_hi, M_lo = net.M[p]
        N_hi, N_lo = net.N[p]
        index = lambda G: G if isinstance(G, int) else G.reg * G.step + G.first

        def over_groups(eng, body, first=1, last=NG - 2):
            body(-1)
            body(0)
            with eng.Fori(0, (last - first + 1) // 2) as i:
                for par in range(2):
                    body(Loop(i, first + par, 2, (last - first + 1) // 2))
            body(NG - 1)
            body(NG)

        block = ctx.enter_context(nc.Block())

        @block.sync
        def _(sp):
            def group(G):
                g = sample(G)
                if g < NG - 1:
                    if g >= 0:
                        long_done(sp, ("x",), G - 1)
                    sp.dma_start(x_nat[:], x_view[index(G + 1)]).then_inc(x_loaded, 16)
                    if g >= 0:
                        long_done(sp, ("c",), G - 1)
                    sp.dma_start(c_nat[:], c_view[index(G + 1)]).then_inc(c_loaded, 16)
                if g > 1:
                    sp.wait_ge(gained, tails.after((), G - 1))
                    sp.dma_start(out_view[index(G - 2)], z[:]).then_inc(stored, 16)
                if g > 0:
                    if g > 1:
                        long_read(sp, ("tail",), G - 1)
                    sp.dma_start(res[:], x_view[index(G - 1)]).then_inc(res_loaded, 16)

            for g in (-1, 0, 1):
                group(g)
            with sp.Fori(0, NG - 3) as i:
                group(Loop(i, 2, 1, NG - 3))
            group(NG - 1)
            group(NG)
            sp.wait_ge(gained, tails.after((), NG))
            sp.dma_start(out_view[NG - 1], z[:]).then_inc(stored, 16)
            sp.wait_ge(stored, 16 * NG)

        @block.tensor
        def _(pe):
            def take(ev, G):
                b = bank(ev, G)
                n = long_use[b].after(ev, G)
                if sample(G) > -1 or n > 1:
                    pe.wait_ge(long_free[b], n - 1)
                return long_ps[:, b, :]

            def turn_tiles(ev, G, src):
                pe.wait_ge(x_loaded if ev == ("x",) else c_loaded, loads.after((), G))
                out = take(ev, G)
                for t in range(TG):
                    ins = nc.tensor.transpose(out[:, t * P:(t + 1) * P], src[:, t, :], net.ident[:])
                ins.then_inc(long_full[bank(ev, G)], 1)
                return ins

            def x_product(k, j, G):
                if sample(G) >= NG - 1:
                    return
                ev, h = ("q", k, j), 4 * k + j
                out = take(ev, G)
                if (k, j) == (0, 0):
                    long_read(pe, ("x",), G)
                mm3(nc, out, M_hi[:, h, :], M_lo[:, h, :], xT_hi[:], xT_lo[:]).then_inc(long_full[bank(ev, G)], 1)

            def ctx_product(k, j, G):
                ev, hs, toks = ("v", k, j), slice(4 * j, 4 * j + 4), slice(k * P, (k + 1) * P)
                out = take(ev, G)
                if (k, j) == (0, 0):
                    long_read(pe, ("c",), G - 1)
                mm3(nc, out, cT_hi[:, toks], cT_lo[:, toks], N_hi[:, hs, :], N_lo[:, hs, :])\
                    .then_inc(long_full[bank(ev, G)], 1)

            def scores(k, b, G, par):
                if (k, b) == (0, 0):
                    long_read(pe, ("q", K - 1, 3), G - 1)
                if number(k, G) > 0:
                    pe.wait_ge(shifted, batch.after((k, b), G) - 2)
                n = 2 * k + b
                keys = slice(n * S, (n + 1) * S)
                for c in range(HP):
                    mm3(nc, score_ps[:, b, c, :], q_hi[:, par, n, 2 * c:2 * c + 2, :], q_lo[:, par, n, 2 * c:2 * c + 2, :],
                        c16_hi[:, keys], c16_lo[:, keys], start=(c == 0), stop=False)
                at = index(G) * GT + n * S
                row = net.mask_row[0:1, bass.ds(at, S)].unsqueeze(1).to_broadcast([1, HP, S])
                nc.tensor.matmul(score_ps[:, b, :, :], net.ones_row[:], row, start=False, stop=True,
                                 skip_group_check=True).then_inc(score_ready, 1)

            def turn_probs(k, half, G):
                if number(k, G) == 0:
                    return
                kb, Gb = before(k, G)
                pe.wait_ge(plo_done if half else phi_done, batch.after((kb, 1), Gb))
                if number(k, G) > 1 or half:
                    pe.wait_ge(turn_copied, turn.after((k, half), G) - 1)
                src = (p_lo if half else p_hi)[:, kb % 2]
                for c in range(HP):
                    ins = nc.tensor.transpose(turn_ps[:, c, :], src[:, c, :, :], net.ident16[:])
                ins.then_inc(turned, 1)

            def prob_product(k, G, quarter):
                if k not in behind2(sample(G)):
                    return
                kb, Gb = before(k, G)
                if quarter == 0:
                    pe.wait_ge(turn_copied, turn.after((kb, 1), Gb))
                    if number(k, G) > 2:
                        pe.wait_ge(y_copied, copies.after(kb, Gb))
                kb, Gb = before(kb, Gb)
                if quarter == 0:
                    long_read(pe, ("v", kb, 3), Gb)
                for h in range(4 * quarter, 4 * quarter + 4):
                    for x_hi, w_hi, b in ((1, 1, 0), (1, 1, 1), (0, 1, 0), (0, 1, 1), (1, 0, 0), (1, 0, 1)):
                        rows = slice(64 * b, 64 * b + 64)
                        w = (v_hi if w_hi else v_lo)[rows, kb % 2, h, :]
                        x = (pT_hi if x_hi else pT_lo)[rows, h // 2, 64 * (h % 2):64 * (h % 2) + 64]
                        ins = nc.tensor.matmul(y_ps[:, b, 0:S], w, x, start=bool(h == 0 and x_hi and w_hi),
                                               stop=bool(h == H - 1 and not w_hi))
                ins.then_inc(pv_done, 1)

            def turn_y(G):
                out = take(("tail",), G)
                pe.wait_ge(y_copied, copies.after(1, G))
                for t in range(TG):
                    ins = nc.tensor.transpose(out[:, t * P:(t + 1) * P], yT[:, t * P:(t + 1) * P], net.ident[:])
                ins.then_inc(long_full[bank(("tail",), G)], 1)

            def group(G):
                g = sample(G)
                par = g % 2
                if g == -1:
                    turn_tiles(("x",), G, x_nat)
                    turn_tiles(("c",), G, c_nat)
                    for k in range(K):
                        for j in range(4):
                            x_product(k, j, G)
                    return
                if g == NG:
                    for k in range(2):
                        for quarter in range(4):
                            prob_product(k, G, quarter)
                        if k == 0:
                            turn_probs(0, 0, G)
                            turn_probs(0, 1, G)
                    turn_y(G)
                    return
                for k in range(K):
                    if k == 0 and g < NG - 1:
                        turn_tiles(("x",), G, x_nat)
                    if k == 0 and g < NG - 1:
                        prob_product(k, G, 0)
                        ctx_product(k, 0, G)
                        scores(k, 0, G, par)
                        x_product(k, 0, G)
                    else:
                        scores(k, 0, G, par)
                        x_product(k, 0, G)
                        prob_product(k, G, 0)
                        ctx_product(k, 0, G)
                    prob_product(k, G, 1)
                    ctx_product(k, 1, G)
                    prob_product(k, G, 2)
                    x_product(k, 1, G)
                    prob_product(k, G, 3)
                    scores(k, 1, G, par)
                    ctx_product(k, 2, G)
                    turn_probs(k, 0, G)
                    ctx_product(k, 3, G)
                    if k == 1 and g > 0:
                        turn_y(G)
                    if k == 3 and g < NG - 1:
                        turn_tiles(("c",), G, c_nat)
                    x_product(k, 2, G)
                    turn_probs(k, 1, G)
                    x_product(k, 3, G)

            over_groups(pe, group)

        def split_parts(ev, G):
            b, g = bank(ev, G), sample(G)
            src = long_ps[:, b, :]
            if ev[0] == "x":
                return src, [(xT_hi[:], xT_lo[:])]
            if ev[0] == "c":
                return src, [(cT_hi[:], cT_lo[:]), (c16_hi[:], c16_lo[:])]
            if ev[0] == "q":
                par, h = (g + 1) % 2, 4 * ev[1] + ev[2]
                return src.rearrange("p (n s) -> p n s", n=8), [(q_hi[:, par, :, h, :], q_lo[:, par, :, h, :])]
            hs = slice(4 * ev[2], 4 * ev[2] + 4)
            return (src.rearrange("p (h n) -> p h n", h=4),
                    [(v_hi[:, ev[1] % 2, hs, :], v_lo[:, ev[1] % 2, hs, :])])

        @block.scalar
        def _(act):
            def high(ev, G):
                long_done(act, ev, G)
                if ev[0] == "v" and number(ev[1], G) > 1:
                    act.wait_ge(pv_done, pv.after((ev[1], ev[2]), G))
                src, parts = split_parts(ev, G)
                for hi, _lo in parts:
                    ins = nc.scalar.activation(hi, src, ACT.Copy)
                ins.then_inc(hi_done, 1)

            def exponential(k, b, G):
                act.wait_ge(shifted, batch.after((k, b), G))
                nc.scalar.activation(prob[:, b], prob[:, b], ACT.Exp).then_inc(exp_done, 1)

            def prob_high(k, b, G):
                act.wait_ge(prob_done, batch.after((k, b), G))
                if number(k, G) > 1 and b == 0:
                    act.wait_ge(turned, turn.after((before(k, G)[0], 1), before(k, G)[1]))
                nc.scalar.activation(p_hi[:, k % 2, :, b, :], prob[:, b], ACT.Copy).then_inc(phi_done, 1)

            def copy_turned(k, half, G):
                act.wait_ge(turned, turn.after((k, half), G))
                if number(k, G) > 1:
                    act.wait_ge(pv_done, pv.after((k, 3), G))
                nc.scalar.activation((pT_lo if half else pT_hi)[:], turn_ps[:], ACT.Copy).then_inc(turn_copied, 1)

            def copy_y(k, G):
                if k not in behind2(sample(G)):
                    return
                act.wait_ge(pv_done, pv.after((k, 3), G))
                col = ((k - 2) % K) * P
                if k == 2 and sample(G) > 0:
                    long_done(act, ("tail",), G)
                nc.scalar.activation(yT[:, col:col + P].rearrange("p (b s) -> p b s", b=2), y_ps[:, :, 0:S],
                                     ACT.Identity, bias=net.out_bias[p][:, 0:1]).then_inc(y_copied, 1)

            def group(G):
                g = sample(G)
                if g == -1:
                    for ev in long_products(g):
                        high(ev, G)
                    return
                if g == NG:
                    prob_high(K - 1, 1, NG - 1)
                    copy_y(0, G)
                    copy_turned(0, 0, G)
                    copy_turned(0, 1, G)
                    copy_y(1, G)
                    return
                more = g < NG - 1
                for k in range(K):
                    if k == 0 and more:
                        high(("x",), G)
                    if k == 0 and more:
                        high(("v", k, 0), G)
                    if more:
                        high(("q", k, 0), G)
                    if number(k, G) > 0:
                        kb, Gb = before(k, G)
                        prob_high(kb, 1, Gb)
                    if k > 0 or not more:
                        high(("v", k, 0), G)
                    exponential(k, 0, G)
                    high(("v", k, 1), G)
                    if more:
                        high(("q", k, 1), G)
                    copy_y(k, G)
                    high(("v", k, 2), G)
                    if number(k, G) > 0:
                        copy_turned(k, 0, G)
                    high(("v", k, 3), G)
                    if k == 3 and more:
                        high(("c",), G)
                    exponential(k, 1, G)
                    if more:
                        high(("q", k, 2), G)
                    if number(k, G) > 0:
                        copy_turned(k, 1, G)
                    prob_high(k, 0, G)
                    if more:
                        high(("q", k, 3), G)

            over_groups(act, group)

        @block.vector
        def _(dve):
            def low(ev, G):
                b = bank(ev, G)
                dve.wait_ge(hi_done, split.after(ev, G))
                src, parts = split_parts(ev, G)
                for hi, lo in parts:
                    hi = f32(hi) if ev[0] in "xc" and hi is parts[0][0] else hi
                    ins = nc.vector.tensor_tensor(lo, src, hi, ALU.subtract)
                ins.then_inc(long_free[b], 1)

            def shift(k, b, G):
                n = batch.after((k, b), G)
                dve.wait_ge(score_ready, n)
                nc.vector.tensor_reduce(top[:, b, :], score_ps[:, b], AX.X, ALU.max).then_inc(top_done, 1)
                if number(k, G) > 0:
                    dve.wait_ge(plo_done, n - 2)
                dve.wait_ge(top_done, n)
                nc.vector.tensor_tensor(prob[:, b], score_ps[:, b], top[:, b, :].unsqueeze(2).to_broadcast([P, HP, S]),
                                        ALU.subtract).then_inc(shifted, 1)

            def totals(k, b, G):
                n = batch.after((k, b), G)
                dve.wait_ge(exp_done, n)
                nc.vector.tensor_reduce(total[:, b, :], prob[:, b], AX.X, ALU.add).then_inc(sum_done, 1)
                dve.wait_ge(sum_done, n)
                nc.vector.reciprocal(rtotal[:, b, :], total[:, b, :]).then_inc(recip_done, 1)

            def residual(G):
                b = bank(("tail",), G)
                dve.wait_ge(res_loaded, res_loads.after((), G))
                if sample(G) > 1:
                    dve.wait_ge(stored, stores.after((), G))
                long_done(dve, ("tail",), G)
                nc.vector.tensor_tensor(z[:], long_ps[:, b, :].rearrange("p (t n) -> p t n", t=TG), res[:],
                                        ALU.add).then_inc(long_free[b], 1)

            def moments(G):
                long_read(dve, ("tail",), G)
                row_moments(nc, dve, lambda t: z[:, t, :], stats, parts, mean[:], var[:], step_done,
                            lambda n: norm_steps.after(("stats", "sums", "parts")[n - 1], G)).then_inc(step_done, 1)

            def normed(G):
                dve.wait_ge(rstd_done, tails.after((), G))
                for t in range(TG):
                    ins = nc.vector.tensor_scalar(z[:, t, :], z[:, t, :], mean[:, t:t + 1], rstd[:, t:t + 1],
                                                  ALU.subtract, ALU.mult)
                ins.then_inc(step_done, 1)

            def group(G):
                g = sample(G)
                if g == -1:
                    for ev in long_products(g):
                        low(ev, G)
                    return
                if g == NG:
                    residual(G)
                    moments(G)
                    normed(G)
                    return
                more = g < NG - 1
                for k in range(K):
                    if k == 0 and more:
                        low(("x",), G)
                    if k == 0 and more:
                        low(("v", k, 0), G)
                    shift(k, 0, G)
                    if more:
                        low(("q", k, 0), G)
                    if k > 0 or not more:
                        low(("v", k, 0), G)
                    totals(k, 0, G)
                    low(("v", k, 1), G)
                    if k == 2 and g > 0:
                        moments(G)
                    if more:
                        low(("q", k, 1), G)
                    shift(k, 1, G)
                    low(("v", k, 2), G)
                    low(("v", k, 3), G)
                    if k == 1 and g > 0:
                        residual(G)
                    if k == 3 and more:
                        low(("c",), G)
                    totals(k, 1, G)
                    if more:
                        low(("q", k, 2), G)
                    if more:
                        low(("q", k, 3), G)
                    if k == 2 and g > 0:
                        normed(G)

            over_groups(dve, group)

        @block.gpsimd
        def _(pool):
            def probabilities(k, b, G):
                n = batch.after((k, b), G)
                pool.wait_ge(recip_done, n)
                nc.gpsimd.tensor_tensor(prob[:, b], prob[:, b], rtotal[:, b, :].unsqueeze(2).to_broadcast([P, HP, S]),
                                        ALU.mult).then_inc(prob_done, 1)

            def prob_low(k, b, G):
                pool.wait_ge(phi_done, batch.after((k, b), G))
                nc.gpsimd.tensor_tensor(p_lo[:, k % 2, :, b, :], prob[:, b], p_hi[:, k % 2, :, b, :],
                                        ALU.subtract).then_inc(plo_done, 1)

            def root(G):
                pool.wait_ge(step_done, norm_steps.after("var", G))
                nc.gpsimd.tensor_tensor(rstd[:], var[:], net.half_neg[:], ALU.pow).then_inc(rstd_done, 1)

            def gain_and_bias(G):
                pool.wait_ge(step_done, norm_steps.after("norm", G))
                wide = lambda t: t[:].unsqueeze(1).to_broadcast([P, TG, P])
                nc.gpsimd.tensor_tensor(z[:], z[:], wide(gain), ALU.mult).then_inc(scaled, 1)
                pool.wait_ge(scaled, tails.after((), G))
                nc.gpsimd.tensor_tensor(z[:], z[:], wide(bias), ALU.add).then_inc(gained, 1)

            def group(G):
                g = sample(G)
                if g == NG:
                    probabilities(K - 1, 1, NG - 1)
                    prob_low(K - 1, 1, NG - 1)
                    root(G)
                    gain_and_bias(G)
                if not 0 <= g < NG:
                    return
                for k in range(K):
                    if number(k, G) > 0:
                        kb, Gb = before(k, G)
                        probabilities(kb, 1, Gb)
                        prob_low(kb, 1, Gb)
                    probabilities(k, 0, G)
                    if k == 2 and g > 0:
                        root(G)
                    if k == 3 and g > 0:
                        gain_and_bias(G)
                    prob_low(k, 0, G)

            over_groups(pool, group)


def feed(nc, net, a, x, out):
    NC = FF // P
    with ExitStack() as ctx:
        sb = lambda name, shape, dt=F32: ctx.enter_context(nc.sbuf_tensor(f"f_{name}", shape, dt))
        sem = lambda name: ctx.enter_context(nc.semaphore(f"f_{name}"))
        raw = sb("raw", [P, EW, P])
        raw_router = sb("raw_router", [EXP, P])
        raw_fc = sb("raw_fc", [P, 2, NC, P])
        fc_hi, fc_lo = sb("fc_hi", [P, 2, NC, P], F32R), sb("fc_lo", [P, 2, NC, P], F32R)
        x_nat, res = sb("x_nat", [P, TG, P]), sb("res", [P, TG, P])
        xT_hi, xT_lo = sb("xT_hi", [P, GT], F32R), sb("xT_lo", [P, GT], F32R)
        h = sb("h", [P, NC, GT])
        h_hi, h_lo = sb("h_hi", [P, NC, GT], F32R), sb("h_lo", [P, NC, GT], F32R)
        yT, z = sb("yT", [P, GT]), sb("z", [P, TG, P])
        ps = ctx.enter_context(nc.psum_tensor("f_ps", [P, 8, 512], F32))
        h_ps, xT_ps, y_ps, yt_ps = ps[:, 0:4], ps[:, 4], ps[:, 5], ps[:, 6]

        raw_in, router_in, fc_in = sem("raw_in"), sem("router_in"), sem("fc_in")
        w_turned, w_hi, w_lo = sem("w_turned"), sem("w_hi"), sem("w_lo")
        x_loaded, res_loaded, stored = sem("x_loaded"), sem("res_loaded"), sem("stored")
        x_turned, x_hi, x_lo = sem("x_turned"), sem("x_hi"), sem("x_lo")
        h_ready, h_act, hi_done, lo_done = sem("h_ready"), sem("h_act"), sem("hi_done"), sem("lo_done")
        y_ready, y_copied, y_turned, added = sem("y_ready"), sem("y_copied"), sem("y_turned"), sem("added")

        SLOTS = range(-1, NG + 1)
        once = lambda first, last: Count(SLOTS, lambda g: [()] * (first <= g <= last))
        turns, firsts_n, backs = once(-1, NG - 2), once(0, NG - 1), once(1, NG)
        seconds = once(1, NG)
        chunks = Count(SLOTS, lambda g: list(range(NC)) if 0 <= g < NG else [])
        jobs = [list(range(j, min(j + 4, EW))) for j in range(0, EW, 4)]
        n_jobs = len(jobs) + 1
        index = lambda G: G if isinstance(G, int) else G.reg * G.step + G.first
        x_view, out_view = (t.rearrange("(g t p) d -> g p t d", p=P, t=TG) for t in (x, out))

        def over_slots(eng, body):
            for g in (-1, 0, 1):
                body(g)
            with eng.Fori(0, NG - 3) as i:
                body(Loop(i, 2, 1, NG - 3))
            for g in (NG - 1, NG):
                body(g)

        block = ctx.enter_context(nc.Block())

        @block.sync
        def _(sp):
            sp.dma_start(x_nat[:], x_view[0]).then_inc(x_loaded, 16)
            sp.dma_start(raw_fc[:, 0], a["fc1_w"].rearrange("d (c n) -> d c n", n=P)).then_inc(fc_in, 16)
            sp.dma_start(raw_fc[:, 1], a["fc2_w"].rearrange("(c p) n -> p c n", p=P)).then_inc(fc_in, 16)
            halves = lambda t: t.rearrange("(h p) d -> p h d", p=P)
            experts_of = lambda t: t.rearrange("e (h p) d -> p (e h) d", p=P)
            for m, (shared, routed) in enumerate((("Wg_s", "Wg"), ("Wu_s", "Wu"))):
                sp.dma_start(raw[:, 18 * m:18 * m + 2], halves(a[shared])).then_inc(raw_in, 16)
                sp.dma_start(raw[:, 18 * m + 2:18 * m + 18], experts_of(a[routed])).then_inc(raw_in, 16)
            sp.dma_start(raw[:, 36:38], a["Wd_s"].rearrange("d (h i) -> d h i", i=P)).then_inc(raw_in, 16)
            for e in range(EXP):
                sp.dma_start(raw[:, 38 + 2 * e:40 + 2 * e], a["Wd"][e].rearrange("d (h i) -> d h i", i=P)).then_inc(raw_in, 16)
            sp.dma_start(raw_router[:], a["Wr"]).then_inc(router_in, 16)

            def slot(G):
                g = sample(G)
                if 0 <= g < NG - 1:
                    sp.wait_ge(x_turned, turns.after((), G - 1))
                    sp.dma_start(x_nat[:], x_view[index(G + 1)]).then_inc(x_loaded, 16)
                if g >= 1:
                    if g > 1:
                        sp.wait_ge(added, backs.after((), G - 1))
                        sp.dma_start(out_view[index(G - 2)], z[:]).then_inc(stored, 16)
                    sp.dma_start(res[:], x_view[index(G - 1)]).then_inc(res_loaded, 16)

            for g in (0, 1):
                slot(g)
            with sp.Fori(0, NG - 3) as i:
                slot(Loop(i, 2, 1, NG - 3))
            for g in (NG - 1, NG):
                slot(g)
            sp.wait_ge(added, backs.after((), NG))
            sp.dma_start(out_view[NG - 1], z[:]).then_inc(stored, 16)
            sp.wait_ge(stored, 16 * NG)

        @block.tensor
        def _(pe):
            pe.wait_ge(router_in, 16)
            nc.tensor.transpose(ps[:, 7, 0:EXP], raw_router[:], net.ident[0:EXP, 0:EXP]).then_inc(w_turned, 1)
            pe.wait_ge(raw_in, 16 * (5 + EXP))
            for j, tiles in enumerate(jobs):
                if j >= 8:
                    pe.wait_ge(w_lo, j - 6)
                if j == 7:
                    pe.wait_ge(w_lo, 1)
                for c, t in enumerate(tiles):
                    ins = nc.tensor.transpose(ps[:, j % 8, c * P:(c + 1) * P], raw[:, t, :], net.ident[:])
                ins.then_inc(w_turned, 1)
            pe.wait_ge(w_lo, n_jobs + 2)

            def slot(G):
                g = sample(G)
                if 1 <= g <= NG:
                    if g > 1:
                        pe.wait_ge(y_copied, seconds.after((), G) - 1)
                    for c in range(NC):
                        pe.wait_ge(lo_done, chunks.after(c, G - 1))
                        ins = mm3(nc, y_ps, fc_hi[:, 1, c, :], fc_lo[:, 1, c, :], h_hi[:, c, :], h_lo[:, c, :],
                                  start=(c == 0), stop=(c == NC - 1))
                    ins.then_inc(y_ready, 1)
                if 0 <= g < NG:
                    pe.wait_ge(x_lo, turns.after((), G - 1))
                    for c in range(NC):
                        if g > 0:
                            pe.wait_ge(h_act, chunks.after(c, G - 1))
                        mm3(nc, h_ps[:, c], fc_hi[:, 0, c, :], fc_lo[:, 0, c, :], xT_hi[:], xT_lo[:])\
                            .then_inc(h_ready, 1)
                if g < NG - 1:
                    pe.wait_ge(x_loaded, index(G) * 16 + 32)
                    for t in range(TG):
                        ins = nc.tensor.transpose(xT_ps[:, t * P:(t + 1) * P], x_nat[:, t, :], net.ident[:])
                    ins.then_inc(x_turned, 1)
                if g >= 1:
                    pe.wait_ge(y_copied, seconds.after((), G))
                    if g > 1:
                        pe.wait_ge(added, backs.after((), G) - 1)
                    for t in range(TG):
                        ins = nc.tensor.transpose(yt_ps[:, t * P:(t + 1) * P], yT[:, t * P:(t + 1) * P], net.ident[:])
                    ins.then_inc(y_turned, 1)

            over_slots(pe, slot)

        @block.scalar
        def _(act):
            act.wait_ge(w_turned, 1)
            nc.scalar.activation(net.router_hi[:], ps[:, 7, 0:EXP], ACT.Copy).then_inc(w_hi, 1)
            for j, tiles in enumerate(jobs):
                act.wait_ge(w_turned, j + 2)
                n = len(tiles)
                nc.scalar.activation(net.experts_hi[:, tiles[0]:tiles[0] + n, :],
                                     ps[:, j % 8, 0:n * P].rearrange("p (t n) -> p t n", n=P), ACT.Copy).then_inc(w_hi, 1)
            act.wait_ge(fc_in, 32)
            for m in range(2):
                nc.scalar.activation(fc_hi[:, m], raw_fc[:, m], ACT.Copy).then_inc(w_hi, 1)

            def slot(G):
                g = sample(G)
                if 1 <= g <= NG:
                    act.wait_ge(y_ready, seconds.after((), G))
                    if g > 1:
                        act.wait_ge(y_turned, backs.after((), G - 1))
                    nc.scalar.activation(yT[:], y_ps, ACT.Identity, bias=net.out_bias["fc2"][:, 0:1])\
                        .then_inc(y_copied, 1)
                if 0 <= g < NG:
                    for c in range(NC):
                        act.wait_ge(h_ready, chunks.after(c, G))
                        if g > 0:
                            act.wait_ge(lo_done, chunks.after(c, G - 1))
                        nc.scalar.activation(h[:, c, :], h_ps[:, c], ACT.Gelu, bias=net.fc1_bias[:, c:c + 1])\
                            .then_inc(h_act, 1)
                        if c > 0:
                            high(c - 1, G)
                    high(NC - 1, G)
                if g < NG - 1:
                    act.wait_ge(x_turned, turns.after((), G))
                    nc.scalar.activation(xT_hi[:], xT_ps, ACT.Copy).then_inc(x_hi, 1)

            def high(c, G):
                act.wait_ge(h_act, chunks.after(c, G))
                nc.scalar.activation(h_hi[:, c, :], h[:, c, :], ACT.Copy).then_inc(hi_done, 1)

            over_slots(act, slot)

        @block.vector
        def _(dve):
            dve.wait_ge(w_hi, 1)
            nc.vector.tensor_tensor(net.router_lo[:], ps[:, 7, 0:EXP], f32(net.router_hi[:]), ALU.subtract).then_inc(w_lo, 1)
            for j, tiles in enumerate(jobs):
                dve.wait_ge(w_hi, j + 2)
                n = len(tiles)
                part = slice(tiles[0], tiles[0] + n)
                nc.vector.tensor_tensor(net.experts_lo[:, part, :], ps[:, j % 8, 0:n * P].rearrange("p (t n) -> p t n", n=P),
                                        f32(net.experts_hi[:, part, :]), ALU.subtract).then_inc(w_lo, 1)
            dve.wait_ge(fc_in, 32)
            for m in range(2):
                dve.wait_ge(w_hi, n_jobs + 1 + m)
                nc.vector.tensor_tensor(fc_lo[:, m], raw_fc[:, m], f32(fc_hi[:, m]), ALU.subtract).then_inc(w_lo, 1)

            def slot(G):
                g = sample(G)
                if 0 <= g < NG:
                    for c in range(NC):
                        dve.wait_ge(hi_done, chunks.after(c, G))
                        nc.vector.tensor_tensor(h_lo[:, c, :], h[:, c, :], f32(h_hi[:, c, :]), ALU.subtract)\
                            .then_inc(lo_done, 1)
                if g < NG - 1:
                    dve.wait_ge(x_hi, turns.after((), G))
                    nc.vector.tensor_tensor(xT_lo[:], xT_ps, f32(xT_hi[:]), ALU.subtract).then_inc(x_lo, 1)
                if g >= 1:
                    dve.wait_ge(y_turned, backs.after((), G))
                    dve.wait_ge(res_loaded, index(G) * 16)
                    if g > 1:
                        dve.wait_ge(stored, index(G) * 16 - 16)
                    nc.vector.tensor_tensor(z[:], yt_ps.rearrange("p (t n) -> p t n", t=TG), res[:], ALU.add)\
                        .then_inc(added, 1)

            over_slots(dve, slot)


def experts(nc, net, a, x3, out):
    NE = EXP + 1
    with ExitStack() as ctx:
        sb = lambda name, shape, dt=F32: ctx.enter_context(nc.sbuf_tensor(f"m_{name}", shape, dt))
        sem = lambda name: ctx.enter_context(nc.semaphore(f"m_{name}"))
        x_in, z, r, m = sb("x_in", [P, TG, P]), sb("z", [P, TG, P]), sb("r", [P, TG, P]), sb("m", [P, TG, P])
        r_kept = sb("r_kept", [P, 2, TG, P])
        xT_hi, xT_lo = sb("xT_hi", [P, 2, GT], F32R), sb("xT_lo", [P, 2, GT], F32R)
        cw_wide = sb("cw_wide", [P, 2, EXP, GT])
        act_g = sb("act_g", [P, 3, GT])
        h = sb("h", [P, 3, 2, GT])
        h_hi, h_lo = sb("h_hi", [P, 3, 2, GT], F32R), sb("h_lo", [P, 3, 2, GT], F32R)
        yT, o = sb("yT", [P, GT]), sb("o", [P, TG, P])
        gate_gain, gate_bias = sb("gate_gain", [P, P]), sb("gate_bias", [P, P])
        stats, parts = sb("stats", [P, TG, 6]), sb("parts", [P, 5, TG])
        mean, var, rstd = sb("mean", [P, TG]), sb("var", [P, TG]), sb("rstd", [P, TG])
        logit, e_neg, prob = sb("logit", [P, TG, EXP]), sb("e_neg", [P, TG, EXP]), sb("prob", [P, TG, EXP])
        e_base = sb("e_base", [P, TG, EXP])
        above, equal = sb("above", [P, TG, EXP, EXP]), sb("equal", [P, TG, EXP, EXP])
        earlier, later = sb("earlier", [P, EXP, EXP]), sb("later", [P, EXP, EXP])
        rank, cw, cwT = sb("rank", [P, TG, EXP]), sb("cw", [P, TG, EXP]), sb("cwT", [EXP, GT])
        cw_dram = nc.dram_tensor("cw_dram", (NG, EXP, GT), F32, kind="Internal").ap()
        psum = lambda name, n: ctx.enter_context(nc.psum_tensor(f"m_{name}_ps", [P, n, 512], F32))
        gate_ps, up_ps, y_ps, turn_ps = psum("gate", 3), psum("up", 3), psum("y", 1), psum("turn", 1)

        SLOTS = range(-1, NG + 1)
        expert = Count(SLOTS, lambda g: list(range(NE)) if 0 <= g < NG else [])
        half = Count(SLOTS, lambda g: [(j, n) for j in range(NE) for n in range(2)] if 0 <= g < NG else [])
        routed = Count(SLOTS, lambda g: [(j, n) for j in range(1, NE) for n in range(2)] if 0 <= g < NG else [])
        pre = Count(SLOTS, lambda g: [()] * (g < NG - 1))
        post = Count(SLOTS, lambda g: [()] * (g > 0))
        turns = Count(SLOTS, lambda g: ["y"] * (g > 0) + ["x", "cw"] * (g < NG - 1))
        NORM3 = ["3 stats", "3 sums", "3 parts", "3 var", "3 gain"]
        NORM_M = ["r", "m stats", "m sums", "m parts", "m var", "m norm"]
        ROUTE = ["logit", "one more", "prob", "compare", "masked", "sum", "rank", "cw"]
        steps = Count(SLOTS, lambda g: (NORM3 + NORM_M + ROUTE) * (g < NG - 1))
        roots = Count(SLOTS, lambda g: ["3", "m"] * (g < NG - 1))

        x3_loaded, x_loaded, cw_saved, stored = sem("x3_loaded"), sem("x_loaded"), sem("cw_saved"), sem("stored")
        cw_loaded = [sem(f"cw_loaded{n}") for n in range(2)]
        gate_ready, up_ready, y_ready = sem("gate_ready"), sem("up_ready"), sem("y_ready")
        silu_done, weighted, h_done, hi_done, lo_done = sem("silu_done"), sem("weighted"), sem("h_done"), sem("hi_done"), sem("lo_done")
        step, root_done, biased, r_saved = sem("step"), sem("root_done"), sem("biased"), sem("r_saved")
        turned, x_hi, x_lo, cw_copied = sem("turned"), sem("x_hi"), sem("x_lo"), sem("cw_copied")
        logits_ready, e_done, y_copied, o_done = sem("logits_ready"), sem("e_done"), sem("y_copied"), sem("o_done")
        consts, gated_consts = sem("consts"), sem("gated_consts")

        index = lambda G: G if isinstance(G, int) else G.reg * G.step + G.first
        x_view, x3_view, out_view = (t.rearrange("(g t p) d -> g p t d", p=P, t=TG) for t in (a["x"], x3, out))
        weights = lambda matrix, j, n: (net.experts_hi[:, 18 * matrix + 2 * j + n, :], net.experts_lo[:, 18 * matrix + 2 * j + n, :])
        ring = lambda j, n: (2 * j + n) % 3

        def lag(j, G, n):
            return (j - n, G) if j >= n else (j - n + NE, G - 1)

        def three_halves_ago(j, n, G):
            jb, Gb = lag(j, G, 2 - n)
            return (jb, 1 - n), Gb

        def over_slots(eng, body, rounds=NG // 2 - 1):
            body(-1)
            body(0)
            with eng.Fori(0, rounds) as i:
                for par in range(2):
                    body(Loop(i, 1 + par, 2, rounds))
            for g in range(1 + 2 * rounds, NG + 1):
                body(g)

        block = ctx.enter_context(nc.Block())

        @block.sync
        def _(sp):
            def load(G):
                sp.dma_start(z[:], x3_view[index(G)]).then_inc(x3_loaded, 16)
                sp.dma_start(x_in[:], x_view[index(G)]).then_inc(x_loaded, 16)

            def slot(G):
                g = sample(G)
                if g == -1:
                    load(0)
                if g < NG - 2:
                    sp.wait_ge(step, steps.after("r", G))
                    load(G + 2)
                if g > 0:
                    sp.wait_ge(o_done, post.after((), G))
                    sp.dma_start(out_view[index(G - 1)], o[:]).then_inc(stored, 16)
                if g < NG - 1:
                    sp.wait_ge(cw_copied, pre.after((), G))
                    sp.dma_start(cw_dram[index(G + 1)], cwT[:]).then_inc(cw_saved, 16)
                    if g > 0:
                        sp.wait_ge(weighted, routed.after((NE - 1, 1), G - 1))
                    sp.wait_ge(cw_saved, index(G) * 16 + 32)
                    for n in range(2):
                        src = cw_dram[index(G + 1), 4 * n:4 * n + 4, :].rearrange("(o e) t -> o e t", o=1)
                        sp.dma_start(cw_wide[:, (g + 1) % 2, 4 * n:4 * n + 4, :], src.to_broadcast([P, 4, GT]))\
                            .then_inc(cw_loaded[n], 16)

            over_slots(sp, slot, NG // 2 - 2)
            sp.wait_ge(stored, 16 * NG)

        @block.tensor
        def _(pe):
            def gates_and_ups(j, G):
                par = sample(G) % 2
                if j == 0:
                    pe.wait_ge(x_lo, pre.after((), G - 1))
                for n in range(2):
                    if 2 * j + n >= 3 or sample(G) > 0:
                        pe.wait_ge(h_done, half.after(*three_halves_ago(j, n, G)))
                    for matrix, ps, ready in ((0, gate_ps, gate_ready), (1, up_ps, up_ready)):
                        mm3(nc, ps[:, ring(j, n), :], *weights(matrix, j, n), xT_hi[:, par, :], xT_lo[:, par, :]).then_inc(ready, 1)

            def down(j, G):
                if j == 0 and sample(G) > 0:
                    pe.wait_ge(y_copied, post.after((), G))
                for n in range(2):
                    pe.wait_ge(lo_done, half.after((j, n), G))
                    ins = mm3(nc, y_ps[:, 0, :], *weights(2, j, n), h_hi[:, j % 3, n, :], h_lo[:, j % 3, n, :],
                              start=(j == 0 and n == 0), stop=(j == NE - 1 and n == 1))
                ins.then_inc(y_ready, 1)

            def turn_y(G):
                pe.wait_ge(y_copied, post.after((), G))
                if sample(G) < NG:
                    pe.wait_ge(cw_copied, pre.after((), G - 1))
                else:
                    pe.wait_ge(o_done, post.after((), G - 1))
                for t in range(TG):
                    ins = nc.tensor.transpose(turn_ps[:, 0, t * P:(t + 1) * P], yT[:, t * P:(t + 1) * P], net.ident[:])
                ins.then_inc(turned, 1)

            def turn_x(G):
                pe.wait_ge(step, steps.after("m norm", G))
                if sample(G) > 0:
                    pe.wait_ge(o_done, post.after((), G))
                elif sample(G) == 0:
                    pe.wait_ge(cw_copied, pre.after((), G - 1))
                for t in range(TG):
                    ins = nc.tensor.transpose(turn_ps[:, 0, t * P:(t + 1) * P], m[:, t, :], net.ident[:])
                ins.then_inc(turned, 1)

            def logits(G):
                par = (sample(G) + 1) % 2
                pe.wait_ge(x_lo, pre.after((), G))
                for t in range(TG):
                    toks = slice(t * P, (t + 1) * P)
                    ins = mm3(nc, turn_ps[:, 0, t * EXP:(t + 1) * EXP], xT_hi[:, par, toks], xT_lo[:, par, toks],
                              net.router_hi[:], net.router_lo[:])
                ins.then_inc(logits_ready, 1)

            def turn_cw(G):
                pe.wait_ge(step, steps.after("cw", G))
                for t in range(TG):
                    ins = nc.tensor.transpose(turn_ps[0:EXP, 0, t * P:(t + 1) * P], cw[:, t, :], net.ident[:])
                ins.then_inc(turned, 1)

            def slot(G):
                g = sample(G)
                for j in range(NE):
                    if 0 <= g < NG:
                        gates_and_ups(j, G)
                    if (0 <= g < NG and (g > 0 or j >= 2)) or (g == NG and j < 2):
                        down(*lag(j, G, 2))
                    if j == AT_TURN_Y and g > 0:
                        turn_y(G)
                    if g < NG - 1:
                        if j == AT_TURN_X:
                            turn_x(G)
                        if j == AT_TURN_X + 1:
                            logits(G)
                        if j == AT_TURN_CW:
                            turn_cw(G)

            over_slots(pe, slot)

        @block.scalar
        def _(act):
            def silu(j, n, G):
                act.wait_ge(gate_ready, half.after((j, n), G))
                nc.scalar.activation(act_g[:, ring(j, n), :], gate_ps[:, ring(j, n), :], ACT.Silu).then_inc(silu_done, 1)

            def high(j, n, G):
                if j == 0:
                    act.wait_ge(h_done, half.after((j, n), G))
                else:
                    act.wait_ge(weighted, routed.after((j, n), G))
                if j >= 3 or sample(G) > 0:
                    jb, Gb = lag(j, G, 3)
                    act.wait_ge(y_ready, expert.after(jb, Gb))
                nc.scalar.activation(h_hi[:, j % 3, n, :], h[:, j % 3, n, :], ACT.Copy).then_inc(hi_done, 1)

            def copy_y(G):
                act.wait_ge(y_ready, expert.after(NE - 1, G - 1))
                if sample(G) > 1:
                    act.wait_ge(turned, turns.after("y", G - 1))
                nc.scalar.activation(yT[:], y_ps[:, 0, :], ACT.Copy).then_inc(y_copied, 1)

            def x_high(G):
                act.wait_ge(turned, turns.after("x", G))
                nc.scalar.activation(xT_hi[:, (sample(G) + 1) % 2, :], turn_ps[:, 0, :], ACT.Copy).then_inc(x_hi, 1)

            def keep_r(G):
                act.wait_ge(step, steps.after("r", G))
                if sample(G) > 0:
                    act.wait_ge(o_done, post.after((), G))
                nc.scalar.activation(r_kept[:, (sample(G) + 1) % 2], r[:], ACT.Copy).then_inc(r_saved, 1)

            def copy_cw(G):
                act.wait_ge(turned, turns.after("cw", G))
                if sample(G) >= 0:
                    act.wait_ge(cw_saved, index(G) * 16 + 16)
                nc.scalar.activation(cwT[:], turn_ps[0:EXP, 0, :], ACT.Copy).then_inc(cw_copied, 1)

            def slot(G):
                g = sample(G)
                for j in range(NE):
                    if j == 2 and g > 0:
                        copy_y(G)
                    if g < NG - 1:
                        if j == AT_TURN_X + 1:
                            x_high(G)
                        if j == AT_TURN_CW + 1:
                            copy_cw(G)
                    for n in range(2):
                        if 0 <= g < NG:
                            silu(j, n, G)
                        if (0 <= g < NG and (g > 0 or j > 0)) or (g == NG and j == 0):
                            jb, Gb = lag(j, G, 1)
                            high(jb, n, Gb)
                    if g < NG - 1 and j == AT_TURN_X + 1:
                        keep_r(G)

            over_slots(act, slot)

        @block.vector
        def _(dve):
            nc.vector.memset(e_base[:], 1 / 2.718281828459045)
            nc.vector.tensor_scalar(gate_bias[:], net.wide["ln3_b"][:], net.gates[:, 0:1], None, ALU.mult).then_inc(gated_consts, 1)
            nc.vector.tensor_scalar(gate_gain[:], net.wide["ln3_g"][:], net.gates[:, 0:1], None, ALU.mult).then_inc(gated_consts, 1)
            dve.wait_ge(gated_consts, 2)
            dve.wait_ge(consts, 4)

            def product(j, n, G):
                dve.wait_ge(up_ready, half.after((j, n), G))
                dve.wait_ge(silu_done, half.after((j, n), G))
                nc.vector.tensor_tensor(h[:, j % 3, n, :], up_ps[:, ring(j, n), :], act_g[:, ring(j, n), :], ALU.mult)\
                    .then_inc(h_done, 1)

            def low(j, n, G):
                dve.wait_ge(hi_done, half.after((j, n), G))
                nc.vector.tensor_tensor(h_lo[:, j % 3, n, :], h[:, j % 3, n, :], f32(h_hi[:, j % 3, n, :]),
                                        ALU.subtract).then_inc(lo_done, 1)

            def output(G):
                dve.wait_ge(turned, turns.after("y", G))
                if sample(G) > 1:
                    dve.wait_ge(stored, index(G) * 16 - 16)
                nc.vector.scalar_tensor_tensor(out=o[:], in0=turn_ps[:, 0, :].rearrange("p (t n) -> p t n", t=TG),
                                               scalar=net.gates[:, 1:2], in1=r_kept[:, (sample(G) - 1) % 2], op0=ALU.mult,
                                               op1=ALU.add).then_inc(o_done, 1)

            def moments(G, rows, names):
                row_moments(nc, dve, rows, stats, parts, mean[:], var[:], step,
                            lambda n: steps.after(names[n - 1], G)).then_inc(step, 1)

            def gain(G):
                for t in range(TG):
                    ins = nc.vector.scalar_tensor_tensor(out=z[:, t, :], in0=z[:, t, :], scalar=mean[:, t:t + 1], in1=gate_gain[:],
                                                         op0=ALU.subtract, op1=ALU.mult)
                ins.then_inc(step, 1)

            def gated(G):
                if sample(G) >= 0:
                    dve.wait_ge(r_saved, pre.after((), G - 1))
                dve.wait_ge(biased, pre.after((), G))
                dve.wait_ge(root_done, roots.after("3", G))
                dve.wait_ge(step, steps.after("3 gain", G))
                for t in range(TG):
                    ins = nc.vector.scalar_tensor_tensor(out=r[:, t, :], in0=z[:, t, :], scalar=rstd[:, t:t + 1], in1=x_in[:, t, :],
                                                         op0=ALU.mult, op1=ALU.add)
                ins.then_inc(step, 1)
                dve.wait_ge(step, steps.after("r", G))

            def normed(G):
                dve.wait_ge(root_done, roots.after("m", G))
                for t in range(TG):
                    ins = nc.vector.tensor_scalar(m[:, t, :], r[:, t, :], mean[:, t:t + 1], rstd[:, t:t + 1], ALU.subtract, ALU.mult)
                ins.then_inc(step, 1)

            def x_low(G):
                par = (sample(G) + 1) % 2
                dve.wait_ge(x_hi, pre.after((), G))
                nc.vector.tensor_tensor(xT_lo[:, par, :], turn_ps[:, 0, :], f32(xT_hi[:, par, :]), ALU.subtract).then_inc(x_lo, 1)

            def add_bias(G):
                dve.wait_ge(logits_ready, pre.after((), G))
                nc.vector.tensor_tensor(logit[:], turn_ps[:, 0, 0:TG * EXP].rearrange("p (t e) -> p t e", t=TG),
                                        net.router_bias[:].unsqueeze(1).to_broadcast([P, TG, EXP]), ALU.add).then_inc(step, 1)

            def route(G):
                def then(ins, name):
                    ins.then_inc(step, 1)
                    dve.wait_ge(step, steps.after(name, G))
                dve.wait_ge(e_done, pre.after((), G))
                then(nc.vector.tensor_scalar(logit[:], e_neg[:], 1.0, None, ALU.add), "one more")
                then(nc.vector.reciprocal(prob[:], logit[:]), "prob")
                other, own = prob[:].unsqueeze(2).to_broadcast([P, TG, EXP, EXP]), prob[:].unsqueeze(3).to_broadcast([P, TG, EXP, EXP])
                wide = lambda t: t[:].unsqueeze(1).to_broadcast([P, TG, EXP, EXP])
                nc.vector.tensor_tensor(equal[:], other, own, ALU.is_ge)
                then(nc.vector.tensor_tensor(above[:], other, own, ALU.is_gt), "compare")
                nc.vector.tensor_tensor(equal[:], equal[:], wide(earlier), ALU.mult)
                then(nc.vector.tensor_tensor(above[:], above[:], wide(later), ALU.mult), "masked")
                then(nc.vector.tensor_tensor(above[:], above[:], equal[:], ALU.add), "sum")
                then(nc.vector.tensor_reduce(rank[:], above[:], AX.X, ALU.add), "rank")
                nc.vector.scalar_tensor_tensor(out=cw[:], in0=rank[:], scalar=1.5, in1=prob[:], op0=ALU.is_lt,
                                               op1=ALU.mult).then_inc(step, 1)

            def slot(G):
                g = sample(G)
                for j in range(NE):
                    if j == AT_TURN_Y + 1 and g > 0:
                        output(G)
                    if g < NG - 1:
                        if j == AT_TURN_X + 1:
                            x_low(G)
                        if j == AT_TURN_X + 2:
                            add_bias(G)
                        if j == AT_TURN_CW:
                            route(G)
                    for n in range(2):
                        if 0 <= g < NG:
                            product(j, n, G)
                        if (0 <= g < NG and (g > 0 or j > 0)) or (g == NG and j == 0):
                            jb, Gb = lag(j, G, 1)
                            low(jb, n, Gb)
                    if g >= NG - 1:
                        continue
                    if j == 0:
                        dve.wait_ge(x3_loaded, index(G) * 16 + 32)
                        moments(G, lambda t: z[:, t, :], NORM3)
                        gain(G)
                    if j == 1:
                        gated(G)
                        moments(G, lambda t: r[:, t, :], NORM_M[1:])
                    if j == 2:
                        normed(G)

            over_slots(dve, slot)

        @block.gpsimd
        def _(pool):
            for n, (t, sign, keep) in enumerate(((earlier, 1, ALU.is_gt), (later, -1, ALU.is_ge))):
                nc.gpsimd.memset(t[:], 1.0).then_inc(consts, 1)
                pool.wait_ge(consts, 2 * n + 1)
                nc.gpsimd.affine_select(out=t[:], in_=t[:], compare_op=keep, fill=0.0, base=0,
                                        pattern=[[sign, EXP], [-sign, EXP]], channel_multiplier=0).then_inc(consts, 1)
            pool.wait_ge(gated_consts, 1)

            def weight(j, n, G):
                pool.wait_ge(h_done, half.after((j, n), G))
                if n == 0 and j in (1, 5):
                    pool.wait_ge(cw_loaded[j // 5], index(G) * 16 + 16)
                nc.gpsimd.tensor_tensor(h[:, j % 3, n, :], h[:, j % 3, n, :], cw_wide[:, sample(G) % 2, j - 1, :],
                                        ALU.mult).then_inc(weighted, 1)

            def root(G, name):
                pool.wait_ge(step, steps.after(name, G))
                nc.gpsimd.tensor_tensor(rstd[:], var[:], net.half_neg[:], ALU.pow).then_inc(root_done, 1)

            def add_gate_bias(G):
                pool.wait_ge(x_loaded, index(G) * 16 + 32)
                nc.gpsimd.tensor_tensor(x_in[:], x_in[:], gate_bias[:].unsqueeze(1).to_broadcast([P, TG, P]), ALU.add)\
                    .then_inc(biased, 1)

            def exponential(G, part):
                tiles = slice(2 * part, 2 * part + 2)
                if part == 0:
                    pool.wait_ge(step, steps.after("logit", G))
                ins = nc.gpsimd.tensor_tensor(e_neg[:, tiles], e_base[:, tiles], logit[:, tiles], ALU.pow)
                if part == 1:
                    ins.then_inc(e_done, 1)

            def slot(G):
                g = sample(G)
                for j in range(NE):
                    if g < NG - 1 and j == AT_TURN_X + 2:
                        exponential(G, 0)
                    if 0 <= g < NG and j > 0:
                        weight(j, 0, G)
                        weight(j, 1, G)
                    if g >= NG - 1:
                        continue
                    if j == 0:
                        add_gate_bias(G)
                        root(G, "3 var")
                    if j == 1:
                        root(G, "m var")
                    if j == AT_TURN_X + 2:
                        exponential(G, 1)

            over_slots(pool, slot)


def program(nc, a, out, stages=4):
    with ExitStack() as ctx:
        net = Net()
        dram = lambda name, shape: nc.dram_tensor(name, shape, F32, kind="Internal").ap()
        sb = lambda name, shape, dt=F32: ctx.enter_context(nc.sbuf_tensor(name, shape, dt))
        net.xn, net.x1, net.x2, net.x3 = (dram(n, (TOK, D)) for n in ("xn", "x1", "x2", "x3"))
        net.ident, net.ident16 = sb("ident", [P, P]), sb("ident16", [P, P], F16)
        net.ones_row, net.mask_row = sb("ones_row", [1, P], BF16), sb("mask_row", [1, TOK], BF16)
        net.half_neg = sb("half_neg", [P, TG])
        net.gates_raw, net.gates = sb("gates_raw", [P, 2]), sb("gates", [P, 2])
        net.wide = {n: sb(f"wide_{n}", [P, D]) for n in ("ln1_g", "ln1_b", "ln2_g", "ln2_b", "ln3_g", "ln3_b")}
        net.router_bias = sb("router_bias", [P, EXP])
        net.out_bias = {n: sb(f"bias_{n}", [P, 1]) for n in ("sa", "ca", "fc2")}
        net.fc1_bias = sb("fc1_bias", [P, FF // P])

        def const_loads(mask_u8):
            loads = [(mask_u8[:], a["mask"].rearrange("(o b) s -> o (b s)", o=1))]
            loads += [(t[:], a[n].rearrange("(o d) -> o d", o=1).to_broadcast([P, D])) for n, t in net.wide.items()]
            loads += [(net.router_bias[:], a["rb"].rearrange("(o d) -> o d", o=1).to_broadcast([P, EXP]))]
            loads += [(net.gates_raw[:, i:i + 1], a[n].rearrange("(o d) -> o d", o=1).to_broadcast([P, 1]))
                      for i, n in enumerate(("g_xattn", "g_ffn"))]
            loads += [(t[:], a[{"sa": "sa_bo", "ca": "ca_bo", "fc2": "fc2_b"}[n]].rearrange("(d o) -> d o", o=1))
                      for n, t in net.out_bias.items()]
            fc1_b = a["fc1_b"].rearrange("(c p o) -> c p o", p=P, o=1)
            loads += [(net.fc1_bias[:, c:c + 1], fc1_b[c]) for c in range(FF // P)]
            return loads

        net.const_loads = const_loads
        net.n_const = 13 + FF // P
        with ExitStack() as ctx_a:
            sba = lambda name: ctx_a.enter_context(nc.sbuf_tensor(name, [P, H, P], F32R))
            net.M = {p: (sba(f"M_hi_{p}"), sba(f"M_lo_{p}")) for p in ("sa", "ca")}
            net.N = {p: (sba(f"N_hi_{p}"), sba(f"N_lo_{p}")) for p in ("sa", "ca")}
            prepare(nc, net, a)
            if stages >= 1:
                attention(nc, net, "sa", net.xn, net.xn, net.wide["ln1_g"], net.wide["ln1_b"], net.x1 if stages > 1 else out)
            if stages >= 2:
                attention(nc, net, "ca", net.x1, a["ctx"], net.wide["ln2_g"], net.wide["ln2_b"], net.x2 if stages > 2 else out)
        net.experts_hi, net.experts_lo = sb("experts_hi", [P, EW, P], F32R), sb("experts_lo", [P, EW, P], F32R)
        net.router_hi, net.router_lo = sb("router_hi", [P, EXP], F32R), sb("router_lo", [P, EXP], F32R)
        if stages >= 3:
            feed(nc, net, a, net.x2, net.x3 if stages > 3 else out)
        if stages >= 4:
            experts(nc, net, a, net.x3, out)


_NAMES = {"x": "x", "ctx": "ctx_1024", "mask": "mask_BxS2_bk0", "g_xattn": "g_xattn", "g_ffn": "g_ffn"}
_NAMES |= {n: f"L0_xattn_{n}" for n in (
    "sa_wq", "sa_wk", "sa_wv", "sa_wo", "sa_bo", "ca_wq", "ca_wk", "ca_wv", "ca_wo", "ca_bo", "ln1_g", "ln1_b",
    "ln2_g", "ln2_b", "ln3_g", "ln3_b", "fc1_w", "fc1_b", "fc2_w", "fc2_b")}
_NAMES |= {n: f"L0_ffn_{n}" for n in ("Wg_s", "Wu_s", "Wd_s", "Wg", "Wu", "Wd", "Wr", "rb")}


def kernel(**inputs):
    import numpy as np
    import concourse.bacc as bacc
    from concourse.bass_utils import run_bass_kernel_spmd

    nc = bacc.Bacc("TRN2", target_bir_lowering=False, num_devices=1)
    arrays, a = {}, {}
    for short, name in _NAMES.items():
        v = np.ascontiguousarray(inputs[name])
        if short in ("x", "ctx"):
            v = v.reshape(TOK, D)
        arrays[f"in_{short}"] = v
        dt = U8 if v.dtype == np.bool_ else mybir.dt.from_np(v.dtype)
        a[short] = nc.dram_tensor(f"in_{short}", v.shape, dt, kind="ExternalInput").ap()
    out = nc.dram_tensor("out", (TOK, D), F32, kind="ExternalOutput").ap()
    program(nc, a, out)
    r = run_bass_kernel_spmd(nc, [arrays], core_ids=[0])
    return r.results[0]["out"].reshape(B, S, D)
```

```python
from contextlib import ExitStack

import concourse.bass as bass
from concourse import mybir

ALU = mybir.AluOpType
ACT = mybir.ActivationFunctionType
AX = mybir.AxisListType
F32, F32R, F16, BF16, U8 = (mybir.dt.float32, mybir.dt.float32r, mybir.dt.float16, mybir.dt.bfloat16,
                            mybir.dt.uint8)

P = 128
B, S, D = 64, 64, 128
H, DH = 16, 64
HP = H // 2
TOK = B * S
GT = 512
NG = TOK // GT
TG = GT // P
FF, EXP = 512, 8
NORM_TILES = 8
EW = 3 * 2 * (EXP + 1)
AT_TURN_Y, AT_TURN_X, AT_TURN_CW = 2, 3, 7
EPS = 1e-5
SCALE = DH ** -0.5
MASKED = -float(2 ** 100)


class Loop:

    def __init__(self, reg, first, step, n):
        self.reg, self.first, self.step, self.n = reg, first, step, n

    def __add__(self, k):
        return Loop(self.reg, self.first + k, self.step, self.n)

    def __sub__(self, k):
        return self + (-k)


def sample(G):
    return G if isinstance(G, int) else G.first


class Count:

    def __init__(self, groups, order, each=1):
        self.n, total = {}, 0
        for g in groups:
            for ev in order(g):
                total += each
                self.n[(ev, g)] = total
        self.total = total

    def after(self, ev, G):
        if isinstance(G, int):
            return self.n[(ev, G)]
        v = [self.n[(ev, G.first + G.step * i)] for i in range(G.n)]
        d = v[1] - v[0]
        assert all(v[i + 1] - v[i] == d for i in range(G.n - 1))
        return G.reg * d + v[0]


class Net:
    pass


def mm3(nc, out, w_hi, w_lo, x_hi, x_lo, start=True, stop=True):
    nc.tensor.matmul(out, w_hi, x_hi, start=start, stop=False, skip_group_check=True)
    nc.tensor.matmul(out, w_hi, x_lo, start=False, stop=False, skip_group_check=True)
    return nc.tensor.matmul(out, w_lo, x_hi, start=False, stop=stop, skip_group_check=True)


def f32(ap):
    return ap.bitcast(F32)


def row_moments(nc, dve, rows, stats, parts, mean, var, step_done, at, tiles=TG):
    d, total, squares = parts[:, 0], parts[:, 1], parts[:, 2]
    for t in range(tiles):
        ins = nc.vector.bn_stats(stats[:, t, :], rows(t))
    ins.then_inc(step_done, 1)
    dve.wait_ge(step_done, at(1))
    nc.vector.tensor_tensor(d, stats[:, :, 1], stats[:, :, 4], ALU.subtract)
    nc.vector.tensor_tensor(total, stats[:, :, 1], stats[:, :, 4], ALU.add)
    nc.vector.tensor_tensor(squares, stats[:, :, 2], stats[:, :, 5], ALU.add).then_inc(step_done, 1)
    dve.wait_ge(step_done, at(2))
    nc.vector.scalar_tensor_tensor(out=parts[:, 3], in0=d, scalar=0.25, in1=d, op0=ALU.mult, op1=ALU.mult)
    nc.vector.tensor_scalar(mean, total, 0.5, None, ALU.mult)
    nc.vector.tensor_scalar(parts[:, 4], squares, 1.0 / D, EPS, ALU.mult, ALU.add).then_inc(step_done, 1)
    dve.wait_ge(step_done, at(3))
    return nc.vector.tensor_tensor(var, parts[:, 3], parts[:, 4], ALU.add)


def prepare(nc, net, a):
    with ExitStack() as ctx:
        sb = lambda name, shape, dt=F32: ctx.enter_context(nc.sbuf_tensor(name, shape, dt))
        sem = lambda name: ctx.enter_context(nc.semaphore(name))
        raw = {(p, w): sb(f"raw_{p}_{w}", [P, 8, P]) for p in ("sa", "ca") for w in ("wq", "wk", "wv", "wo")}
        turned = {(p, w): sb(f"turned_{p}_{w}", [P, 8, P]) for p in ("sa", "ca") for w in ("wq", "wk", "wv")}
        mask_u8 = sb("mask_u8", [1, TOK], U8)
        NQ, NT = TOK // P // NORM_TILES, NORM_TILES
        x_in = sb("p_x_in", [P, NQ, NT, P])
        stats, parts = sb("p_stats", [P, NT, 6]), sb("p_parts", [P, 5, NT])
        mean, var, rstd = (sb(f"p_{n}", [P, NQ, NT]) for n in ("mean", "var", "rstd"))
        ps = ctx.enter_context(nc.psum_tensor("p_ps", [P, 8, 512], F32))
        const_in, xn_stored = sem("const_in"), sem("xn_stored")
        x_loaded = [sem(f"x_loaded{n}") for n in range(NQ)]
        w_in = {(p, w): sem(f"w_in_{p}_{w}") for p in ("sa", "ca") for w in ("wq", "wk", "wv", "wo")}
        zeroed, ready, mask_ready, tanh_done = sem("zeroed"), sem("ready"), sem("mask_ready"), sem("tanh_done")
        pe_done, act_done, dve_done = sem("p_pe_done"), sem("p_act_done"), sem("p_dve_done")
        step_done, var_done, rstd_done, norm_done = sem("step_done"), sem("var_done"), sem("rstd_done"), sem("norm_done")

        jobs = []
        for p in ("sa", "ca"):
            jobs += [("turn", p, w, half) for w in ("wq", "wk", "wv") for half in range(2)]
            jobs += [(what, p, half, par) for what in "MN" for half in range(2) for par in range(2)]
        lo_after = {}
        for j, job in enumerate(jobs):
            if job[0] != "turn":
                lo_after[j] = len(lo_after) + 1
        x_view, xn_view = (t.rearrange("(n t p) d -> n p t d", p=P, t=NT) for t in (a["x"], net.xn))

        block = ctx.enter_context(nc.Block())

        @block.sync
        def _(sp):
            def load_weights(p):
                for w in ("wq", "wk", "wv"):
                    sp.dma_start(raw[p, w][:], a[f"{p}_{w}"].rearrange("d (c n) -> d c n", n=P)).then_inc(w_in[p, w], 16)
                sp.dma_start(raw[p, "wo"][:], a[f"{p}_wo"].rearrange("(c p) n -> p c n", p=P)).then_inc(w_in[p, "wo"], 16)

            load_weights("sa")
            load_weights("ca")
            for dst, src in net.const_loads(mask_u8):
                sp.dma_start(dst, src).then_inc(const_in, 16)
            for n in range(NQ):
                sp.wait_ge(norm_done, n + 1)
                sp.dma_start(xn_view[n], x_in[:, n]).then_inc(xn_stored, 16)
            sp.wait_ge(xn_stored, 16 * NQ)

        @block.tensor
        def _(pe):
            pe.wait_ge(ready, 2)
            for j, (what, p, x, y) in enumerate(jobs):
                if what == "turn":
                    pe.wait_ge(w_in[p, x], 16)
                elif what == "N" and x == 0 and y == 0:
                    pe.wait_ge(w_in[p, "wo"], 16)
                if j >= 8:
                    pe.wait_ge(act_done, j - 7)
                    if j - 8 in lo_after:
                        pe.wait_ge(dve_done, lo_after[j - 8])
                if what != "turn" and x == 0 and y == 0:
                    base = 0 if p == "sa" else len(jobs) // 2
                    pe.wait_ge(act_done, base + (4 if what == "M" else 6))
                for c in range(4):
                    out = ps[:, j % 8, c * P:(c + 1) * P]
                    if what == "turn":
                        ins = nc.tensor.transpose(out, raw[p, x][:, 4 * y + c, :], net.ident[:])
                    else:
                        rows = slice(64 * y, 64 * y + 64)
                        left, right = ("wq", turned[p, "wk"]) if what == "M" else ("wv", raw[p, "wo"])
                        ins = nc.tensor.matmul(out, turned[p, left][rows, 4 * x + c, :],
                                               right[rows, 4 * x + c, :], start=True, stop=True)
                ins.then_inc(pe_done, 1)

        def composed(what, p, x, y):
            hi, lo = net.M[p] if what == "M" else net.N[p]
            heads = slice(8 * x + y, 8 * x + y + 7, 2)
            return hi[:, heads, :], lo[:, heads, :], SCALE if what == "M" else 1.0

        @block.scalar
        def _(act):
            for n in range(NQ):
                act.dma_start(x_in[:, n], x_view[n]).then_inc(x_loaded[n], 16)
            for j, (what, p, x, y) in enumerate(jobs):
                act.wait_ge(pe_done, j + 1)
                src = ps[:, j % 8, :].rearrange("p (c n) -> p c n", c=4)
                if what == "turn":
                    nc.scalar.activation(turned[p, x][:, 4 * y:4 * y + 4, :], src, ACT.Copy).then_inc(act_done, 1)
                else:
                    hi, lo, scale = composed(what, p, x, y)
                    nc.scalar.activation(hi, src, ACT.Copy, scale=scale).then_inc(act_done, 1)
            act.wait_ge(const_in, 16 * net.n_const)
            nc.scalar.activation(net.gates[:], net.gates_raw[:], ACT.Tanh).then_inc(tanh_done, 1)

        @block.vector
        def _(dve):
            nc.vector.memset(net.half_neg[:], -0.5)
            for n in range(NQ + 1):
                if n < NQ:
                    dve.wait_ge(x_loaded[n], 16)
                    row_moments(nc, dve, lambda t: x_in[:, n, t, :], stats, parts, mean[:, n], var[:, n], step_done,
                                lambda step: 3 * n + step, tiles=NT).then_inc(var_done, 1)
                if n > 0:
                    dve.wait_ge(rstd_done, n)
                    for t in range(NT):
                        rows = x_in[:, n - 1, t, :]
                        ins = nc.vector.tensor_scalar(rows, rows, mean[:, n - 1, t:t + 1], rstd[:, n - 1, t:t + 1],
                                                      ALU.subtract, ALU.mult)
                    ins.then_inc(norm_done, 1)
            for j, (what, p, x, y) in enumerate(jobs):
                if what != "turn":
                    dve.wait_ge(act_done, j + 1)
                    hi, lo, scale = composed(what, p, x, y)
                    src = ps[:, j % 8, :].rearrange("p (c n) -> p c n", c=4)
                    nc.vector.scalar_tensor_tensor(out=lo, in0=src, scalar=scale, in1=f32(hi), op0=ALU.mult,
                                                   op1=ALU.subtract).then_inc(dve_done, 1)
            dve.wait_ge(const_in, 16 * net.n_const)
            nc.vector.tensor_scalar(net.mask_row[:], mask_u8[:], MASKED, None, ALU.mult).then_inc(mask_ready, 1)

        @block.gpsimd
        def _(pool):
            for n, ident in enumerate((net.ident, net.ident16)):
                nc.gpsimd.memset(ident[:], 0.0).then_inc(zeroed, 1)
                pool.wait_ge(zeroed, n + 1)
                nc.gpsimd.affine_select(out=ident[:], in_=ident[:], compare_op=ALU.not_equal, fill=1.0, base=0,
                                        pattern=[[-1, P]], channel_multiplier=1).then_inc(ready, 1)
            nc.gpsimd.memset(net.ones_row[:], 1.0).then_inc(zeroed, 1)
            for n in range(NQ):
                pool.wait_ge(var_done, n + 1)
                nc.gpsimd.tensor_tensor(rstd[:, n], var[:, n], net.half_neg[:], ALU.pow).then_inc(rstd_done, 1)


class Layer:

    def __init__(self, name, x, ctx, out, gain, bias):
        self.name, self.gain, self.bias = name, gain, bias
        self.x, self.ctx, self.out = (t.rearrange("(g t p) d -> g p t d", p=P, t=TG) for t in (x, ctx, out))


def load_shared_expert(sp, net, a):
    sp.dma_start(net.raw_router[:], a["Wr"]).then_inc(net.router_in, 16)
    sp.dma_start(net.raw_fc[:, 0], a["fc1_w"].rearrange("d (c n) -> d c n", n=P)).then_inc(net.fc_in, 16)
    sp.dma_start(net.raw_fc[:, 1], a["fc2_w"].rearrange("(c p) n -> p c n", p=P)).then_inc(net.fc_in, 16)
    load_expert(sp, net, a["Wg_s"], a["Wu_s"], a["Wd_s"])


def load_expert(sp, net, wg, wu, wd):
    sp.dma_start(net.raw_expert[:, 0:2], wg.rearrange("(h p) d -> p h d", p=P)).then_inc(net.raw_in, 16)
    sp.dma_start(net.raw_expert[:, 2:4], wu.rearrange("(h p) d -> p h d", p=P)).then_inc(net.raw_in, 16)
    sp.dma_start(net.raw_expert[:, 4:6], wd.rearrange("d (h i) -> d h i", i=P)).then_inc(net.raw_in, 16)


def attentions(nc, net, layers, a):
    K = TG
    LAST = NG * len(layers)
    with ExitStack() as ctx:
        sb = lambda name, shape, dt=F32: ctx.enter_context(nc.sbuf_tensor(f"a_{name}", shape, dt))
        sem = lambda name: ctx.enter_context(nc.semaphore(f"a_{name}"))
        x_nat, c_nat, res = sb("x_nat", [P, TG, P]), sb("c_nat", [P, TG, P]), sb("res", [P, TG, P])
        xT_hi, xT_lo = sb("xT_hi", [P, GT], F32R), sb("xT_lo", [P, GT], F32R)
        cT_hi, cT_lo = sb("cT_hi", [P, GT], F32R), sb("cT_lo", [P, GT], F32R)
        c16_hi, c16_lo = sb("c16_hi", [P, GT], F16), sb("c16_lo", [P, GT], F16)
        q_hi, q_lo = sb("q_hi", [P, 2, 8, H, S], F16), sb("q_lo", [P, 2, 8, H, S], F16)
        v_hi, v_lo = sb("v_hi", [P, 2, H, P], F16), sb("v_lo", [P, 2, H, P], F16)
        prob = sb("prob", [P, 2, HP, S])
        p_hi, p_lo = sb("p_hi", [P, 2, HP, 2, S], F16), sb("p_lo", [P, 2, HP, 2, S], F16)
        pT_hi, pT_lo = sb("pT_hi", [P, HP, P], F16), sb("pT_lo", [P, HP, P], F16)
        yT = sb("yT", [P, GT])
        z = sb("z", [P, TG, P])
        top, total, rtotal = sb("top", [P, 2, HP]), sb("total", [P, 2, HP]), sb("rtotal", [P, 2, HP])
        stats, parts = sb("stats", [P, TG, 6]), sb("parts", [P, 5, TG])
        mean, var, rstd = sb("mean", [P, TG]), sb("var", [P, TG]), sb("rstd", [P, TG])

        score_ps = ctx.enter_context(nc.psum_tensor("a_score_ps", [P, 2, HP, S], F32))
        turn_ps = ctx.enter_context(nc.psum_tensor("a_turn_ps", [P, HP, P], F16))
        y_ps = ctx.enter_context(nc.psum_tensor("a_y_ps", [P, 2, 512], F32))
        long_ps = ctx.enter_context(nc.psum_tensor("a_long_ps", [P, 3, 512], F32))

        def long_products(G):
            if G == -1:
                return [("x",), ("c",)] + [("q", k, j) for k in range(K) for j in range(4)]
            if G == LAST:
                return [("tail",)]
            ev = []
            more = G < LAST - 1
            for k in range(K):
                q, v = [("q", k, 0)] * more, [("v", k, 0)]
                ev += [("x",)] * (k == 0 and more) + (v + q if k == 0 else q + v) + [("v", k, 1)]
                ev += [("q", k, 1)] * more + [None] * (k == 2 and more)
                ev += [("v", k, 2), ("v", k, 3)]
                ev += [("tail",) if G > 0 else None] * (k == 1) + [("c",)] * (k == 3 and more)
                ev += [("q", k, 2), ("q", k, 3)] * more
            return ev

        ALL = range(-1, LAST + 1)
        bank_of = {(ev, g): i % 3 for g in ALL for i, ev in enumerate(long_products(g)) if ev}

        def bank(ev, G):
            return bank_of[(ev, sample(G))]

        long_use = [Count(ALL, lambda g, b=b: [ev for ev in long_products(g) if ev and bank_of[(ev, g)] == b])
                    for b in range(3)]
        split = Count(ALL, lambda g: [ev for ev in long_products(g) if ev and ev != ("tail",)])
        slots = lambda g: range(K) if 0 <= g < LAST else ()
        batch = Count(ALL, lambda g: [(k, b) for k in slots(g) for b in range(2)])
        behind = lambda g: [k for k in range(K) if 0 < K * g + k <= K * LAST]
        turn = Count(ALL, lambda g: [(k, h) for k in behind(g) for h in range(2)])
        behind2 = lambda g: [k for k in range(K) if 1 < K * g + k <= K * LAST + 1]
        pv = Count(ALL, lambda g: [(k, quarter) for k in behind2(g) for quarter in range(4)])
        copies = Count(ALL, behind2)
        tails = Count(ALL, lambda g: [()] * (g > 0))
        norm_steps = Count(ALL, lambda g: ["stats", "sums", "parts", "var", "norm"] * (g > 0))
        loads = Count(ALL, lambda g: [()] * (g < LAST - 1), each=16)
        res_loads = Count(ALL, lambda g: [()] * (g > 0), each=16)
        stores = Count(list(ALL) + [LAST + 1], lambda g: [()] * (g > 1), each=16)

        x_loaded, c_loaded, res_loaded, stored = sem("x_loaded"), sem("c_loaded"), sem("res_loaded"), sem("stored")
        long_full = [sem(f"long_full{b}") for b in range(3)]
        long_free = [sem(f"long_free{b}") for b in range(3)]
        hi_done = sem("hi_done")
        score_ready, shifted, exp_done = sem("score_ready"), sem("shifted"), sem("exp_done")
        top_done, sum_done, recip_done = sem("top_done"), sem("sum_done"), sem("recip_done")
        prob_done, phi_done, plo_done = sem("prob_done"), sem("phi_done"), sem("plo_done")
        turned, turn_copied = sem("turned"), sem("turn_copied")
        pv_done, y_copied = sem("pv_done"), sem("y_copied")
        step_done, rstd_done, scaled, gained = sem("step_done"), sem("rstd_done"), sem("scaled"), sem("gained")

        def long_done(eng, ev, G):
            eng.wait_ge(long_full[bank(ev, G)], long_use[bank(ev, G)].after(ev, G))

        def long_read(eng, ev, G):
            eng.wait_ge(long_free[bank(ev, G)], long_use[bank(ev, G)].after(ev, G))

        before = lambda k, G: (k - 1, G) if k else (K - 1, G - 1)
        number = lambda k, G: K * sample(G) + k
        index = lambda G: G if isinstance(G, int) else G.reg * G.step + G.first
        layer = lambda G: layers[sample(G) // NG]
        within = lambda G: index(G - sample(G) // NG * NG)

        def over_groups(eng, body):
            body(-1)
            rounds = (NG - 2) // 2
            for first in range(0, LAST, NG):
                body(first)
                with eng.Fori(0, rounds) as i:
                    for par in range(2):
                        body(Loop(i, first + 1 + par, 2, rounds))
                body(first + NG - 1)
            body(LAST)

        block = ctx.enter_context(nc.Block())

        @block.sync
        def _(sp):
            def group(G):
                g = sample(G)
                if g < LAST - 1:
                    if g >= 0:
                        long_done(sp, ("x",), G - 1)
                    sp.dma_start(x_nat[:], layer(G + 1).x[within(G + 1)]).then_inc(x_loaded, 16)
                    if g >= 0:
                        long_done(sp, ("c",), G - 1)
                    sp.dma_start(c_nat[:], layer(G + 1).ctx[within(G + 1)]).then_inc(c_loaded, 16)
                if g > 1:
                    sp.wait_ge(gained, tails.after((), G - 1))
                    sp.dma_start(layer(G - 2).out[within(G - 2)], z[:]).then_inc(stored, 16)
                if g > 0:
                    if g > 1:
                        long_read(sp, ("tail",), G - 1)
                    sp.dma_start(res[:], layer(G - 1).x[within(G - 1)]).then_inc(res_loaded, 16)

            group(-1)
            load_shared_expert(sp, net, a)
            for first in range(0, LAST, NG):
                group(first)
                group(first + 1)
                with sp.Fori(0, NG - 3) as i:
                    group(Loop(i, first + 2, 1, NG - 3))
                group(first + NG - 1)
            group(LAST)
            sp.dma_start(net.feed_x[:], layers[-1].out[0]).then_inc(net.feed_x_in, 16)
            sp.wait_ge(gained, tails.after((), LAST))
            sp.dma_start(layers[-1].out[NG - 1], z[:]).then_inc(stored, 16)
            sp.wait_ge(stored, 16 * LAST)

        @block.tensor
        def _(pe):
            def take(ev, G):
                b = bank(ev, G)
                n = long_use[b].after(ev, G)
                if sample(G) > -1 or n > 1:
                    pe.wait_ge(long_free[b], n - 1)
                return long_ps[:, b, :]

            def turn_tiles(ev, G, src):
                pe.wait_ge(x_loaded if ev == ("x",) else c_loaded, loads.after((), G))
                out = take(ev, G)
                for t in range(TG):
                    ins = nc.tensor.transpose(out[:, t * P:(t + 1) * P], src[:, t, :], net.ident[:])
                ins.then_inc(long_full[bank(ev, G)], 1)
                return ins

            def x_product(k, j, G):
                if sample(G) >= LAST - 1:
                    return
                ev, h = ("q", k, j), 4 * k + j
                out = take(ev, G)
                if (k, j) == (0, 0):
                    long_read(pe, ("x",), G)
                M_hi, M_lo = net.M[layer(G + 1).name]
                mm3(nc, out, M_hi[:, h, :], M_lo[:, h, :], xT_hi[:], xT_lo[:]).then_inc(long_full[bank(ev, G)], 1)

            def ctx_product(k, j, G):
                ev, hs, toks = ("v", k, j), slice(4 * j, 4 * j + 4), slice(k * P, (k + 1) * P)
                out = take(ev, G)
                if (k, j) == (0, 0):
                    long_read(pe, ("c",), G - 1)
                N_hi, N_lo = net.N[layer(G).name]
                mm3(nc, out, cT_hi[:, toks], cT_lo[:, toks], N_hi[:, hs, :], N_lo[:, hs, :])\
                    .then_inc(long_full[bank(ev, G)], 1)

            def scores(k, b, G, par):
                if (k, b) == (0, 0):
                    long_read(pe, ("q", K - 1, 3), G - 1)
                if number(k, G) > 0:
                    pe.wait_ge(shifted, batch.after((k, b), G) - 2)
                n = 2 * k + b
                keys = slice(n * S, (n + 1) * S)
                for c in range(HP):
                    mm3(nc, score_ps[:, b, c, :], q_hi[:, par, n, 2 * c:2 * c + 2, :], q_lo[:, par, n, 2 * c:2 * c + 2, :],
                        c16_hi[:, keys], c16_lo[:, keys], start=(c == 0), stop=False)
                at = within(G) * GT + n * S
                row = net.mask_row[0:1, bass.ds(at, S)].unsqueeze(1).to_broadcast([1, HP, S])
                nc.tensor.matmul(score_ps[:, b, :, :], net.ones_row[:], row, start=False, stop=True,
                                 skip_group_check=True).then_inc(score_ready, 1)

            def turn_probs(k, half, G):
                if number(k, G) == 0:
                    return
                kb, Gb = before(k, G)
                pe.wait_ge(plo_done if half else phi_done, batch.after((kb, 1), Gb))
                if number(k, G) > 1 or half:
                    pe.wait_ge(turn_copied, turn.after((k, half), G) - 1)
                src = (p_lo if half else p_hi)[:, kb % 2]
                for c in range(HP):
                    ins = nc.tensor.transpose(turn_ps[:, c, :], src[:, c, :, :], net.ident16[:])
                ins.then_inc(turned, 1)

            def prob_product(k, G, quarter):
                if k not in behind2(sample(G)):
                    return
                kb, Gb = before(k, G)
                if quarter == 0:
                    pe.wait_ge(turn_copied, turn.after((kb, 1), Gb))
                    if number(k, G) > 2:
                        pe.wait_ge(y_copied, copies.after(kb, Gb))
                kb, Gb = before(kb, Gb)
                if quarter == 0:
                    long_read(pe, ("v", kb, 3), Gb)
                for h in range(4 * quarter, 4 * quarter + 4):
                    for x_hi, w_hi, b in ((1, 1, 0), (1, 1, 1), (0, 1, 0), (0, 1, 1), (1, 0, 0), (1, 0, 1)):
                        rows = slice(64 * b, 64 * b + 64)
                        w = (v_hi if w_hi else v_lo)[rows, kb % 2, h, :]
                        x = (pT_hi if x_hi else pT_lo)[rows, h // 2, 64 * (h % 2):64 * (h % 2) + 64]
                        ins = nc.tensor.matmul(y_ps[:, b, 0:S], w, x, start=bool(h == 0 and x_hi and w_hi),
                                               stop=bool(h == H - 1 and not w_hi))
                ins.then_inc(pv_done, 1)

            def turn_y(G):
                out = take(("tail",), G)
                pe.wait_ge(y_copied, copies.after(1, G))
                for t in range(TG):
                    ins = nc.tensor.transpose(out[:, t * P:(t + 1) * P], yT[:, t * P:(t + 1) * P], net.ident[:])
                ins.then_inc(long_full[bank(("tail",), G)], 1)

            def group(G):
                g = sample(G)
                par = g % 2
                if g == -1:
                    turn_tiles(("x",), G, x_nat)
                    turn_tiles(("c",), G, c_nat)
                    for k in range(K):
                        for j in range(4):
                            x_product(k, j, G)
                    return
                if g == LAST:
                    for k in range(2):
                        for quarter in range(4):
                            prob_product(k, G, quarter)
                        if k == 0:
                            turn_probs(0, 0, G)
                            turn_probs(0, 1, G)
                    turn_y(G)
                    return
                for k in range(K):
                    if k == 0 and g < LAST - 1:
                        turn_tiles(("x",), G, x_nat)
                    if k == 0:
                        prob_product(k, G, 0)
                        ctx_product(k, 0, G)
                        scores(k, 0, G, par)
                        x_product(k, 0, G)
                    else:
                        scores(k, 0, G, par)
                        x_product(k, 0, G)
                        prob_product(k, G, 0)
                        ctx_product(k, 0, G)
                    prob_product(k, G, 1)
                    ctx_product(k, 1, G)
                    prob_product(k, G, 2)
                    x_product(k, 1, G)
                    prob_product(k, G, 3)
                    scores(k, 1, G, par)
                    ctx_product(k, 2, G)
                    turn_probs(k, 0, G)
                    ctx_product(k, 3, G)
                    if k == 1 and g > 0:
                        turn_y(G)
                    if k == 3 and g < LAST - 1:
                        turn_tiles(("c",), G, c_nat)
                    x_product(k, 2, G)
                    turn_probs(k, 1, G)
                    x_product(k, 3, G)

            over_groups(pe, group)

        def split_parts(ev, G):
            b, g = bank(ev, G), sample(G)
            src = long_ps[:, b, :]
            if ev[0] == "x":
                return src, [(xT_hi[:], xT_lo[:])]
            if ev[0] == "c":
                return src, [(cT_hi[:], cT_lo[:]), (c16_hi[:], c16_lo[:])]
            if ev[0] == "q":
                par, h = (g + 1) % 2, 4 * ev[1] + ev[2]
                return src.rearrange("p (n s) -> p n s", n=8), [(q_hi[:, par, :, h, :], q_lo[:, par, :, h, :])]
            hs = slice(4 * ev[2], 4 * ev[2] + 4)
            return (src.rearrange("p (h n) -> p h n", h=4),
                    [(v_hi[:, ev[1] % 2, hs, :], v_lo[:, ev[1] % 2, hs, :])])

        @block.scalar
        def _(act):
            def high(ev, G):
                long_done(act, ev, G)
                if ev[0] == "v" and number(ev[1], G) > 1:
                    act.wait_ge(pv_done, pv.after((ev[1], ev[2]), G))
                src, parts = split_parts(ev, G)
                for hi, _lo in parts:
                    ins = nc.scalar.activation(hi, src, ACT.Copy)
                ins.then_inc(hi_done, 1)

            def exponential(k, b, G):
                act.wait_ge(shifted, batch.after((k, b), G))
                nc.scalar.activation(prob[:, b], prob[:, b], ACT.Exp).then_inc(exp_done, 1)

            def prob_high(k, b, G):
                act.wait_ge(prob_done, batch.after((k, b), G))
                if number(k, G) > 1 and b == 0:
                    act.wait_ge(turned, turn.after((before(k, G)[0], 1), before(k, G)[1]))
                nc.scalar.activation(p_hi[:, k % 2, :, b, :], prob[:, b], ACT.Copy).then_inc(phi_done, 1)

            def copy_turned(k, half, G):
                act.wait_ge(turned, turn.after((k, half), G))
                if number(k, G) > 1:
                    act.wait_ge(pv_done, pv.after((k, 3), G))
                nc.scalar.activation((pT_lo if half else pT_hi)[:], turn_ps[:], ACT.Copy).then_inc(turn_copied, 1)

            def copy_y(k, G):
                if k not in behind2(sample(G)):
                    return
                act.wait_ge(pv_done, pv.after((k, 3), G))
                col, name = ((k - 2) % K) * P, layer(G if k >= 2 else G - 1).name
                if k == 2 and sample(G) > 0:
                    long_done(act, ("tail",), G)
                nc.scalar.activation(yT[:, col:col + P].rearrange("p (b s) -> p b s", b=2), y_ps[:, :, 0:S],
                                     ACT.Identity, bias=net.out_bias[name][:, 0:1]).then_inc(y_copied, 1)

            def group(G):
                g = sample(G)
                if g == -1:
                    for ev in long_products(g):
                        high(ev, G)
                    return
                if g == LAST:
                    prob_high(K - 1, 1, LAST - 1)
                    copy_y(0, G)
                    copy_turned(0, 0, G)
                    copy_turned(0, 1, G)
                    copy_y(1, G)
                    return
                more = g < LAST - 1
                for k in range(K):
                    if k == 0 and more:
                        high(("x",), G)
                    if k == 0:
                        high(("v", k, 0), G)
                    if more:
                        high(("q", k, 0), G)
                    if number(k, G) > 0:
                        kb, Gb = before(k, G)
                        prob_high(kb, 1, Gb)
                    if k > 0:
                        high(("v", k, 0), G)
                    exponential(k, 0, G)
                    high(("v", k, 1), G)
                    if more:
                        high(("q", k, 1), G)
                    copy_y(k, G)
                    high(("v", k, 2), G)
                    if number(k, G) > 0:
                        copy_turned(k, 0, G)
                    high(("v", k, 3), G)
                    if k == 3 and more:
                        high(("c",), G)
                    exponential(k, 1, G)
                    if more:
                        high(("q", k, 2), G)
                    if number(k, G) > 0:
                        copy_turned(k, 1, G)
                    prob_high(k, 0, G)
                    if more:
                        high(("q", k, 3), G)

            over_groups(act, group)

        @block.vector
        def _(dve):
            def low(ev, G):
                b = bank(ev, G)
                dve.wait_ge(hi_done, split.after(ev, G))
                src, parts = split_parts(ev, G)
                for hi, lo in parts:
                    hi = f32(hi) if ev[0] in "xc" and hi is parts[0][0] else hi
                    ins = nc.vector.tensor_tensor(lo, src, hi, ALU.subtract)
                ins.then_inc(long_free[b], 1)

            def shift(k, b, G):
                n = batch.after((k, b), G)
                dve.wait_ge(score_ready, n)
                nc.vector.tensor_reduce(top[:, b, :], score_ps[:, b], AX.X, ALU.max).then_inc(top_done, 1)
                if number(k, G) > 0:
                    dve.wait_ge(plo_done, n - 2)
                dve.wait_ge(top_done, n)
                nc.vector.tensor_tensor(prob[:, b], score_ps[:, b], top[:, b, :].unsqueeze(2).to_broadcast([P, HP, S]),
                                        ALU.subtract).then_inc(shifted, 1)

            def totals(k, b, G):
                n = batch.after((k, b), G)
                dve.wait_ge(exp_done, n)
                nc.vector.tensor_reduce(total[:, b, :], prob[:, b], AX.X, ALU.add).then_inc(sum_done, 1)
                dve.wait_ge(sum_done, n)
                nc.vector.reciprocal(rtotal[:, b, :], total[:, b, :]).then_inc(recip_done, 1)

            def residual(G):
                b = bank(("tail",), G)
                dve.wait_ge(res_loaded, res_loads.after((), G))
                if sample(G) > 1:
                    dve.wait_ge(stored, stores.after((), G))
                long_done(dve, ("tail",), G)
                nc.vector.tensor_tensor(z[:], long_ps[:, b, :].rearrange("p (t n) -> p t n", t=TG), res[:],
                                        ALU.add).then_inc(long_free[b], 1)

            def moments(G):
                long_read(dve, ("tail",), G)
                row_moments(nc, dve, lambda t: z[:, t, :], stats, parts, mean[:], var[:], step_done,
                            lambda n: norm_steps.after(("stats", "sums", "parts")[n - 1], G)).then_inc(step_done, 1)

            def normed(G):
                dve.wait_ge(rstd_done, tails.after((), G))
                for t in range(TG):
                    ins = nc.vector.tensor_scalar(z[:, t, :], z[:, t, :], mean[:, t:t + 1], rstd[:, t:t + 1],
                                                  ALU.subtract, ALU.mult)
                ins.then_inc(step_done, 1)

            def group(G):
                g = sample(G)
                if g == -1:
                    for ev in long_products(g):
                        low(ev, G)
                    return
                if g == LAST:
                    residual(G)
                    moments(G)
                    normed(G)
                    return
                more = g < LAST - 1
                for k in range(K):
                    if k == 0 and more:
                        low(("x",), G)
                    if k == 0:
                        low(("v", k, 0), G)
                    shift(k, 0, G)
                    if more:
                        low(("q", k, 0), G)
                    if k > 0:
                        low(("v", k, 0), G)
                    totals(k, 0, G)
                    low(("v", k, 1), G)
                    if k == 2 and g > 0:
                        moments(G)
                    if more:
                        low(("q", k, 1), G)
                    shift(k, 1, G)
                    low(("v", k, 2), G)
                    low(("v", k, 3), G)
                    if k == 1 and g > 0:
                        residual(G)
                    if k == 3 and more:
                        low(("c",), G)
                    totals(k, 1, G)
                    if more:
                        low(("q", k, 2), G)
                    if more:
                        low(("q", k, 3), G)
                    if k == 2 and g > 0:
                        normed(G)

            over_groups(dve, group)

        @block.gpsimd
        def _(pool):
            def probabilities(k, b, G):
                n = batch.after((k, b), G)
                pool.wait_ge(recip_done, n)
                nc.gpsimd.tensor_tensor(prob[:, b], prob[:, b], rtotal[:, b, :].unsqueeze(2).to_broadcast([P, HP, S]),
                                        ALU.mult).then_inc(prob_done, 1)

            def prob_low(k, b, G):
                pool.wait_ge(phi_done, batch.after((k, b), G))
                nc.gpsimd.tensor_tensor(p_lo[:, k % 2, :, b, :], prob[:, b], p_hi[:, k % 2, :, b, :],
                                        ALU.subtract).then_inc(plo_done, 1)

            def root(G):
                pool.wait_ge(step_done, norm_steps.after("var", G))
                nc.gpsimd.tensor_tensor(rstd[:], var[:], net.half_neg[:, 0:TG], ALU.pow).then_inc(rstd_done, 1)

            def gain_and_bias(G):
                pool.wait_ge(step_done, norm_steps.after("norm", G))
                wide = lambda t: t[:].unsqueeze(1).to_broadcast([P, TG, P])
                nc.gpsimd.tensor_tensor(z[:], z[:], wide(layer(G - 1).gain), ALU.mult).then_inc(scaled, 1)
                pool.wait_ge(scaled, tails.after((), G))
                nc.gpsimd.tensor_tensor(z[:], z[:], wide(layer(G - 1).bias), ALU.add).then_inc(gained, 1)

            def group(G):
                g = sample(G)
                if g == LAST:
                    probabilities(K - 1, 1, LAST - 1)
                    prob_low(K - 1, 1, LAST - 1)
                    root(G)
                    gain_and_bias(G)
                if not 0 <= g < LAST:
                    return
                for k in range(K):
                    if number(k, G) > 0:
                        kb, Gb = before(k, G)
                        probabilities(kb, 1, Gb)
                        prob_low(kb, 1, Gb)
                    probabilities(k, 0, G)
                    if k == 2 and g > 0:
                        root(G)
                    if k == 3 and g > 0:
                        gain_and_bias(G)
                    prob_low(k, 0, G)

            over_groups(pool, group)


def feed(nc, net, a, x, out):
    NC = FF // P
    with ExitStack() as ctx:
        sb = lambda name, shape, dt=F32: ctx.enter_context(nc.sbuf_tensor(f"f_{name}", shape, dt))
        sem = lambda name: ctx.enter_context(nc.semaphore(f"f_{name}"))
        raw, raw_router, raw_fc, x_nat = net.raw_expert, net.raw_router, net.raw_fc, net.feed_x
        fc_hi, fc_lo = sb("fc_hi", [P, 2, NC, P], F32R), sb("fc_lo", [P, 2, NC, P], F32R)
        res = sb("res", [P, TG, P])
        xT_hi, xT_lo = sb("xT_hi", [P, GT], F32R), sb("xT_lo", [P, GT], F32R)
        h = sb("h", [P, NC, GT])
        h_hi, h_lo = sb("h_hi", [P, NC, GT], F32R), sb("h_lo", [P, NC, GT], F32R)
        yT, z = sb("yT", [P, GT]), sb("z", [P, TG, P])
        ps = ctx.enter_context(nc.psum_tensor("f_ps", [P, 8, 512], F32))
        h_ps, xT_ps, y_ps, yt_ps, w_ps = ps[:, 0:4], ps[:, 4], ps[:, 5], ps[:, 6], ps[:, 7]

        raw_in, router_in, fc_in = net.raw_in, net.router_in, net.fc_in
        w_turned, w_hi, w_lo = sem("w_turned"), sem("w_hi"), sem("w_lo")
        router_turned, router_split = sem("router_turned"), sem("router_split")
        fc_split, router_hi_done = sem("fc_split"), sem("router_hi_done")
        x_loaded, res_loaded, stored = net.feed_x_in, sem("res_loaded"), sem("stored")
        x_turned, x_hi, x_lo = sem("x_turned"), sem("x_hi"), sem("x_lo")
        h_ready, h_act, hi_done, lo_done = sem("h_ready"), sem("h_act"), sem("hi_done"), sem("lo_done")
        y_ready, y_copied, y_turned, added = sem("y_ready"), sem("y_copied"), sem("y_turned"), sem("added")

        SLOTS = range(-1, NG + 1)
        once = lambda first, last: Count(SLOTS, lambda g: [()] * (first <= g <= last))
        turns, firsts_n, backs = once(-1, NG - 2), once(0, NG - 1), once(1, NG)
        seconds = once(1, NG)
        chunks = Count(SLOTS, lambda g: list(range(NC)) if 0 <= g < NG else [])
        w_jobs = Count(SLOTS, lambda g: [0, 1] if g < NG else [])
        index = lambda G: G if isinstance(G, int) else G.reg * G.step + G.first
        x_view, out_view = (t.rearrange("(g t p) d -> g p t d", p=P, t=TG) for t in (x, out))

        def expert_tiles(t, job, G):
            if isinstance(G, int):
                return t[:, 6 * (G + 1) + 3 * job:6 * (G + 1) + 3 * job + 3, :]
            return t[:, bass.ds(index(G) * 6 + 6 + 3 * job, 3), :]

        def over_slots(eng, body):
            for g in (-1, 0, 1):
                body(g)
            with eng.Fori(0, NG - 3) as i:
                body(Loop(i, 2, 1, NG - 3))
            for g in (NG - 1, NG):
                body(g)

        block = ctx.enter_context(nc.Block())

        @block.sync
        def _(sp):
            def slot(G):
                g = sample(G)
                if 0 <= g < NG:
                    sp.wait_ge(w_turned, w_jobs.after(1, G - 1))
                    load_expert(sp, net, a["Wg"][index(G)], a["Wu"][index(G)], a["Wd"][index(G)])
                if 0 <= g < NG - 1:
                    sp.wait_ge(x_turned, turns.after((), G - 1))
                    sp.dma_start(x_nat[:], x_view[index(G + 1)]).then_inc(x_loaded, 16)
                if g >= 1:
                    if g > 1:
                        sp.wait_ge(added, backs.after((), G - 1))
                        sp.dma_start(out_view[index(G - 2)], z[:]).then_inc(stored, 16)
                    sp.dma_start(res[:], x_view[index(G - 1)]).then_inc(res_loaded, 16)

            for g in (0, 1):
                slot(g)
            with sp.Fori(0, NG - 3) as i:
                slot(Loop(i, 2, 1, NG - 3))
            for g in (NG - 1, NG):
                slot(g)
            sp.dma_start(net.z[:], out_view[0]).then_inc(net.z_in, 16)
            sp.dma_start(net.x_in[:], a["x"].rearrange("(g t p) d -> g p t d", p=P, t=TG)[0]).then_inc(net.x_loaded, 16)
            sp.wait_ge(added, backs.after((), NG))
            sp.dma_start(out_view[NG - 1], z[:]).then_inc(stored, 16)
            sp.wait_ge(stored, 16 * NG)

        @block.tensor
        def _(pe):
            pe.wait_ge(router_in, 16)
            nc.tensor.transpose(w_ps[:, 0:EXP], raw_router[:], net.ident[0:EXP, 0:EXP]).then_inc(router_turned, 1)

            def turn_weights(job, G):
                if job == 0:
                    pe.wait_ge(raw_in, index(G) * 48 + 96)
                if sample(G) > -1 or job > 0:
                    pe.wait_ge(w_lo, w_jobs.after(job, G) - 1)
                else:
                    pe.wait_ge(router_split, 1)
                for c in range(3):
                    ins = nc.tensor.transpose(w_ps[:, c * P:(c + 1) * P], raw[:, 3 * job + c, :], net.ident[:])
                ins.then_inc(w_turned, 1)

            def slot(G):
                g = sample(G)
                if 1 <= g <= NG:
                    if g > 1:
                        pe.wait_ge(y_copied, seconds.after((), G) - 1)
                    for c in range(NC):
                        pe.wait_ge(lo_done, chunks.after(c, G - 1))
                        ins = mm3(nc, y_ps, fc_hi[:, 1, c, :], fc_lo[:, 1, c, :], h_hi[:, c, :], h_lo[:, c, :],
                                  start=(c == 0), stop=(c == NC - 1))
                    ins.then_inc(y_ready, 1)
                if g < NG:
                    turn_weights(0, G)
                if 0 <= g < NG:
                    if g == 0:
                        pe.wait_ge(fc_split, 4)
                    pe.wait_ge(x_lo, turns.after((), G - 1))
                    for c in range(NC):
                        if g > 0:
                            pe.wait_ge(h_act, chunks.after(c, G - 1))
                        mm3(nc, h_ps[:, c], fc_hi[:, 0, c, :], fc_lo[:, 0, c, :], xT_hi[:], xT_lo[:])\
                            .then_inc(h_ready, 1)
                if g < NG:
                    turn_weights(1, G)
                if g < NG - 1:
                    pe.wait_ge(x_loaded, index(G) * 16 + 32)
                    for t in range(TG):
                        ins = nc.tensor.transpose(xT_ps[:, t * P:(t + 1) * P], x_nat[:, t, :], net.ident[:])
                    ins.then_inc(x_turned, 1)
                if g >= 1:
                    pe.wait_ge(y_copied, seconds.after((), G))
                    if g > 1:
                        pe.wait_ge(added, backs.after((), G) - 1)
                    for t in range(TG):
                        ins = nc.tensor.transpose(yt_ps[:, t * P:(t + 1) * P], yT[:, t * P:(t + 1) * P], net.ident[:])
                    ins.then_inc(y_turned, 1)

            over_slots(pe, slot)

        @block.scalar
        def _(act):
            act.wait_ge(router_turned, 1)
            nc.scalar.activation(net.router_hi[:], w_ps[:, 0:EXP], ACT.Copy).then_inc(router_hi_done, 1)
            act.wait_ge(fc_in, 32)
            for m in range(2):
                nc.scalar.activation(fc_hi[:, m], raw_fc[:, m], ACT.Copy).then_inc(fc_split, 1)

            def weights_high(job, G):
                act.wait_ge(w_turned, w_jobs.after(job, G))
                nc.scalar.activation(expert_tiles(net.experts_hi, job, G), w_ps[:, 0:3 * P].rearrange("p (t n) -> p t n", n=P),
                                     ACT.Copy).then_inc(w_hi, 1)

            def slot(G):
                g = sample(G)
                if 1 <= g <= NG:
                    act.wait_ge(y_ready, seconds.after((), G))
                    if g > 1:
                        act.wait_ge(y_turned, backs.after((), G - 1))
                    nc.scalar.activation(yT[:], y_ps, ACT.Identity, bias=net.out_bias["fc2"][:, 0:1])\
                        .then_inc(y_copied, 1)
                if g < NG:
                    weights_high(0, G)
                if 0 <= g < NG:
                    for c in range(NC):
                        act.wait_ge(h_ready, chunks.after(c, G))
                        if g > 0:
                            act.wait_ge(lo_done, chunks.after(c, G - 1))
                        nc.scalar.activation(h[:, c, :], h_ps[:, c], ACT.Gelu, bias=net.fc1_bias[:, c:c + 1])\
                            .then_inc(h_act, 1)
                if g < NG:
                    weights_high(1, G)
                if g < NG - 1:
                    act.wait_ge(x_turned, turns.after((), G))
                    nc.scalar.activation(xT_hi[:], xT_ps, ACT.Copy).then_inc(x_hi, 1)

            over_slots(act, slot)

        @block.vector
        def _(dve):
            dve.wait_ge(router_hi_done, 1)
            nc.vector.tensor_tensor(net.router_lo[:], w_ps[:, 0:EXP], f32(net.router_hi[:]), ALU.subtract).then_inc(router_split, 1)
            for m in range(2):
                dve.wait_ge(fc_split, 2)
                nc.vector.tensor_tensor(fc_lo[:, m], raw_fc[:, m], f32(fc_hi[:, m]), ALU.subtract).then_inc(fc_split, 1)

            def weights_low(job, G):
                dve.wait_ge(w_hi, w_jobs.after(job, G))
                nc.vector.tensor_tensor(expert_tiles(net.experts_lo, job, G), w_ps[:, 0:3 * P].rearrange("p (t n) -> p t n", n=P),
                                        f32(expert_tiles(net.experts_hi, job, G)), ALU.subtract).then_inc(w_lo, 1)

            def split_h(c, G):
                dve.wait_ge(h_act, chunks.after(c, G))
                nc.vector.tensor_copy(h_hi[:, c, :], h[:, c, :]).then_inc(hi_done, 1)
                dve.wait_ge(hi_done, chunks.after(c, G))
                nc.vector.tensor_tensor(h_lo[:, c, :], h[:, c, :], f32(h_hi[:, c, :]), ALU.subtract).then_inc(lo_done, 1)

            def slot(G):
                g = sample(G)
                if g < NG:
                    weights_low(0, G)
                if 0 <= g < NG:
                    for c in range(NC):
                        split_h(c, G)
                if g < NG:
                    weights_low(1, G)
                if g < NG - 1:
                    dve.wait_ge(x_hi, turns.after((), G))
                    nc.vector.tensor_tensor(xT_lo[:], xT_ps, f32(xT_hi[:]), ALU.subtract).then_inc(x_lo, 1)
                if g >= 1:
                    dve.wait_ge(y_turned, backs.after((), G))
                    dve.wait_ge(res_loaded, index(G) * 16)
                    if g > 1:
                        dve.wait_ge(stored, index(G) * 16 - 16)
                    nc.vector.tensor_tensor(z[:], yt_ps.rearrange("p (t n) -> p t n", t=TG), res[:], ALU.add)\
                        .then_inc(added, 1)

            over_slots(dve, slot)


def experts(nc, net, a, x3, out):
    NE = EXP + 1
    with ExitStack() as ctx:
        sb = lambda name, shape, dt=F32: ctx.enter_context(nc.sbuf_tensor(f"m_{name}", shape, dt))
        sem = lambda name: ctx.enter_context(nc.semaphore(f"m_{name}"))
        x_in, z, r, m = net.x_in, net.z, sb("r", [P, TG, P]), sb("m", [P, TG, P])
        r_kept = sb("r_kept", [P, 2, TG, P])
        xT_hi, xT_lo = sb("xT_hi", [P, 2, GT], F32R), sb("xT_lo", [P, 2, GT], F32R)
        cw_wide = sb("cw_wide", [P, 2, EXP, GT])
        act_g = sb("act_g", [P, 3, GT])
        h = sb("h", [P, 3, 2, GT])
        h_hi, h_lo = sb("h_hi", [P, 3, 2, GT], F32R), sb("h_lo", [P, 3, 2, GT], F32R)
        yT, o = sb("yT", [P, GT]), sb("o", [P, TG, P])
        gate_gain, gate_bias = sb("gate_gain", [P, P]), sb("gate_bias", [P, P])
        stats, parts = sb("stats", [P, TG, 6]), sb("parts", [P, 5, TG])
        mean, var, rstd = sb("mean", [P, TG]), sb("var", [P, TG]), sb("rstd", [P, TG])
        logit, e_neg, prob = sb("logit", [P, TG, EXP]), sb("e_neg", [P, TG, EXP]), sb("prob", [P, TG, EXP])
        e_base = sb("e_base", [P, TG, EXP])
        above, equal = sb("above", [P, TG, EXP, EXP]), sb("equal", [P, TG, EXP, EXP])
        earlier, later = sb("earlier", [P, EXP, EXP]), sb("later", [P, EXP, EXP])
        rank, cw, cwT = sb("rank", [P, TG, EXP]), sb("cw", [P, TG, EXP]), sb("cwT", [EXP, GT])
        cw_dram = nc.dram_tensor("cw_dram", (NG, EXP, GT), F32, kind="Internal").ap()
        psum = lambda name, n: ctx.enter_context(nc.psum_tensor(f"m_{name}_ps", [P, n, 512], F32))
        gate_ps, up_ps, y_ps, turn_ps = psum("gate", 3), psum("up", 3), psum("y", 1), psum("turn", 1)

        SLOTS = range(-1, NG + 1)
        expert = Count(SLOTS, lambda g: list(range(NE)) if 0 <= g < NG else [])
        half = Count(SLOTS, lambda g: [(j, n) for j in range(NE) for n in range(2)] if 0 <= g < NG else [])
        routed = Count(SLOTS, lambda g: [(j, n) for j in range(1, NE) for n in range(2)] if 0 <= g < NG else [])
        pre = Count(SLOTS, lambda g: [()] * (g < NG - 1))
        post = Count(SLOTS, lambda g: [()] * (g > 0))
        turns = Count(SLOTS, lambda g: ["y"] * (g > 0) + ["x", "cw"] * (g < NG - 1))
        NORM3 = ["3 stats", "3 sums", "3 parts", "3 var", "3 gain"]
        NORM_M = ["r", "m stats", "m sums", "m parts", "m var", "m norm"]
        ROUTE = ["logit", "one more", "prob", "compare", "masked", "sum", "rank", "cw"]
        steps = Count(SLOTS, lambda g: (NORM3 + NORM_M + ROUTE) * (g < NG - 1))
        roots = Count(SLOTS, lambda g: ["3", "m"] * (g < NG - 1))

        x3_loaded, x_loaded, cw_saved, stored = net.z_in, net.x_loaded, sem("cw_saved"), sem("stored")
        cw_loaded = [sem(f"cw_loaded{n}") for n in range(2)]
        gate_ready, up_ready, y_ready = sem("gate_ready"), sem("up_ready"), sem("y_ready")
        silu_done, weighted, h_done, hi_done, lo_done = sem("silu_done"), sem("weighted"), sem("h_done"), sem("hi_done"), sem("lo_done")
        step, root_done, biased, r_saved = sem("step"), sem("root_done"), sem("biased"), sem("r_saved")
        turned, x_hi, x_lo, cw_copied = sem("turned"), sem("x_hi"), sem("x_lo"), sem("cw_copied")
        logits_ready, e_done, y_copied, o_done = sem("logits_ready"), sem("e_done"), sem("y_copied"), sem("o_done")
        consts, gated_consts = sem("consts"), sem("gated_consts")

        index = lambda G: G if isinstance(G, int) else G.reg * G.step + G.first
        x_view, x3_view, out_view = (t.rearrange("(g t p) d -> g p t d", p=P, t=TG) for t in (a["x"], x3, out))
        weights = lambda matrix, j, n: (net.experts_hi[:, 6 * j + 2 * matrix + n, :], net.experts_lo[:, 6 * j + 2 * matrix + n, :])
        ring = lambda j, n: (2 * j + n) % 3

        def lag(j, G, n):
            return (j - n, G) if j >= n else (j - n + NE, G - 1)

        def three_halves_ago(j, n, G):
            jb, Gb = lag(j, G, 2 - n)
            return (jb, 1 - n), Gb

        def over_slots(eng, body, rounds=NG // 2 - 1):
            body(-1)
            body(0)
            with eng.Fori(0, rounds) as i:
                for par in range(2):
                    body(Loop(i, 1 + par, 2, rounds))
            for g in range(1 + 2 * rounds, NG + 1):
                body(g)

        block = ctx.enter_context(nc.Block())

        @block.sync
        def _(sp):
            def load(G):
                sp.dma_start(z[:], x3_view[index(G)]).then_inc(x3_loaded, 16)
                sp.dma_start(x_in[:], x_view[index(G)]).then_inc(x_loaded, 16)

            def slot(G):
                g = sample(G)
                if g < NG - 2:
                    sp.wait_ge(step, steps.after("r", G))
                    load(G + 2)
                if g > 0:
                    sp.wait_ge(o_done, post.after((), G))
                    sp.dma_start(out_view[index(G - 1)], o[:]).then_inc(stored, 16)
                if g < NG - 1:
                    sp.wait_ge(cw_copied, pre.after((), G))
                    sp.dma_start(cw_dram[index(G + 1)], cwT[:]).then_inc(cw_saved, 16)
                    if g > 0:
                        sp.wait_ge(weighted, routed.after((NE - 1, 1), G - 1))
                    sp.wait_ge(cw_saved, index(G) * 16 + 32)
                    for n in range(2):
                        src = cw_dram[index(G + 1), 4 * n:4 * n + 4, :].rearrange("(o e) t -> o e t", o=1)
                        sp.dma_start(cw_wide[:, (g + 1) % 2, 4 * n:4 * n + 4, :], src.to_broadcast([P, 4, GT]))\
                            .then_inc(cw_loaded[n], 16)

            over_slots(sp, slot, NG // 2 - 2)
            sp.wait_ge(stored, 16 * NG)

        @block.tensor
        def _(pe):
            def gates_and_ups(j, G):
                par = sample(G) % 2
                if j == 0:
                    pe.wait_ge(x_lo, pre.after((), G - 1))
                for n in range(2):
                    if 2 * j + n >= 3 or sample(G) > 0:
                        pe.wait_ge(h_done, half.after(*three_halves_ago(j, n, G)))
                    for matrix, ps, ready in ((0, gate_ps, gate_ready), (1, up_ps, up_ready)):
                        mm3(nc, ps[:, ring(j, n), :], *weights(matrix, j, n), xT_hi[:, par, :], xT_lo[:, par, :]).then_inc(ready, 1)

            def down(j, G):
                if j == 0 and sample(G) > 0:
                    pe.wait_ge(y_copied, post.after((), G))
                for n in range(2):
                    pe.wait_ge(lo_done, half.after((j, n), G))
                    ins = mm3(nc, y_ps[:, 0, :], *weights(2, j, n), h_hi[:, j % 3, n, :], h_lo[:, j % 3, n, :],
                              start=(j == 0 and n == 0), stop=(j == NE - 1 and n == 1))
                ins.then_inc(y_ready, 1)

            def turn_y(G):
                pe.wait_ge(y_copied, post.after((), G))
                if sample(G) < NG:
                    pe.wait_ge(cw_copied, pre.after((), G - 1))
                else:
                    pe.wait_ge(o_done, post.after((), G - 1))
                for t in range(TG):
                    ins = nc.tensor.transpose(turn_ps[:, 0, t * P:(t + 1) * P], yT[:, t * P:(t + 1) * P], net.ident[:])
                ins.then_inc(turned, 1)

            def turn_x(G):
                pe.wait_ge(step, steps.after("m norm", G))
                if sample(G) > 0:
                    pe.wait_ge(o_done, post.after((), G))
                elif sample(G) == 0:
                    pe.wait_ge(cw_copied, pre.after((), G - 1))
                for t in range(TG):
                    ins = nc.tensor.transpose(turn_ps[:, 0, t * P:(t + 1) * P], m[:, t, :], net.ident[:])
                ins.then_inc(turned, 1)

            def logits(G):
                par = (sample(G) + 1) % 2
                pe.wait_ge(x_lo, pre.after((), G))
                for t in range(TG):
                    toks = slice(t * P, (t + 1) * P)
                    ins = mm3(nc, turn_ps[:, 0, t * EXP:(t + 1) * EXP], xT_hi[:, par, toks], xT_lo[:, par, toks],
                              net.router_hi[:], net.router_lo[:])
                ins.then_inc(logits_ready, 1)

            def turn_cw(G):
                pe.wait_ge(step, steps.after("cw", G))
                for t in range(TG):
                    ins = nc.tensor.transpose(turn_ps[0:EXP, 0, t * P:(t + 1) * P], cw[:, t, :], net.ident[:])
                ins.then_inc(turned, 1)

            def slot(G):
                g = sample(G)
                for j in range(NE):
                    if 0 <= g < NG:
                        gates_and_ups(j, G)
                    if (0 <= g < NG and (g > 0 or j >= 2)) or (g == NG and j < 2):
                        down(*lag(j, G, 2))
                    if j == AT_TURN_Y and g > 0:
                        turn_y(G)
                    if g < NG - 1:
                        if j == AT_TURN_X:
                            turn_x(G)
                        if j == AT_TURN_X + 1:
                            logits(G)
                        if j == AT_TURN_CW and g >= 0:
                            turn_cw(G)
                    if g == 0 and j == 1:
                        turn_cw(-1)

            over_slots(pe, slot)

        @block.scalar
        def _(act):
            def silu(j, n, G):
                act.wait_ge(gate_ready, half.after((j, n), G))
                nc.scalar.activation(act_g[:, ring(j, n), :], gate_ps[:, ring(j, n), :], ACT.Silu).then_inc(silu_done, 1)

            def high(j, n, G):
                if j == 0:
                    act.wait_ge(h_done, half.after((j, n), G))
                else:
                    act.wait_ge(weighted, routed.after((j, n), G))
                if j >= 3 or sample(G) > 0:
                    jb, Gb = lag(j, G, 3)
                    act.wait_ge(y_ready, expert.after(jb, Gb))
                nc.scalar.activation(h_hi[:, j % 3, n, :], h[:, j % 3, n, :], ACT.Copy).then_inc(hi_done, 1)

            def copy_y(G):
                act.wait_ge(y_ready, expert.after(NE - 1, G - 1))
                if sample(G) > 1:
                    act.wait_ge(turned, turns.after("y", G - 1))
                nc.scalar.activation(yT[:], y_ps[:, 0, :], ACT.Copy).then_inc(y_copied, 1)

            def x_high(G):
                act.wait_ge(turned, turns.after("x", G))
                nc.scalar.activation(xT_hi[:, (sample(G) + 1) % 2, :], turn_ps[:, 0, :], ACT.Copy).then_inc(x_hi, 1)

            def keep_r(G):
                act.wait_ge(step, steps.after("r", G))
                if sample(G) > 0:
                    act.wait_ge(o_done, post.after((), G))
                nc.scalar.activation(r_kept[:, (sample(G) + 1) % 2], r[:], ACT.Copy).then_inc(r_saved, 1)

            def copy_cw(G):
                act.wait_ge(turned, turns.after("cw", G))
                if sample(G) >= 0:
                    act.wait_ge(cw_saved, index(G) * 16 + 16)
                nc.scalar.activation(cwT[:], turn_ps[0:EXP, 0, :], ACT.Copy).then_inc(cw_copied, 1)

            def slot(G):
                g = sample(G)
                for j in range(NE):
                    if j == 2 and g > 0:
                        copy_y(G)
                    if g < NG - 1:
                        if j == AT_TURN_X + 1:
                            x_high(G)
                        if j == AT_TURN_CW + 1 and g >= 0:
                            copy_cw(G)
                    if g == 0 and j == 2:
                        copy_cw(-1)
                    for n in range(2):
                        if 0 <= g < NG:
                            silu(j, n, G)
                        if (0 <= g < NG and (g > 0 or j > 0)) or (g == NG and j == 0):
                            jb, Gb = lag(j, G, 1)
                            high(jb, n, Gb)
                    if g < NG - 1 and j == AT_TURN_X + 1:
                        keep_r(G)

            over_slots(act, slot)

        @block.vector
        def _(dve):
            nc.vector.memset(e_base[:], 1 / 2.718281828459045)
            nc.vector.tensor_scalar(gate_bias[:], net.wide["ln3_b"][:], net.gates[:, 0:1], None, ALU.mult).then_inc(gated_consts, 1)
            nc.vector.tensor_scalar(gate_gain[:], net.wide["ln3_g"][:], net.gates[:, 0:1], None, ALU.mult).then_inc(gated_consts, 1)
            dve.wait_ge(gated_consts, 2)
            dve.wait_ge(consts, 4)

            def product(j, n, G):
                dve.wait_ge(up_ready, half.after((j, n), G))
                dve.wait_ge(silu_done, half.after((j, n), G))
                nc.vector.tensor_tensor(h[:, j % 3, n, :], up_ps[:, ring(j, n), :], act_g[:, ring(j, n), :], ALU.mult)\
                    .then_inc(h_done, 1)

            def low(j, n, G):
                dve.wait_ge(hi_done, half.after((j, n), G))
                nc.vector.tensor_tensor(h_lo[:, j % 3, n, :], h[:, j % 3, n, :], f32(h_hi[:, j % 3, n, :]),
                                        ALU.subtract).then_inc(lo_done, 1)

            def output(G):
                dve.wait_ge(turned, turns.after("y", G))
                if sample(G) > 1:
                    dve.wait_ge(stored, index(G) * 16 - 16)
                nc.vector.scalar_tensor_tensor(out=o[:], in0=turn_ps[:, 0, :].rearrange("p (t n) -> p t n", t=TG),
                                               scalar=net.gates[:, 1:2], in1=r_kept[:, (sample(G) - 1) % 2], op0=ALU.mult,
                                               op1=ALU.add).then_inc(o_done, 1)

            def moments(G, rows, names):
                row_moments(nc, dve, rows, stats, parts, mean[:], var[:], step,
                            lambda n: steps.after(names[n - 1], G)).then_inc(step, 1)

            def gain(G):
                for t in range(TG):
                    ins = nc.vector.scalar_tensor_tensor(out=z[:, t, :], in0=z[:, t, :], scalar=mean[:, t:t + 1], in1=gate_gain[:],
                                                         op0=ALU.subtract, op1=ALU.mult)
                ins.then_inc(step, 1)

            def gated(G):
                if sample(G) >= 0:
                    dve.wait_ge(r_saved, pre.after((), G - 1))
                dve.wait_ge(biased, pre.after((), G))
                dve.wait_ge(root_done, roots.after("3", G))
                dve.wait_ge(step, steps.after("3 gain", G))
                for t in range(TG):
                    ins = nc.vector.scalar_tensor_tensor(out=r[:, t, :], in0=z[:, t, :], scalar=rstd[:, t:t + 1], in1=x_in[:, t, :],
                                                         op0=ALU.mult, op1=ALU.add)
                ins.then_inc(step, 1)
                dve.wait_ge(step, steps.after("r", G))

            def normed(G):
                dve.wait_ge(root_done, roots.after("m", G))
                for t in range(TG):
                    ins = nc.vector.tensor_scalar(m[:, t, :], r[:, t, :], mean[:, t:t + 1], rstd[:, t:t + 1], ALU.subtract, ALU.mult)
                ins.then_inc(step, 1)

            def x_low(G):
                par = (sample(G) + 1) % 2
                dve.wait_ge(x_hi, pre.after((), G))
                nc.vector.tensor_tensor(xT_lo[:, par, :], turn_ps[:, 0, :], f32(xT_hi[:, par, :]), ALU.subtract).then_inc(x_lo, 1)

            def add_bias(G):
                dve.wait_ge(logits_ready, pre.after((), G))
                nc.vector.tensor_tensor(logit[:], turn_ps[:, 0, 0:TG * EXP].rearrange("p (t e) -> p t e", t=TG),
                                        net.router_bias[:].unsqueeze(1).to_broadcast([P, TG, EXP]), ALU.add).then_inc(step, 1)

            def route(G):
                def then(ins, name):
                    ins.then_inc(step, 1)
                    dve.wait_ge(step, steps.after(name, G))
                dve.wait_ge(e_done, pre.after((), G))
                then(nc.vector.tensor_scalar(logit[:], e_neg[:], 1.0, None, ALU.add), "one more")
                then(nc.vector.reciprocal(prob[:], logit[:]), "prob")
                other, own = prob[:].unsqueeze(2).to_broadcast([P, TG, EXP, EXP]), prob[:].unsqueeze(3).to_broadcast([P, TG, EXP, EXP])
                wide = lambda t: t[:].unsqueeze(1).to_broadcast([P, TG, EXP, EXP])
                nc.vector.tensor_tensor(equal[:], other, own, ALU.is_ge)
                then(nc.vector.tensor_tensor(above[:], other, own, ALU.is_gt), "compare")
                nc.vector.tensor_tensor(equal[:], equal[:], wide(earlier), ALU.mult)
                then(nc.vector.tensor_tensor(above[:], above[:], wide(later), ALU.mult), "masked")
                then(nc.vector.tensor_tensor(above[:], above[:], equal[:], ALU.add), "sum")
                then(nc.vector.tensor_reduce(rank[:], above[:], AX.X, ALU.add), "rank")
                nc.vector.scalar_tensor_tensor(out=cw[:], in0=rank[:], scalar=1.5, in1=prob[:], op0=ALU.is_lt,
                                               op1=ALU.mult).then_inc(step, 1)

            def slot(G):
                g = sample(G)
                for j in range(NE):
                    if j == AT_TURN_Y + 1 and g > 0:
                        output(G)
                    if g < NG - 1:
                        if j == AT_TURN_X + 1:
                            x_low(G)
                        if j == AT_TURN_X + 2:
                            add_bias(G)
                        if j == AT_TURN_CW and g >= 0:
                            route(G)
                    for n in range(2):
                        if 0 <= g < NG:
                            product(j, n, G)
                        if (0 <= g < NG and (g > 0 or j > 0)) or (g == NG and j == 0):
                            jb, Gb = lag(j, G, 1)
                            low(jb, n, Gb)
                    if g == 0 and j == 0:
                        route(-1)
                    if g >= NG - 1:
                        continue
                    if j == 0:
                        dve.wait_ge(x3_loaded, index(G) * 16 + 32)
                        moments(G, lambda t: z[:, t, :], NORM3)
                        gain(G)
                    if j == 1:
                        gated(G)
                        moments(G, lambda t: r[:, t, :], NORM_M[1:])
                    if j == 2:
                        normed(G)

            over_slots(dve, slot)

        @block.gpsimd
        def _(pool):
            for n, (t, sign, keep) in enumerate(((earlier, 1, ALU.is_gt), (later, -1, ALU.is_ge))):
                nc.gpsimd.memset(t[:], 1.0).then_inc(consts, 1)
                pool.wait_ge(consts, 2 * n + 1)
                nc.gpsimd.affine_select(out=t[:], in_=t[:], compare_op=keep, fill=0.0, base=0,
                                        pattern=[[sign, EXP], [-sign, EXP]], channel_multiplier=0).then_inc(consts, 1)
            pool.wait_ge(gated_consts, 1)

            def weight(j, n, G):
                pool.wait_ge(h_done, half.after((j, n), G))
                if n == 0 and j in (1, 5):
                    pool.wait_ge(cw_loaded[j // 5], index(G) * 16 + 16)
                nc.gpsimd.tensor_tensor(h[:, j % 3, n, :], h[:, j % 3, n, :], cw_wide[:, sample(G) % 2, j - 1, :],
                                        ALU.mult).then_inc(weighted, 1)

            def root(G, name):
                pool.wait_ge(step, steps.after(name, G))
                nc.gpsimd.tensor_tensor(rstd[:], var[:], net.half_neg[:, 0:TG], ALU.pow).then_inc(root_done, 1)

            def add_gate_bias(G):
                pool.wait_ge(x_loaded, index(G) * 16 + 32)
                nc.gpsimd.tensor_tensor(x_in[:], x_in[:], gate_bias[:].unsqueeze(1).to_broadcast([P, TG, P]), ALU.add)\
                    .then_inc(biased, 1)

            def exponential(G, part):
                tiles = slice(2 * part, 2 * part + 2)
                if part == 0:
                    pool.wait_ge(step, steps.after("logit", G))
                ins = nc.gpsimd.tensor_tensor(e_neg[:, tiles], e_base[:, tiles], logit[:, tiles], ALU.pow)
                if part == 1:
                    ins.then_inc(e_done, 1)

            def slot(G):
                g = sample(G)
                for j in range(NE):
                    if g < NG - 1 and j == AT_TURN_X + 2:
                        exponential(G, 0)
                    if 0 <= g < NG and j > 0:
                        weight(j, 0, G)
                        weight(j, 1, G)
                    if g >= NG - 1:
                        continue
                    if j == 0:
                        add_gate_bias(G)
                        root(G, "3 var")
                    if j == 1:
                        root(G, "m var")
                    if j == AT_TURN_X + 2:
                        exponential(G, 1)

            over_slots(pool, slot)


def program(nc, a, out):
    with ExitStack() as ctx:
        net = Net()
        dram = lambda name, shape: nc.dram_tensor(name, shape, F32, kind="Internal").ap()
        sb = lambda name, shape, dt=F32: ctx.enter_context(nc.sbuf_tensor(name, shape, dt))
        net.xn, net.x1, net.x2, net.x3 = (dram(n, (TOK, D)) for n in ("xn", "x1", "x2", "x3"))
        net.ident, net.ident16 = sb("ident", [P, P]), sb("ident16", [P, P], F16)
        net.ones_row, net.mask_row = sb("ones_row", [1, P], BF16), sb("mask_row", [1, TOK], BF16)
        net.half_neg = sb("half_neg", [P, NORM_TILES])
        net.gates_raw, net.gates = sb("gates_raw", [P, 2]), sb("gates", [P, 2])
        net.wide = {n: sb(f"wide_{n}", [P, D]) for n in ("ln1_g", "ln1_b", "ln2_g", "ln2_b", "ln3_g", "ln3_b")}
        net.router_bias = sb("router_bias", [P, EXP])
        net.out_bias = {n: sb(f"bias_{n}", [P, 1]) for n in ("sa", "ca", "fc2")}
        net.fc1_bias = sb("fc1_bias", [P, FF // P])

        def const_loads(mask_u8):
            loads = [(mask_u8[:], a["mask"].rearrange("(o b) s -> o (b s)", o=1))]
            loads += [(t[:], a[n].rearrange("(o d) -> o d", o=1).to_broadcast([P, D])) for n, t in net.wide.items()]
            loads += [(net.router_bias[:], a["rb"].rearrange("(o d) -> o d", o=1).to_broadcast([P, EXP]))]
            loads += [(net.gates_raw[:, i:i + 1], a[n].rearrange("(o d) -> o d", o=1).to_broadcast([P, 1]))
                      for i, n in enumerate(("g_xattn", "g_ffn"))]
            loads += [(t[:], a[{"sa": "sa_bo", "ca": "ca_bo", "fc2": "fc2_b"}[n]].rearrange("(d o) -> d o", o=1))
                      for n, t in net.out_bias.items()]
            fc1_b = a["fc1_b"].rearrange("(c p o) -> c p o", p=P, o=1)
            loads += [(net.fc1_bias[:, c:c + 1], fc1_b[c]) for c in range(FF // P)]
            return loads

        net.const_loads = const_loads
        net.n_const = 13 + FF // P
        net.raw_expert = sb("raw_expert", [P, 6, P])
        net.raw_router, net.raw_fc = sb("raw_router", [EXP, P]), sb("raw_fc", [P, 2, FF // P, P])
        net.feed_x = sb("feed_x", [P, TG, P])
        sem = lambda name: ctx.enter_context(nc.semaphore(name))
        net.raw_in, net.router_in, net.fc_in, net.feed_x_in = sem("raw_in"), sem("router_in"), sem("fc_in"), sem("feed_x_in")
        net.z_in, net.x_loaded = sem("x3_in"), sem("experts_x_in")
        with ExitStack() as ctx_a:
            sba = lambda name: ctx_a.enter_context(nc.sbuf_tensor(name, [P, H, P], F32R))
            net.M = {p: (sba(f"M_hi_{p}"), sba(f"M_lo_{p}")) for p in ("sa", "ca")}
            net.N = {p: (sba(f"N_hi_{p}"), sba(f"N_lo_{p}")) for p in ("sa", "ca")}
            prepare(nc, net, a)
            attentions(nc, net, [
                Layer("sa", net.xn, net.xn, net.x1, net.wide["ln1_g"], net.wide["ln1_b"]),
                Layer("ca", net.x1, a["ctx"], net.x2, net.wide["ln2_g"], net.wide["ln2_b"])], a)
        net.experts_hi, net.experts_lo = sb("experts_hi", [P, EW, P], F32R), sb("experts_lo", [P, EW, P], F32R)
        net.x_in, net.z = sb("x_in", [P, TG, P]), sb("z", [P, TG, P])
        net.router_hi, net.router_lo = sb("router_hi", [P, EXP], F32R), sb("router_lo", [P, EXP], F32R)
        feed(nc, net, a, net.x2, net.x3)
        experts(nc, net, a, net.x3, out)


_NAMES = {"x": "x", "ctx": "ctx_1024", "mask": "mask_BxS2_bk0", "g_xattn": "g_xattn", "g_ffn": "g_ffn"}
_NAMES |= {n: f"L0_xattn_{n}" for n in (
    "sa_wq", "sa_wk", "sa_wv", "sa_wo", "sa_bo", "ca_wq", "ca_wk", "ca_wv", "ca_wo", "ca_bo", "ln1_g", "ln1_b",
    "ln2_g", "ln2_b", "ln3_g", "ln3_b", "fc1_w", "fc1_b", "fc2_w", "fc2_b")}
_NAMES |= {n: f"L0_ffn_{n}" for n in ("Wg_s", "Wu_s", "Wd_s", "Wg", "Wu", "Wd", "Wr", "rb")}


def kernel(**inputs):
    import numpy as np
    import concourse.bacc as bacc
    from concourse.bass_utils import run_bass_kernel_spmd

    nc = bacc.Bacc("TRN2", target_bir_lowering=False, num_devices=1)
    arrays, a = {}, {}
    for short, name in _NAMES.items():
        v = np.ascontiguousarray(inputs[name])
        if short in ("x", "ctx"):
            v = v.reshape(TOK, D)
        arrays[f"in_{short}"] = v
        dt = U8 if v.dtype == np.bool_ else mybir.dt.from_np(v.dtype)
        a[short] = nc.dram_tensor(f"in_{short}", v.shape, dt, kind="ExternalInput").ap()
    out = nc.dram_tensor("out", (TOK, D), F32, kind="ExternalOutput").ap()
    program(nc, a, out)
    r = run_bass_kernel_spmd(nc, [arrays], core_ids=[0])
    return r.results[0]["out"].reshape(B, S, D)
```
